# Optimizing a Trainium2 kernel written in Bass

```python
import numpy as np
import jax
import jax.numpy as jnp

def _softmax(x, axis=-1):
    return jax.nn.softmax(x, axis=axis)

def _gelu(x):
    return jax.nn.gelu(x, approximate=True)

def _silu(x):
    return jax.nn.silu(x)

def _sigmoid(x):
    return jax.nn.sigmoid(x)

def _layernorm(x, axis=-1, eps=1e-05):
    m = jnp.mean(x, axis=axis, keepdims=True)
    v = jnp.var(x, axis=axis, keepdims=True)
    return (x - m) / jnp.sqrt(v + eps)

def _scatter_add(tgt, idx, src, axis=0):
    return tgt.at[idx].add(src)

def _segment_sum(src, seg, n):
    return jax.ops.segment_sum(src, seg, n)
kernel_name = 'mk_seq_postln_d2_jaxref_r8_dd024f'

def setup_inputs(seed: int=0):
    np.random.seed(seed)
    _w = jnp.asarray

    def _L0_attn_setup():
        import jax, jax.numpy as jnp
        import numpy as np
        HIDDEN = 256
        NUM_HEADS = 16
        HEAD_DIM = 128
        OUT = NUM_HEADS * HEAD_DIM
        B, T = (4, 256)

        def _wkv(r, k, v, time_decay, time_first):
            w = jnp.exp(-jnp.exp(time_decay))
            u = time_first
            kv = k * v
            r_t = jnp.moveaxis(r, 1, 0)
            kv_t = jnp.moveaxis(kv, 1, 0)

            def step(state, inp):
                rt, kvt = inp
                out = (state + u * kvt) * rt
                new_state = state * w + kvt
                return (new_state, out)
            state0 = jnp.zeros(r.shape[:1] + r.shape[2:], dtype=r.dtype)
            _, out = jax.lax.scan(step, state0, (r_t, kv_t))
            return jnp.moveaxis(out, 0, 1)
        key = jax.random.key(seed)
        ks = jax.random.split(key, 8)
        hidden_states = jax.random.normal(ks[0], (B, T, HIDDEN), dtype=jnp.float32)
        scale = 0.02
        Wr = jax.random.normal(ks[1], (OUT, HIDDEN), dtype=jnp.float32) * scale
        Wk = jax.random.normal(ks[2], (OUT, HIDDEN), dtype=jnp.float32) * scale
        Wv = jax.random.normal(ks[3], (OUT, HIDDEN), dtype=jnp.float32) * scale
        Wo = jax.random.normal(ks[4], (HIDDEN, OUT), dtype=jnp.float32) * scale
        time_decay = jax.random.uniform(ks[5], (NUM_HEADS, HEAD_DIM), minval=-4.0, maxval=-1.0, dtype=jnp.float32)
        time_first = jax.random.uniform(ks[6], (NUM_HEADS, HEAD_DIM), minval=-0.5, maxval=0.5, dtype=jnp.float32)
        time_mix_k = jnp.full((1, 1, HIDDEN), 0.5, dtype=jnp.float32)
        time_mix_v = jnp.full((1, 1, HIDDEN), 0.5, dtype=jnp.float32)
        time_mix_r = jnp.full((1, 1, HIDDEN), 0.5, dtype=jnp.float32)
        return {'hidden_states': hidden_states, 'Wr': Wr, 'Wk': Wk, 'Wv': Wv, 'Wo': Wo, 'time_decay': time_decay, 'time_first': time_first, 'time_mix_k': time_mix_k, 'time_mix_v': time_mix_v, 'time_mix_r': time_mix_r}
    _L0_attn_in = _L0_attn_setup()

    def _L0_ffn_setup():
        import jax, jax.numpy as jnp
        import numpy as np
        DIM = 256
        HID = 704
        ZERO_POINT = 128.0

        def _qlinear(x, wq, scale):
            W = (wq.astype(jnp.float32) - ZERO_POINT) * scale[:, None]
            return jnp.einsum('bsd,hd->bsh', x, W)
        key = jax.random.key(seed)
        ks = jax.random.split(key, 7)
        B, S = (4, 256)
        sg = jax.random.uniform(ks[1], (HID,)) * (0.02 / np.sqrt(DIM)) + 0.0001
        su = jax.random.uniform(ks[3], (HID,)) * (0.02 / np.sqrt(DIM)) + 0.0001
        sd = jax.random.uniform(ks[5], (DIM,)) * (0.02 / np.sqrt(HID)) + 0.0001
        return {'x': jax.random.normal(ks[0], (B, S, DIM), dtype=jnp.float32), 'wq_gate': jax.random.randint(ks[2], (HID, DIM), 0, 32, dtype=jnp.int32), 's_gate': sg, 'wq_up': jax.random.randint(ks[4], (HID, DIM), 0, 32, dtype=jnp.int32), 's_up': su, 'wq_down': jax.random.randint(ks[6], (DIM, HID), 0, 32, dtype=jnp.int32), 's_down': sd}
    _L0_ffn_in = _L0_ffn_setup()

    def _L1_attn_setup():
        import jax, jax.numpy as jnp
        import numpy as np
        HID = 256
        H = 16
        QLR = 192
        KVLR = 64
        DN = 128
        DR = 64
        DV = 128
        DQ = DN + DR
        B = 2
        S = 256
        THETA = 10000.0
        EPS = 1e-06

        def rms_norm(x, w, eps=EPS):
            x32 = x.astype(jnp.float32)
            var = jnp.mean(x32 * x32, axis=-1, keepdims=True)
            return (w * (x32 * jax.lax.rsqrt(var + eps))).astype(x.dtype)

        def rotate_half(x):
            x1, x2 = jnp.split(x, 2, axis=-1)
            return jnp.concatenate((-x2, x1), axis=-1)

        def rope_tables(seq_len, dim, base=THETA):
            inv_freq = 1.0 / base ** (jnp.arange(0, dim, 2, dtype=jnp.float32) / dim)
            t = jnp.arange(seq_len, dtype=jnp.float32)
            freqs = jnp.outer(t, inv_freq)
            emb = jnp.concatenate((freqs, freqs), -1)
            return (jnp.cos(emb), jnp.sin(emb))
        key = jax.random.key(seed)
        ks = jax.random.split(key, 8)
        sd = lambda fan_in: 1.0 / np.sqrt(fan_in)
        return {'hidden_states': jax.random.normal(ks[0], (B, S, HID), jnp.float32), 'w_qa': jax.random.normal(ks[1], (QLR, HID), jnp.float32) * sd(HID), 'q_a_ln_w': jnp.ones((QLR,), jnp.float32), 'w_qb': jax.random.normal(ks[2], (H * DQ, QLR), jnp.float32) * sd(QLR), 'w_kva': jax.random.normal(ks[3], (KVLR + DR, HID), jnp.float32) * sd(HID), 'kv_a_ln_w': jnp.ones((KVLR,), jnp.float32), 'w_kvb': jax.random.normal(ks[4], (H * (DN + DV), KVLR), jnp.float32) * sd(KVLR), 'w_o': jax.random.normal(ks[5], (HID, H * DV), jnp.float32) * sd(H * DV)}
    _L1_attn_in = _L1_attn_setup()

    def _L1_ffn_setup():
        import math
        import jax, jax.numpy as jnp
        import numpy as np
        from jax import lax
        D = 256
        I = 128
        E = 32
        K = 4
        NG = 8
        TKG = 3
        NSH = 2
        SCALE = 2.5
        CF = 1.25
        B, S = (2, 256)

        def _router(x, router_w, e_bias):
            scores = jax.nn.sigmoid(x @ router_w.T)
            sc = scores + e_bias[None, :]
            T = x.shape[0]
            gs = sc.reshape(T, NG, E // NG)
            group_scores = lax.top_k(gs, 2)[0].sum(-1)
            _, gidx = lax.top_k(group_scores, TKG)
            gmask = jnp.zeros((T, NG), sc.dtype).at[jnp.arange(T)[:, None], gidx].set(1.0)
            smask = jnp.repeat(gmask, E // NG, axis=1)
            masked = jnp.where(smask > 0, sc, 0.0)
            _, topk_idx = lax.top_k(masked, K)
            topk_w = jnp.take_along_axis(scores, topk_idx, axis=1)
            topk_w = topk_w / (topk_w.sum(-1, keepdims=True) + 1e-20)
            topk_w = topk_w * SCALE
            return (topk_idx.astype(jnp.int32), topk_w)

        def _moe_forward(hidden_states, router_w, e_bias, W_gate, W_up, W_down, shared_gate, shared_up, shared_down):
            b, s, d = hidden_states.shape
            T = b * s
            C = int(math.ceil(CF * T / E))
            EC = E * C
            x = hidden_states.reshape(T, d)
            topk_idx, topk_w = _router(x, router_w, e_bias)
            expert_flat = topk_idx.reshape(-1)
            w_flat = topk_w.reshape(-1)
            tok_flat = jnp.repeat(jnp.arange(T, dtype=jnp.int32), K)
            sort_ix = jnp.argsort(expert_flat)
            e_sorted = expert_flat[sort_ix]
            tok_s = tok_flat[sort_ix]
            w_s = w_flat[sort_ix]
            counts = jnp.zeros(E, jnp.int32).at[e_sorted].add(1)
            group_start = jnp.concatenate([jnp.zeros(1, jnp.int32), jnp.cumsum(counts)[:-1].astype(jnp.int32)])
            pos = jnp.arange(T * K, dtype=jnp.int32) - group_start[e_sorted]
            valid = pos < C
            dest = e_sorted * C + jnp.where(valid, pos, 0)
            slots_token = jnp.zeros(EC, jnp.int32).at[dest].add(jnp.where(valid, tok_s, 0))
            slots_w = jnp.zeros(EC, w_s.dtype).at[dest].add(jnp.where(valid, w_s, 0.0))
            Xp = x[slots_token].reshape(E, C, d)
            G = jnp.einsum('ecd,edi->eci', Xp, W_gate)
            U = jnp.einsum('ecd,edi->eci', Xp, W_up)
            Y = jnp.einsum('eci,eid->ecd', jax.nn.silu(G) * U, W_down)
            Yf = Y.reshape(EC, d) * slots_w[:, None]
            out = jnp.zeros((T, d), x.dtype).at[slots_token].add(Yf)
            shared = jax.nn.silu(x @ shared_gate.T) * (x @ shared_up.T) @ shared_down.T
            return (out + shared).reshape(b, s, d)
        key = jax.random.key(seed)
        ks = jax.random.split(key, 8)

        def rn(k, shape, scale=0.02):
            return jax.random.normal(k, shape, jnp.float32) * scale
        return {'hidden_states': jax.random.normal(ks[0], (B, S, D), jnp.float32), 'router_w': rn(ks[1], (E, D)), 'e_bias': jnp.zeros((E,), jnp.float32), 'W_gate': rn(ks[2], (E, D, I)), 'W_up': rn(ks[3], (E, D, I)), 'W_down': rn(ks[4], (E, I, D)), 'shared_gate': rn(ks[5], (I * NSH, D)), 'shared_up': rn(ks[6], (I * NSH, D)), 'shared_down': rn(ks[7], (D, I * NSH))}
    _L1_ffn_in = _L1_ffn_setup()
    _d = {'L0_attn_hidden_states': _L0_attn_in['hidden_states'], 'L0_attn_Wr': _L0_attn_in['Wr'], 'L0_attn_Wk': _L0_attn_in['Wk'], 'L0_attn_Wv': _L0_attn_in['Wv'], 'L0_attn_Wo': _L0_attn_in['Wo'], 'L0_attn_time_decay': _L0_attn_in['time_decay'], 'L0_attn_time_first': _L0_attn_in['time_first'], 'L0_attn_time_mix_k': _L0_attn_in['time_mix_k'], 'L0_attn_time_mix_v': _L0_attn_in['time_mix_v'], 'L0_attn_time_mix_r': _L0_attn_in['time_mix_r'], 'L0_ffn_wq_gate': _L0_ffn_in['wq_gate'], 'L0_ffn_s_gate': _L0_ffn_in['s_gate'], 'L0_ffn_wq_up': _L0_ffn_in['wq_up'], 'L0_ffn_s_up': _L0_ffn_in['s_up'], 'L0_ffn_wq_down': _L0_ffn_in['wq_down'], 'L0_ffn_s_down': _L0_ffn_in['s_down'], 'L1_attn_w_qa': _L1_attn_in['w_qa'], 'L1_attn_q_a_ln_w': _L1_attn_in['q_a_ln_w'], 'L1_attn_w_qb': _L1_attn_in['w_qb'], 'L1_attn_w_kva': _L1_attn_in['w_kva'], 'L1_attn_kv_a_ln_w': _L1_attn_in['kv_a_ln_w'], 'L1_attn_w_kvb': _L1_attn_in['w_kvb'], 'L1_attn_w_o': _L1_attn_in['w_o'], 'L1_ffn_router_w': _L1_ffn_in['router_w'], 'L1_ffn_e_bias': _L1_ffn_in['e_bias'], 'L1_ffn_W_gate': _L1_ffn_in['W_gate'], 'L1_ffn_W_up': _L1_ffn_in['W_up'], 'L1_ffn_W_down': _L1_ffn_in['W_down'], 'L1_ffn_shared_gate': _L1_ffn_in['shared_gate'], 'L1_ffn_shared_up': _L1_ffn_in['shared_up'], 'L1_ffn_shared_down': _L1_ffn_in['shared_down']}
    _x0 = _d['L0_attn_hidden_states']
    _d['L0_attn_hidden_states'] = jax.random.normal(jax.random.fold_in(jax.random.key(seed), 1), (16, 256, 256), dtype=_x0.dtype)
    del _x0
    return _d

def reference(L0_attn_hidden_states, L0_attn_Wr, L0_attn_Wk, L0_attn_Wv, L0_attn_Wo, L0_attn_time_decay, L0_attn_time_first, L0_attn_time_mix_k, L0_attn_time_mix_v, L0_attn_time_mix_r, L0_ffn_wq_gate, L0_ffn_s_gate, L0_ffn_wq_up, L0_ffn_s_up, L0_ffn_wq_down, L0_ffn_s_down, L1_attn_w_qa, L1_attn_q_a_ln_w, L1_attn_w_qb, L1_attn_w_kva, L1_attn_kv_a_ln_w, L1_attn_w_kvb, L1_attn_w_o, L1_ffn_router_w, L1_ffn_e_bias, L1_ffn_W_gate, L1_ffn_W_up, L1_ffn_W_down, L1_ffn_shared_gate, L1_ffn_shared_up, L1_ffn_shared_down):

    def _L0_attn_ref(hidden_states, Wr, Wk, Wv, Wo, time_decay, time_first, time_mix_k, time_mix_v, time_mix_r):
        import jax, jax.numpy as jnp
        import numpy as np
        HIDDEN = 256
        NUM_HEADS = 16
        HEAD_DIM = 128
        OUT = NUM_HEADS * HEAD_DIM
        B, T = (4, 256)

        def _wkv(r, k, v, time_decay, time_first):
            w = jnp.exp(-jnp.exp(time_decay))
            u = time_first
            kv = k * v
            r_t = jnp.moveaxis(r, 1, 0)
            kv_t = jnp.moveaxis(kv, 1, 0)

            def step(state, inp):
                rt, kvt = inp
                out = (state + u * kvt) * rt
                new_state = state * w + kvt
                return (new_state, out)
            state0 = jnp.zeros(r.shape[:1] + r.shape[2:], dtype=r.dtype)
            _, out = jax.lax.scan(step, state0, (r_t, kv_t))
            return jnp.moveaxis(out, 0, 1)
        Bc, Tc, _ = hidden_states.shape
        xx = jnp.concatenate([jnp.zeros_like(hidden_states[:, :1]), hidden_states[:, :-1]], axis=1)
        xk = hidden_states * time_mix_k + xx * (1.0 - time_mix_k)
        xv = hidden_states * time_mix_v + xx * (1.0 - time_mix_v)
        xr = hidden_states * time_mix_r + xx * (1.0 - time_mix_r)
        receptance = jax.nn.sigmoid(jnp.einsum('bth,oh->bto', xr, Wr))
        key = jnp.einsum('bth,oh->bto', xk, Wk)
        value = jnp.einsum('bth,oh->bto', xv, Wv)
        receptance = receptance.reshape(Bc, Tc, NUM_HEADS, HEAD_DIM)
        key = key.reshape(Bc, Tc, NUM_HEADS, HEAD_DIM)
        value = value.reshape(Bc, Tc, NUM_HEADS, HEAD_DIM)
        wkv = _wkv(receptance, key, value, time_decay, time_first)
        attn = wkv.reshape(Bc, Tc, OUT)
        return jnp.einsum('bto,ho->bth', attn, Wo)

    def _L0_ffn_ref(x, wq_gate, s_gate, wq_up, s_up, wq_down, s_down):
        import jax, jax.numpy as jnp
        import numpy as np
        DIM = 256
        HID = 704
        ZERO_POINT = 128.0

        def _qlinear(x, wq, scale):
            W = (wq.astype(jnp.float32) - ZERO_POINT) * scale[:, None]
            return jnp.einsum('bsd,hd->bsh', x, W)
        gate = _qlinear(x, wq_gate, s_gate)
        gate = jax.nn.silu(gate)
        up = _qlinear(x, wq_up, s_up)
        return _qlinear(gate * up, wq_down, s_down)

    def _L1_attn_ref(hidden_states, w_qa, q_a_ln_w, w_qb, w_kva, kv_a_ln_w, w_kvb, w_o):
        import jax, jax.numpy as jnp
        import numpy as np
        HID = 256
        H = 16
        QLR = 192
        KVLR = 64
        DN = 128
        DR = 64
        DV = 128
        DQ = DN + DR
        B = 2
        S = 256
        THETA = 10000.0
        EPS = 1e-06

        def rms_norm(x, w, eps=EPS):
            x32 = x.astype(jnp.float32)
            var = jnp.mean(x32 * x32, axis=-1, keepdims=True)
            return (w * (x32 * jax.lax.rsqrt(var + eps))).astype(x.dtype)

        def rotate_half(x):
            x1, x2 = jnp.split(x, 2, axis=-1)
            return jnp.concatenate((-x2, x1), axis=-1)

        def rope_tables(seq_len, dim, base=THETA):
            inv_freq = 1.0 / base ** (jnp.arange(0, dim, 2, dtype=jnp.float32) / dim)
            t = jnp.arange(seq_len, dtype=jnp.float32)
            freqs = jnp.outer(t, inv_freq)
            emb = jnp.concatenate((freqs, freqs), -1)
            return (jnp.cos(emb), jnp.sin(emb))
        b, s, _ = hidden_states.shape
        scale = DQ ** (-0.5)
        cos, sin = rope_tables(s, DR)
        cq = rms_norm(hidden_states @ w_qa.T, q_a_ln_w)
        q = (cq @ w_qb.T).reshape(b, s, H, DQ).transpose(0, 2, 1, 3)
        q_nope, q_pe = (q[..., :DN], q[..., DN:])
        q_pe = q_pe * cos + rotate_half(q_pe) * sin
        ckv = hidden_states @ w_kva.T
        k_pe = ckv[..., KVLR:].reshape(b, s, 1, DR).transpose(0, 2, 1, 3)
        k_pe = k_pe * cos + rotate_half(k_pe) * sin
        ckv_l = rms_norm(ckv[..., :KVLR], kv_a_ln_w)
        kv = (ckv_l @ w_kvb.T).reshape(b, s, H, DN + DV).transpose(0, 2, 1, 3)
        k_nope, v = (kv[..., :DN], kv[..., DN:])
        q_full = jnp.concatenate([q_nope, q_pe], axis=-1)
        k_full = jnp.concatenate([k_nope, jnp.broadcast_to(k_pe, (b, H, s, DR))], axis=-1)
        scores = jnp.einsum('bhqd,bhkd->bhqk', q_full, k_full) * scale
        causal = jnp.triu(jnp.ones((s, s), dtype=bool), k=1)
        scores = jnp.where(causal, -jnp.inf, scores)
        attn = jax.nn.softmax(scores.astype(jnp.float32), axis=-1).astype(q_full.dtype)
        out = jnp.einsum('bhqk,bhkd->bhqd', attn, v)
        out = out.transpose(0, 2, 1, 3).reshape(b, s, H * DV)
        return out @ w_o.T

    def _L1_ffn_ref(hidden_states, router_w, e_bias, W_gate, W_up, W_down, shared_gate, shared_up, shared_down):
        import math
        import jax, jax.numpy as jnp
        import numpy as np
        from jax import lax
        D = 256
        I = 128
        E = 32
        K = 4
        NG = 8
        TKG = 3
        NSH = 2
        SCALE = 2.5
        CF = 1.25
        B, S = (2, 256)

        def _router(x, router_w, e_bias):
            scores = jax.nn.sigmoid(x @ router_w.T)
            sc = scores + e_bias[None, :]
            T = x.shape[0]
            gs = sc.reshape(T, NG, E // NG)
            group_scores = lax.top_k(gs, 2)[0].sum(-1)
            _, gidx = lax.top_k(group_scores, TKG)
            gmask = jnp.zeros((T, NG), sc.dtype).at[jnp.arange(T)[:, None], gidx].set(1.0)
            smask = jnp.repeat(gmask, E // NG, axis=1)
            masked = jnp.where(smask > 0, sc, 0.0)
            _, topk_idx = lax.top_k(masked, K)
            topk_w = jnp.take_along_axis(scores, topk_idx, axis=1)
            topk_w = topk_w / (topk_w.sum(-1, keepdims=True) + 1e-20)
            topk_w = topk_w * SCALE
            return (topk_idx.astype(jnp.int32), topk_w)

        def _moe_forward(hidden_states, router_w, e_bias, W_gate, W_up, W_down, shared_gate, shared_up, shared_down):
            b, s, d = hidden_states.shape
            T = b * s
            C = int(math.ceil(CF * T / E))
            EC = E * C
            x = hidden_states.reshape(T, d)
            topk_idx, topk_w = _router(x, router_w, e_bias)
            expert_flat = topk_idx.reshape(-1)
            w_flat = topk_w.reshape(-1)
            tok_flat = jnp.repeat(jnp.arange(T, dtype=jnp.int32), K)
            sort_ix = jnp.argsort(expert_flat)
            e_sorted = expert_flat[sort_ix]
            tok_s = tok_flat[sort_ix]
            w_s = w_flat[sort_ix]
            counts = jnp.zeros(E, jnp.int32).at[e_sorted].add(1)
            group_start = jnp.concatenate([jnp.zeros(1, jnp.int32), jnp.cumsum(counts)[:-1].astype(jnp.int32)])
            pos = jnp.arange(T * K, dtype=jnp.int32) - group_start[e_sorted]
            valid = pos < C
            dest = e_sorted * C + jnp.where(valid, pos, 0)
            slots_token = jnp.zeros(EC, jnp.int32).at[dest].add(jnp.where(valid, tok_s, 0))
            slots_w = jnp.zeros(EC, w_s.dtype).at[dest].add(jnp.where(valid, w_s, 0.0))
            Xp = x[slots_token].reshape(E, C, d)
            G = jnp.einsum('ecd,edi->eci', Xp, W_gate)
            U = jnp.einsum('ecd,edi->eci', Xp, W_up)
            Y = jnp.einsum('eci,eid->ecd', jax.nn.silu(G) * U, W_down)
            Yf = Y.reshape(EC, d) * slots_w[:, None]
            out = jnp.zeros((T, d), x.dtype).at[slots_token].add(Yf)
            shared = jax.nn.silu(x @ shared_gate.T) * (x @ shared_up.T) @ shared_down.T
            return (out + shared).reshape(b, s, d)
        return _moe_forward(hidden_states, router_w, e_bias, W_gate, W_up, W_down, shared_gate, shared_up, shared_down)
    x = L0_attn_hidden_states
    x = _layernorm(x + _L0_attn_ref(x, L0_attn_Wr, L0_attn_Wk, L0_attn_Wv, L0_attn_Wo, L0_attn_time_decay, L0_attn_time_first, L0_attn_time_mix_k, L0_attn_time_mix_v, L0_attn_time_mix_r), axis=-1)
    x = _layernorm(x + _L0_ffn_ref(x, L0_ffn_wq_gate, L0_ffn_s_gate, L0_ffn_wq_up, L0_ffn_s_up, L0_ffn_wq_down, L0_ffn_s_down), axis=-1)
    x = _layernorm(x + _L1_attn_ref(x, L1_attn_w_qa, L1_attn_q_a_ln_w, L1_attn_w_qb, L1_attn_w_kva, L1_attn_kv_a_ln_w, L1_attn_w_kvb, L1_attn_w_o), axis=-1)
    x = _layernorm(x + _L1_ffn_ref(x, L1_ffn_router_w, L1_ffn_e_bias, L1_ffn_W_gate, L1_ffn_W_up, L1_ffn_W_down, L1_ffn_shared_gate, L1_ffn_shared_up, L1_ffn_shared_down), axis=-1)
    return x

_drawn_inputs = setup_inputs


def setup_inputs(seed=0):
    import zlib

    import numpy as np

    out = dict(_drawn_inputs(seed))
    spreads = {'L0_attn_time_mix_k': (0.5, 0.6),
     'L0_attn_time_mix_v': (0.5, 0.6),
     'L0_attn_time_mix_r': (0.5, 0.6),
     'L1_attn_q_a_ln_w': (1.0, 0.2),
     'L1_attn_kv_a_ln_w': (1.0, 0.2),
     'L1_ffn_e_bias': (0.0, 0.8)}
    factors = {'L0_attn_Wr': 5.383,
     'L0_attn_time_first': 7.638,
     'L0_ffn_s_gate': 8.0,
     'L0_ffn_s_up': 8.0,
     'L0_ffn_s_down': 8.0,
     'L1_ffn_router_w': 8.0,
     'L1_ffn_W_gate': 7.616,
     'L1_ffn_W_up': 7.491,
     'L1_ffn_W_down': 7.499,
     'L1_ffn_shared_gate': 3.395,
     'L1_ffn_shared_up': 3.355,
     'L1_ffn_shared_down': 3.354}
    for name, (base, spread) in spreads.items():
        noise = np.random.default_rng([zlib.crc32(name.encode()), seed]).standard_normal(out[name].shape)
        drawn = base * np.exp(spread * noise) if base else spread * noise
        out[name] = jnp.asarray(drawn.astype(out[name].dtype))
    for name, factor in factors.items():
        out[name] = (out[name] * factor).astype(out[name].dtype)
    return out
```

```python
import numpy as np
import concourse.bass as bass
from concourse import mybir
from contextlib import ExitStack

F32 = mybir.dt.float32
F32R = mybir.dt.float32r
BF16 = mybir.dt.bfloat16
U32 = mybir.dt.uint32
I32 = mybir.dt.int32
ALU = mybir.AluOpType
ACT = mybir.ActivationFunctionType
AX = mybir.AxisListType

P = 128
D = 256
KD = D // P
SEQ = 256
TOKENS = 16 * SEQ
BLK = 512
BS = BLK // SEQ
BT = BLK // P
NB = TOKENS // BLK
LN_EPS = 1e-5

HH, HL, LH = (0, 0), (0, 1), (1, 0)
PARTS = (HH, HL, LH)


def over_blocks(eng, body):
    body(0, first=True, last=False)
    with eng.Fori(1, NB - 1) as blk:
        body(blk, first=False, last=False)
    body(NB - 1, first=False, last=True)


def wait_reuse(eng, sem, n, depth):
    if isinstance(n, int) and n < depth:
        return
    eng.wait_ge(sem, n - depth + 1)


def wait_first(eng, sem, value, passed):
    eng.wait_ge(sem, value)
    eng.sem_inc(passed, 1)


class Scope:

    def __init__(self, nc, ctx, phase):
        self.nc, self.ctx, self.phase = nc, ctx, phase
        self.sems = []
        ctx.callback(self.clear)

    def clear(self):
        self.nc.clear_and_free_semaphores(self.sems)
        self.nc.all_engine_barrier()

    def sb(self, name, shape, dt=F32):
        return self.ctx.enter_context(self.nc.sbuf_tensor(f"{self.phase}_{name}", shape, dt))

    def ps(self, name):
        return self.ctx.enter_context(self.nc.psum_tensor(f"{self.phase}_{name}", [P, 512], F32))

    def sem(self, name):
        self.sems.append(self.nc.alloc_semaphore(name=f"{self.phase}_{name}"))
        return self.sems[-1]


def rows(dram, blk):
    return dram[bass.ds(blk * BLK, BLK), :].rearrange("(j p) d -> p j d", p=P)


CH = 16
WCOLS = 3 * D + D


def rwkv_phase(nc, x_t, x_tok, w_rkvo, decay, first_u, mixes, x1):
    with ExitStack() as ctx:
        s = Scope(nc, ctx, "rwkv")
        w_part = [s.sb("w_high", [P, CH, WCOLS], F32R), s.sb("w_low", [P, CH, WCOLS], F32R)]
        w_raw = s.sb("w_raw", [P, 2, WCOLS])
        decay_w = s.sb("decay_w", [P, CH])
        decay_e = s.sb("decay_e", [P, CH])
        bonus_u = s.sb("bonus_u", [P, CH])
        mix = s.sb("mix", [P, 3 * KD])
        mix_rest = s.sb("mix_rest", [P, 3 * KD])
        x_in = s.sb("x_in", [P, KD, BS, SEQ + 1])
        mixed = s.sb("mixed", [P, 3, KD, BLK])
        m_part = [s.sb("m_high", [P, 3, KD, BLK], F32R), s.sb("m_low", [P, 3, KD, BLK], F32R)]
        gate = s.sb("gate", [P, 2, BLK])
        key = s.sb("key", [P, 2, BLK])
        kv = s.sb("kv", [P, BLK])
        state = s.sb("state", [P, BS, SEQ + 1])
        o_part = [s.sb("o_high", [P, 2, BLK], F32R), s.sb("o_low", [P, 2, BLK], F32R)]
        x_res = s.sb("x_res", [P, BT, D])
        stats = s.sb("stats", [P, BT, 6])
        moments = s.sb("moments", [P, BT, 2])
        minus_half = s.sb("minus_half", [P, BT])
        var_eps = s.sb("var_eps", [P, BT])
        rstd = s.sb("rstd", [P, BT])
        proj_ps = [[s.ps(f"{q}{i}") for q in ("r", "k", "v")] for i in range(2)]
        out_ps = [s.ps("out0"), s.ps("out1")]

        consts_in = s.sem("consts_in")
        passed = s.sem("passed")
        raw_in = [s.sem("raw_in0"), s.sem("raw_in1")]
        w_high_done = s.sem("w_high_done")
        w_low_done = s.sem("w_low_done")
        x_in_done = s.sem("x_in_done")
        res_in = s.sem("res_in")
        stored = s.sem("stored")
        zeroed = s.sem("zeroed")
        decay_exp = s.sem("decay_exp")
        decay_done = s.sem("decay_done")
        rest_done = s.sem("rest_done")
        shift_scaled = s.sem("shift_scaled")
        mixed_done = s.sem("mixed_done")
        m_high_done = s.sem("m_high_done")
        m_low_done = s.sem("m_low_done")
        projected = [s.sem(f"{q}_projected") for q in ("r", "k", "v")]
        gate_done = s.sem("gate_done")
        key_done = s.sem("key_done")
        kv_done = s.sem("kv_done")
        scan_done = s.sem("scan_done")
        wkv_done = s.sem("wkv_done")
        gated_done = s.sem("gated_done")
        o_high_done = s.sem("o_high_done")
        o_low_done = s.sem("o_low_done")
        step_out_done = s.sem("step_out_done")
        res_added = s.sem("res_added")
        stats_done = s.sem("stats_done")
        var_done = s.sem("var_done")
        rstd_done = s.sem("rstd_done")
        normed = s.sem("normed")

        def x_now(k):
            return x_in[:, k, :, 1:SEQ + 1]

        def x_before(k):
            return x_in[:, k, :, 0:SEQ]

        block = ctx.enter_context(nc.Block())

        @block.sync
        def _(sp):
            sp.dma_start(decay_e[:, :], decay).then_inc(consts_in, 16)
            sp.dma_start(bonus_u[:, :], first_u).then_inc(consts_in, 16)
            sp.dma_start(mix[:, :], mixes).then_inc(consts_in, 16)

            def load_x(blk):
                for k in range(KD):
                    sp.dma_start(x_now(k), x_t[k * P:(k + 1) * P, bass.ds(blk * BLK, BLK)]
                                 .rearrange("p (s t) -> p s t", s=BS)).then_inc(x_in_done, 16)

            def load_w(c):
                if c >= 2:
                    sp.wait_ge(w_high_done, c - 1)
                    sp.wait_ge(w_low_done, c - 1)
                sp.dma_start(w_raw[:, c % 2, :], w_rkvo[c]).then_inc(raw_in[c % 2], 16)

            sp.wait_ge(zeroed, 1)
            load_x(0)
            for c in range(4):
                load_w(c)

            def body(blk, first, last):
                if not first:
                    sp.wait_ge(stored, 16 * blk)
                sp.dma_start(x_res[:, :, :], rows(x_tok, blk)).then_inc(res_in, 16)
                if not last:
                    sp.wait_ge(shift_scaled, 3 * blk + 3)
                    sp.wait_ge(mixed_done, 3 * blk + 3)
                    load_x(blk + 1)
                if first:
                    for c in range(4, CH):
                        load_w(c)
                sp.wait_ge(normed, blk + 1)
                sp.dma_start(rows(x1, blk), x_res[:, :, :]).then_inc(stored, 16)

            over_blocks(sp, body)
            sp.wait_ge(stored, 16 * NB)

        @block.gpsimd
        def _(pool):
            nc.gpsimd.memset(minus_half[:, :], -0.5)
            nc.gpsimd.memset(x_in[:, :, :, 0:1], 0.0).then_inc(zeroed, 1)

            def body(blk, first, last):
                for c in range(CH):
                    n = CH * blk + c
                    pool.wait_ge(gate_done, n + 1)
                    pool.wait_ge(wkv_done, n + 1)
                    nc.gpsimd.tensor_tensor(gate[:, c % 2, :], key[:, c % 2, :], gate[:, c % 2, :],
                                            ALU.mult).then_inc(gated_done, 1)
                    if c == 2 and not first:
                        rsqrt(blk - 1)

            def rsqrt(blk):
                pool.wait_ge(var_done, blk + 1)
                nc.gpsimd.tensor_tensor(rstd[:, :], var_eps[:, :], minus_half[:, :], ALU.pow)\
                    .then_inc(rstd_done, 1)

            over_blocks(pool, body)
            rsqrt(NB - 1)

        @block.scalar
        def _(act):
            act.wait_ge(consts_in, 48)
            nc.scalar.activation(decay_e[:, :], decay_e[:, :], ACT.Exp).then_inc(decay_exp, 1)
            act.wait_ge(decay_exp, 1)
            nc.scalar.activation(decay_w[:, :], decay_e[:, :], ACT.Exp, scale=-1.0)\
                .then_inc(decay_done, 1)

            def shift_scale(blk, q):
                act.wait_ge(x_in_done, 32 * (blk + 1))
                if not (isinstance(blk, int) and blk == 0):
                    act.wait_ge(m_high_done, 3 * blk)
                    act.wait_ge(m_low_done, 3 * blk)
                for k in range(KD):
                    last = nc.scalar.activation(mixed[:, q, k, :].rearrange("p (s t) -> p s t", s=BS),
                                                x_before(k), ACT.Copy,
                                                scale=mix_rest[:, q * KD + k:q * KD + k + 1])
                last.then_inc(shift_scaled, 1)

            def m_high(blk, q):
                act.wait_ge(mixed_done, 3 * blk + q + 1)
                if not (isinstance(blk, int) and blk == 0):
                    act.wait_ge(projected[q], CH * blk)
                nc.scalar.activation(m_part[0][:, q, :, :], mixed[:, q, :, :], ACT.Copy)\
                    .then_inc(m_high_done, 1)

            def w_high(c):
                act.wait_ge(raw_in[c % 2], 16 * (c // 2 + 1))
                nc.scalar.activation(w_part[0][:, c, :], w_raw[:, c % 2, :], ACT.Copy)\
                    .then_inc(w_high_done, 1)

            def o_high(n, c):
                act.wait_ge(gated_done, n + 1)
                wait_reuse(act, step_out_done, n, 2)
                nc.scalar.activation(o_part[0][:, c % 2, :], gate[:, c % 2, :], ACT.Copy)\
                    .then_inc(o_high_done, 1)

            act.wait_ge(rest_done, 1)
            for q in range(3):
                shift_scale(0, q)
            for q in range(3):
                m_high(0, q)
            for c in range(3):
                w_high(c)

            def body(blk, first, last):
                for c in range(CH):
                    n = CH * blk + c
                    act.wait_ge(projected[0], n + 1)
                    wait_reuse(act, o_high_done, n, 2)
                    wait_reuse(act, o_low_done, n, 2)
                    nc.scalar.activation(gate[:, c % 2, :], proj_ps[c % 2][0][:, :], ACT.Sigmoid)\
                        .then_inc(gate_done, 1)
                    if c == CH - 1 and not last:
                        m_high(blk + 1, 0)
                    act.wait_ge(projected[1], n + 1)
                    wait_reuse(act, gated_done, n, 2)
                    nc.scalar.activation(key[:, c % 2, :], proj_ps[c % 2][1][:, :], ACT.Copy)\
                        .then_inc(key_done, 1)
                    if c == CH - 1 and not last:
                        m_high(blk + 1, 1)
                        m_high(blk + 1, 2)
                    if not (first and c == 0):
                        o_high(n - 1, c - 1)
                    if first and c + 3 < CH:
                        w_high(c + 3)
                    if 4 <= c < 7 and not last:
                        shift_scale(blk + 1, c - 4)

            over_blocks(act, body)
            o_high(CH * NB - 1, CH - 1)

        @block.vector
        def _(dve):
            dve.wait_ge(consts_in, 48)
            nc.vector.tensor_scalar(mix_rest[:, :], mix[:, :], -1.0, 1.0, ALU.mult, ALU.add)\
                .then_inc(rest_done, 1)
            nc.vector.memset(state[:, :, 0:1], 0.0)
            dve.wait_ge(decay_done, 1)

            def mix_now(blk, q):
                dve.wait_ge(shift_scaled, 3 * blk + q + 1)
                for k in range(KD):
                    m = mixed[:, q, k, :].rearrange("p (s t) -> p s t", s=BS)
                    last = nc.vector.scalar_tensor_tensor(m, x_now(k), mix[:, q * KD + k:q * KD + k + 1],
                                                          m, ALU.mult, ALU.add)
                last.then_inc(mixed_done, 1)

            def m_low(blk, q):
                dve.wait_ge(m_high_done, 3 * blk + q + 1)
                nc.vector.tensor_tensor(m_part[1][:, q, :, :], mixed[:, q, :, :],
                                        m_part[0][:, q, :, :].bitcast(F32), ALU.subtract)\
                    .then_inc(m_low_done, 1)

            def w_low(c):
                dve.wait_ge(w_high_done, c + 1)
                nc.vector.tensor_tensor(w_part[1][:, c, :], w_raw[:, c % 2, :],
                                        w_part[0][:, c, :].bitcast(F32), ALU.subtract)\
                    .then_inc(w_low_done, 1)

            def o_low(n, c):
                dve.wait_ge(o_high_done, n + 1)
                nc.vector.tensor_tensor(o_part[1][:, c % 2, :], gate[:, c % 2, :],
                                        o_part[0][:, c % 2, :].bitcast(F32), ALU.subtract)\
                    .then_inc(o_low_done, 1)

            def layer_norm(blk):
                dve.wait_ge(step_out_done, CH * (blk + 1))
                dve.wait_ge(res_in, 16 * (blk + 1))
                for h in range(2):
                    last = nc.vector.tensor_tensor(x_res[:, 2 * h:2 * h + 2, :],
                                                   out_ps[h][:, :].rearrange("p (j d) -> p j d", d=D),
                                                   x_res[:, 2 * h:2 * h + 2, :], ALU.add)
                last.then_inc(res_added, 1)
                dve.wait_ge(res_added, blk + 1)
                for j in range(BT):
                    last = nc.vector.bn_stats(stats[:, j, :], x_res[:, j, :])
                last.then_inc(stats_done, 1)
                wait_first(dve, stats_done, 2 * blk + 1, passed)
                for j in range(BT):
                    last = nc.vector.bn_aggr(moments[:, j, :], stats[:, j, :])
                last.then_inc(stats_done, 1)
                dve.wait_ge(stats_done, 2 * blk + 2)
                nc.vector.tensor_scalar(var_eps[:, :], moments[:, :, 1], LN_EPS, None, ALU.add)\
                    .then_inc(var_done, 1)

            def apply_norm(blk):
                dve.wait_ge(rstd_done, blk + 1)
                for j in range(BT):
                    last = nc.vector.tensor_scalar(x_res[:, j, :], x_res[:, j, :], moments[:, j, 0:1],
                                                   rstd[:, j:j + 1], ALU.subtract, ALU.mult)
                last.then_inc(normed, 1)

            for q in range(3):
                mix_now(0, q)
            for q in range(3):
                m_low(0, q)
            for c in range(3):
                w_low(c)

            def body(blk, first, last):
                for c in range(CH):
                    n = CH * blk + c
                    if c == CH - 1 and not last:
                        m_low(blk + 1, 0)
                    dve.wait_ge(projected[2], n + 1)
                    dve.wait_ge(key_done, n + 1)
                    wait_reuse(dve, wkv_done, n, 1)
                    nc.vector.tensor_tensor(kv[:, :], proj_ps[c % 2][2][:, :], key[:, c % 2, :],
                                            ALU.mult).then_inc(kv_done, 1)
                    dve.wait_ge(kv_done, n + 1)
                    for q in range(BS):
                        last_scan = nc.vector.tensor_tensor_scan(
                            out=state[:, q, 1:SEQ + 1],
                            data0=decay_w[:, c:c + 1].to_broadcast([P, SEQ]),
                            data1=kv[:, q * SEQ:(q + 1) * SEQ], initial=0.0,
                            op0=ALU.mult, op1=ALU.add)
                    last_scan.then_inc(scan_done, 1)
                    dve.wait_ge(scan_done, n + 1)
                    nc.vector.scalar_tensor_tensor(key[:, c % 2, :].rearrange("p (s t) -> p s t", s=BS),
                                                   kv[:, :].rearrange("p (s t) -> p s t", s=BS),
                                                   bonus_u[:, c:c + 1], state[:, :, 0:SEQ],
                                                   ALU.mult, ALU.add).then_inc(wkv_done, 1)
                    if c == CH - 1 and not last:
                        m_low(blk + 1, 1)
                        m_low(blk + 1, 2)
                    if not (first and c == 0):
                        o_low(n - 1, c - 1)
                    if first and c + 3 < CH:
                        w_low(c + 3)
                    if c == 1 and not first:
                        layer_norm(blk - 1)
                    if c == 3 and not first:
                        apply_norm(blk - 1)
                    if 5 <= c < 8 and not last:
                        mix_now(blk + 1, c - 5)

            over_blocks(dve, body)
            o_low(CH * NB - 1, CH - 1)
            layer_norm(NB - 1)
            apply_norm(NB - 1)

        @block.tensor
        def _(pe):
            def project(blk, c, first):
                n = CH * blk + c
                if first:
                    pe.wait_ge(w_high_done, c + 1)
                    pe.wait_ge(w_low_done, c + 1)
                for q, read in enumerate((gate_done, key_done, kv_done)):
                    if c == 0:
                        pe.wait_ge(m_high_done, 3 * blk + q + 1)
                        pe.wait_ge(m_low_done, 3 * blk + q + 1)
                    wait_reuse(pe, read, n, 2)
                    for i, (wp, mp) in enumerate(PARTS):
                        for k in range(KD):
                            col = (q * KD + k) * P
                            last = nc.tensor.matmul(proj_ps[c % 2][q][:, :],
                                                    w_part[wp][:, c, col:col + P],
                                                    m_part[mp][:, q, k, :],
                                                    start=(i == 0 and k == 0),
                                                    stop=(i == 2 and k == KD - 1))
                    last.then_inc(projected[q], 1)

            def step_out(blk, c):
                n = CH * blk + c
                pe.wait_ge(o_high_done, n + 1)
                pe.wait_ge(o_low_done, n + 1)
                if c == 0 and not (isinstance(blk, int) and blk == 0):
                    pe.wait_ge(res_added, blk)
                for j in range(BT):
                    for i, (op, wp) in enumerate(PARTS):
                        last = nc.tensor.matmul(out_ps[j // 2][:, (j % 2) * D:(j % 2 + 1) * D],
                                                o_part[op][:, c % 2, j * P:(j + 1) * P],
                                                w_part[wp][:, c, 3 * D:4 * D],
                                                start=(c == 0 and i == 0 and j % 2 == 0),
                                                stop=(c == CH - 1 and i == 2),
                                                skip_group_check=True)
                last.then_inc(step_out_done, 1)

            def body(blk, first, last):
                for c in range(CH):
                    project(blk, c, first)
                    if c >= 2:
                        step_out(blk, c - 2)
                    elif not first:
                        step_out(blk - 1, CH - 2 + c)

            over_blocks(pe, body)
            step_out(NB - 1, CH - 2)
            step_out(NB - 1, CH - 1)


HID = 704
HC = -(-HID // P)
HPAD = HC * P
HTAIL = HID - (HC - 1) * P
ZERO_POINT = 128.0


def ffn_phase(nc, ident_dram, wq_gate_up, wq_down, s_gate_up, s_down, x1, x2):
    with ExitStack() as ctx:
        s = Scope(nc, ctx, "ffn")
        ident = s.sb("ident", [P, P])
        code = s.sb("code", [P, 2, KD, HID], I32)
        code_down = s.sb("code_down", [P, HC, D], I32)
        centred = s.sb("centred", [P, 2, KD, HID])
        centred_down = s.sb("centred_down", [P, HC, D])
        w_part = [s.sb("w_high", [P, 2, KD, HPAD], F32R), s.sb("w_low", [P, 2, KD, HPAD], F32R)]
        wd_part = [s.sb("wd_high", [P, HC, D], F32R), s.sb("wd_low", [P, HC, D], F32R)]
        scale_hid = s.sb("scale_hid", [P, 2, HC])
        scale_out = s.sb("scale_out", [P, 2, D])
        x_rows = s.sb("x_rows", [P, BT, D])
        x_res = s.sb("x_res", [P, BT, D])
        xt_part = [s.sb("xt_high", [P, KD, BLK], F32R), s.sb("xt_low", [P, KD, BLK], F32R)]
        gate = s.sb("gate", [P, 2, BLK])
        hidden = s.sb("hidden", [P, 2, BLK])
        h_part = [s.sb("h_high", [P, 2, BLK], F32R), s.sb("h_low", [P, 2, BLK], F32R)]
        y_rows = s.sb("y_rows", [P, BT, D])
        x_out = s.sb("x_out", [P, BT, D])
        stats = s.sb("stats", [P, BT, 6])
        moments = s.sb("moments", [P, BT, 2])
        minus_half = s.sb("minus_half", [P, BT])
        var_eps = s.sb("var_eps", [P, BT])
        rstd = s.sb("rstd", [P, BT])
        hid_ps = [[s.ps(f"{q}{i}") for q in ("gate", "up")] for i in range(2)]
        out_ps = [s.ps("out0"), s.ps("out1")]
        xt_ps = [s.ps("xt0"), s.ps("xt1")]

        codes_in = s.sem("codes_in")
        consts_in = s.sem("consts_in")
        passed = s.sem("passed")
        rows_in = s.sem("rows_in")
        res_in = s.sem("res_in")
        stored = s.sem("stored")
        padded = s.sem("padded")
        half_set = s.sem("half_set")
        centred_done = s.sem("centred_done")
        w_high_done = s.sem("w_high_done")
        w_low_done = s.sem("w_low_done")
        transposed = s.sem("transposed")
        xt_high_done = s.sem("xt_high_done")
        xt_low_done = s.sem("xt_low_done")
        gate_ready = s.sem("gate_ready")
        up_ready = s.sem("up_ready")
        gate_done = s.sem("gate_done")
        hidden_done = s.sem("hidden_done")
        h_high_done = s.sem("h_high_done")
        h_low_done = s.sem("h_low_done")
        step_out_done = s.sem("step_out_done")
        scaled = s.sem("scaled")
        res_added = s.sem("res_added")
        stats_done = s.sem("stats_done")
        var_done = s.sem("var_done")
        rstd_done = s.sem("rstd_done")
        normed = s.sem("normed")

        block = ctx.enter_context(nc.Block())

        @block.sync
        def _(sp):
            sp.dma_start(ident[:, :], ident_dram).then_inc(consts_in, 16)
            for i in range(2):
                sp.dma_start(code[:, i, :, :], wq_gate_up[i].rearrange("(k p) h -> p k h", p=P))\
                    .then_inc(codes_in, 16)
            sp.dma_start(code_down[:, 0:HC - 1, :],
                         wq_down[0:(HC - 1) * P, :].rearrange("(c p) d -> p c d", p=P)).then_inc(codes_in, 16)
            sp.dma_start(code_down[0:HTAIL, HC - 1, :], wq_down[(HC - 1) * P:HID, :]).then_inc(codes_in, 16)
            sp.dma_start(scale_hid[:, :, :], s_gate_up).then_inc(consts_in, 16)
            for i in range(2):
                sp.dma_start(scale_out[:, i, :], s_down.partition_broadcast(P)).then_inc(consts_in, 16)

            sp.dma_start(x_rows[:, :, :], rows(x1, 0)).then_inc(rows_in, 16)

            def body(blk, first, last):
                if not first:
                    sp.wait_ge(res_added, blk)
                sp.dma_start(x_res[:, :, :], rows(x1, blk)).then_inc(res_in, 16)
                if not last:
                    sp.wait_ge(transposed, blk + 1)
                    sp.dma_start(x_rows[:, :, :], rows(x1, blk + 1)).then_inc(rows_in, 16)
                sp.wait_ge(normed, blk + 1)
                sp.dma_start(rows(x2, blk), x_out[:, :, :]).then_inc(stored, 16)

            over_blocks(sp, body)
            sp.wait_ge(stored, 16 * NB)

        @block.gpsimd
        def _(pool):
            nc.gpsimd.memset(minus_half[:, :], -0.5).then_inc(half_set, 1)
            pool.wait_ge(half_set, 1)

            def body(blk, first, last):
                pool.wait_ge(var_done, blk + 1)
                nc.gpsimd.tensor_tensor(rstd[:, :], var_eps[:, :], minus_half[:, :], ALU.pow)\
                    .then_inc(rstd_done, 1)

            over_blocks(pool, body)

        @block.scalar
        def _(act):
            def w_high(part):
                act.wait_ge(centred_done, part + 1)
                if part < 2 * KD:
                    i, k = part // KD, part % KD
                    out, src = w_part[0][:, i, k, 0:HID], centred[:, i, k, :]
                else:
                    out, src = wd_part[0][:, :, :], centred_down[:, :, :]
                nc.scalar.activation(out, src, ACT.Copy).then_inc(w_high_done, 1)

            def xt_high(blk):
                act.wait_ge(transposed, blk + 1)
                if not (isinstance(blk, int) and blk == 0):
                    act.wait_ge(up_ready, HC * blk)
                for k in range(KD):
                    nc.scalar.activation(xt_part[0][:, k, :], xt_ps[k][:, :], ACT.Copy)\
                        .then_inc(xt_high_done, 1)

            def h_high(n, j):
                act.wait_ge(hidden_done, n + 1)
                wait_reuse(act, step_out_done, n, 2)
                nc.scalar.activation(h_part[0][:, j % 2, :], hidden[:, j % 2, :], ACT.Copy)\
                    .then_inc(h_high_done, 1)

            for part in range(2 * KD + 1):
                w_high(part)
            xt_high(0)

            def body(blk, first, last):
                for j in range(HC):
                    n = HC * blk + j
                    act.wait_ge(gate_ready, n + 1)
                    wait_reuse(act, hidden_done, n, 2)
                    nc.scalar.activation(gate[:, j % 2, :], hid_ps[j % 2][0][:, :], ACT.Silu,
                                         scale=scale_hid[:, 0, j:j + 1]).then_inc(gate_done, 1)
                    if j == HC - 1 and not last:
                        xt_high(blk + 1)
                    if not (first and j == 0):
                        h_high(n - 1, (j - 1) % 2)

            over_blocks(act, body)
            h_high(HC * NB - 1, HC - 1)

        @block.vector
        def _(dve):
            nc.vector.memset(code_down[HTAIL:P, HC - 1, :], int(ZERO_POINT)).then_inc(padded, 1)
            for i in range(2):
                nc.vector.memset(w_part[i][:, :, :, HID:HPAD].bitcast(F32), 0.0).then_inc(padded, 1)
            dve.wait_ge(codes_in, 64)
            dve.wait_ge(padded, 1)
            for part in range(2 * KD + 1):
                if part < 2 * KD:
                    i, k = part // KD, part % KD
                    out, src = centred[:, i, k, :], code[:, i, k, :]
                else:
                    out, src = centred_down[:, :, :], code_down[:, :, :]
                nc.vector.tensor_scalar(out, src, -ZERO_POINT, None, ALU.add).then_inc(centred_done, 1)
            for part in range(2 * KD + 1):
                dve.wait_ge(w_high_done, part + 1)
                if part < 2 * KD:
                    i, k = part // KD, part % KD
                    out, src, high = (w_part[1][:, i, k, 0:HID], centred[:, i, k, :],
                                      w_part[0][:, i, k, 0:HID])
                else:
                    out, src, high = wd_part[1][:, :, :], centred_down[:, :, :], wd_part[0][:, :, :]
                nc.vector.tensor_tensor(out, src, high.bitcast(F32), ALU.subtract).then_inc(w_low_done, 1)

            def xt_low(blk):
                for k in range(KD):
                    dve.wait_ge(xt_high_done, KD * blk + k + 1)
                    nc.vector.tensor_tensor(xt_part[1][:, k, :], xt_ps[k][:, :],
                                            xt_part[0][:, k, :].bitcast(F32), ALU.subtract)\
                        .then_inc(xt_low_done, 1)

            def h_low(n, j):
                dve.wait_ge(h_high_done, n + 1)
                nc.vector.tensor_tensor(h_part[1][:, j % 2, :], hidden[:, j % 2, :],
                                        h_part[0][:, j % 2, :].bitcast(F32), ALU.subtract)\
                    .then_inc(h_low_done, 1)

            def layer_norm(blk):
                dve.wait_ge(step_out_done, HC * (blk + 1))
                if not (isinstance(blk, int) and blk == 0):
                    dve.wait_ge(normed, blk)
                for h in range(2):
                    last = nc.vector.tensor_tensor(y_rows[:, 2 * h:2 * h + 2, :],
                                                   out_ps[h][:, :].rearrange("p (j d) -> p j d", d=D),
                                                   scale_out[:, :, :], ALU.mult)
                last.then_inc(scaled, 1)
                dve.wait_ge(scaled, blk + 1)
                dve.wait_ge(res_in, 16 * (blk + 1))
                nc.vector.tensor_tensor(y_rows[:, :, :], y_rows[:, :, :], x_res[:, :, :], ALU.add).then_inc(res_added, 1)
                dve.wait_ge(res_added, blk + 1)
                for j in range(BT):
                    last = nc.vector.bn_stats(stats[:, j, :], y_rows[:, j, :])
                last.then_inc(stats_done, 1)
                wait_first(dve, stats_done, 2 * blk + 1, passed)
                for j in range(BT):
                    last = nc.vector.bn_aggr(moments[:, j, :], stats[:, j, :])
                last.then_inc(stats_done, 1)
                dve.wait_ge(stats_done, 2 * blk + 2)
                nc.vector.tensor_scalar(var_eps[:, :], moments[:, :, 1], LN_EPS, None, ALU.add)\
                    .then_inc(var_done, 1)

            def apply_norm(blk):
                dve.wait_ge(rstd_done, blk + 1)
                if not (isinstance(blk, int) and blk == 0):
                    dve.wait_ge(stored, 16 * blk)
                for j in range(BT):
                    last = nc.vector.tensor_scalar(x_out[:, j, :], y_rows[:, j, :], moments[:, j, 0:1],
                                                   rstd[:, j:j + 1], ALU.subtract, ALU.mult)
                last.then_inc(normed, 1)

            xt_low(0)
            dve.wait_ge(consts_in, 16 * 4)

            def body(blk, first, last):
                for j in range(HC):
                    n = HC * blk + j
                    dve.wait_ge(up_ready, n + 1)
                    dve.wait_ge(gate_done, n + 1)
                    wait_reuse(dve, h_low_done, n, 2)
                    nc.vector.scalar_tensor_tensor(hidden[:, j % 2, :], hid_ps[j % 2][1][:, :],
                                                   scale_hid[:, 1, j:j + 1], gate[:, j % 2, :],
                                                   ALU.mult, ALU.mult).then_inc(hidden_done, 1)
                    if j == HC - 1 and not last:
                        xt_low(blk + 1)
                    if not (first and j == 0):
                        h_low(n - 1, (j - 1) % 2)
                    if j == 1 and not first:
                        layer_norm(blk - 1)
                    if j == 2 and not first:
                        apply_norm(blk - 1)

            over_blocks(dve, body)
            h_low(HC * NB - 1, HC - 1)
            layer_norm(NB - 1)
            apply_norm(NB - 1)

        @block.tensor
        def _(pe):
            def transpose_rows(blk):
                pe.wait_ge(rows_in, 16 * (blk + 1))
                if not (isinstance(blk, int) and blk == 0):
                    pe.wait_ge(xt_low_done, KD * blk)
                for k in range(KD):
                    for j in range(BT):
                        last = nc.tensor.transpose(
                            xt_ps[k][:, j * P:(j + 1) * P],
                            x_rows[:, j, k * P:(k + 1) * P],
                            ident[:, :])
                last.then_inc(transposed, 1)

            def project(blk, j, first):
                n = HC * blk + j
                if j == 0:
                    pe.wait_ge(xt_high_done, KD * (blk + 1))
                    pe.wait_ge(xt_low_done, KD * (blk + 1))
                for i, (ready, read) in enumerate(((gate_ready, gate_done), (up_ready, hidden_done))):
                    if first and j == 0:
                        pe.wait_ge(w_high_done, KD * (i + 1))
                        pe.wait_ge(w_low_done, KD * (i + 1))
                        pe.wait_ge(padded, 3)
                    wait_reuse(pe, read, n, 2)
                    for q, (wp, xp) in enumerate(PARTS):
                        for k in range(KD):
                            last = nc.tensor.matmul(hid_ps[j % 2][i][:, :],
                                                    w_part[wp][:, i, k, j * P:(j + 1) * P],
                                                    xt_part[xp][:, k, :],
                                                    start=(q == 0 and k == 0),
                                                    stop=(q == 2 and k == KD - 1))
                    last.then_inc(ready, 1)

            def step_out(blk, j):
                n = HC * blk + j
                pe.wait_ge(h_high_done, n + 1)
                pe.wait_ge(h_low_done, n + 1)
                if isinstance(blk, int) and blk == 0:
                    if j == 0:
                        pe.wait_ge(w_high_done, 2 * KD + 1)
                        pe.wait_ge(w_low_done, 2 * KD + 1)
                elif j == 0:
                    pe.wait_ge(scaled, blk)
                for t in range(BT):
                    for i, (hp, wp) in enumerate(PARTS):
                        last = nc.tensor.matmul(out_ps[t // 2][:, (t % 2) * D:(t % 2 + 1) * D],
                                                h_part[hp][:, j % 2, t * P:(t + 1) * P],
                                                wd_part[wp][:, j, :],
                                                start=(j == 0 and i == 0 and t % 2 == 0),
                                                stop=(j == HC - 1 and i == 2),
                                                skip_group_check=True)
                last.then_inc(step_out_done, 1)

            pe.wait_ge(consts_in, 16 * 4)
            transpose_rows(0)

            def body(blk, first, last):
                for j in range(HC):
                    project(blk, j, first)
                    if j >= 2:
                        step_out(blk, j - 2)
                    elif not first:
                        step_out(blk - 1, HC - 2 + j)
                    if j == 3 and not last:
                        transpose_rows(blk + 1)

            over_blocks(pe, body)
            step_out(NB - 1, HC - 2)
            step_out(NB - 1, HC - 1)


NSEQ = TOKENS // SEQ
HEADS = 16
QLR = 192
QP = QLR // 2
KVL = 64
DN = 128
DR = 64
DV = 128
LATC = QLR + KVL + DR
RMS_EPS = 1e-6
SLOTS = 12
MLAC = QLR + KVL + KVL + D
HG = 4
MASKED = 1e30

TURNS = (("q1", 0, 0), ("o_before", 0, 0), ("q1", 1, 1), ("q1", 2, 2), ("k", 0, 2), ("q1", 3, 3),
         ("q0", 0, 4), ("o_before", 1, 4), ("q0", 1, 5), ("x", 0, 6), ("q0", 2, 6), ("q0", 3, 7),
         ("y_before", 0, 8), ("o0", 0, 9), ("o0", 1, 10), ("cq", 0, 10), ("y0", 0, 11))
FIRST_TURNS = 9


def turn_exists(kind, seq):
    if not isinstance(seq, int):
        return True
    if kind in ("o_before", "y_before"):
        return seq >= 1
    return seq + {"q0": 1, "k": 1, "x": 2, "cq": 2}.get(kind, 0) < NSEQ


def turns_before(seq, i, split_only=False):
    def counts(t, of):
        return turn_exists(t[0], of) and not (split_only and t[0][0] == "y")
    if not isinstance(seq, int):
        each = sum(counts(t, 1) for t in TURNS)
        return each * (seq - 1) + turns_before(1, i, split_only)
    done = sum(counts(t, of) for of in range(seq) for t in TURNS)
    return FIRST_TURNS + done + sum(counts(t, seq) for t in TURNS[:i])


def turn_of(kind, index):
    return next(i for i, t in enumerate(TURNS) if t[:2] == (kind, index))


def attention_phase(nc, ident_dram, w_lat, w_heads, w_pe, ln_q, ln_kv, rope_q, rope_k, mask_dram, x2, x3):
    with ExitStack() as ctx:
        s = Scope(nc, ctx, "mla")

        def both(name, shape):
            return [s.sb(name + "_high", shape, F32R), s.sb(name + "_low", shape, F32R)]

        ident = s.sb("ident", [P, P])
        mask = s.sb("mask", [P, SEQ])
        lnq = s.sb("lnq", [P, 2])
        lnkv = s.sb("lnkv", [P, KVL])
        rq = s.sb("rq", [P, 2, 2, DR])
        rk = s.sb("rk", [P, 2, 2, DR])
        w_raw = s.sb("w_raw", [P, 2, HG, MLAC])
        wl_raw = s.sb("wl_raw", [P, KD, LATC])
        wl_part = both("wl", [P, KD, LATC])
        wq_part = both("wq", [P, 2, 2 * HEADS * DR])
        wvo_part = both("wvo", [P, HEADS // 2, D])
        x_rows = s.sb("x_rows", [P, 2, D])
        x_res = s.sb("x_res", [P, 2, D])
        xt_part = both("xt", [P, KD, SEQ])
        squares = s.sb("squares", [P, QLR + KVL])
        mean_sq = s.sb("mean_sq", [P, 2])
        lat_rstd = s.sb("lat_rstd", [P, 2])
        cq_rows = s.sb("cq_rows", [P, 2, QLR])
        k_rows = s.sb("k_rows", [P, 2, KVL + DR])
        k_turn = s.sb("k_turn", [P, 2, 2, DR])
        cq_part = both("cq", [P, 2, SEQ])
        k_part = both("k", [P, 2, SEQ])
        v_part = both("v", [P, 2, 2, KVL])
        q_rows = s.sb("q_rows", [P, 2, HEADS, KVL + DR])
        q_cos = s.sb("q_cos", [P, 2, 512])
        q_sin = s.sb("q_sin", [P, 2, 512])
        q_part = both("q", [P, 2, HEADS * P])
        masked = s.sb("masked", [P, 2, 512])
        least = s.sb("least", [P, 2, HG])
        probs = s.sb("probs", [P, 3, 512])
        row_sum = s.sb("row_sum", [P, 2, HEADS])
        row_inv = s.sb("row_inv", [P, 8])
        p_part = both("p", [P, 2, 512])
        o_rows = s.sb("o_rows", [P, 2, HEADS * KVL])
        o_part = both("o", [P, 2, HEADS // 2, P])
        y_rows = s.sb("y_rows", [P, 2, D])
        x_out = s.sb("x_out", [P, 2, D])
        stats = s.sb("stats", [P, 2, 6])
        moments = s.sb("moments", [P, 2, 2])
        minus_half = s.sb("minus_half", [P, 2])
        var_eps = s.sb("var_eps", [P, 2])
        rstd = s.sb("rstd", [P, 2])
        score_ps = [s.ps("score0"), s.ps("score1")]
        pt_ps = [s.ps("pt0"), s.ps("pt1")]
        o_ps = [s.ps("o0"), s.ps("o1")]
        proj_ps = s.ps("proj")
        turn_ps = s.ps("turn")

        consts_in = s.sem("consts_in")
        passed = s.sem("passed")
        pe_in = s.sem("pe_in")
        raw_in = [s.sem("raw_in0"), s.sem("raw_in1")]
        rows_in = s.sem("rows_in")
        res_in = s.sem("res_in")
        stored = s.sem("stored")
        half_set = s.sem("half_set")
        wl_high = s.sem("wl_high")
        wl_low = s.sem("wl_low")
        wpe_high = s.sem("wpe_high")
        wpe_low = s.sem("wpe_low")
        multiplied = s.sem("multiplied")
        mult_high = s.sem("mult_high")
        mult_low = s.sem("mult_low")
        turn_filled = s.sem("turn_filled")
        turn_high = s.sem("turn_high")
        turn_read = s.sem("turn_read")
        lat_ready = s.sem("lat_ready")
        squared = s.sem("squared")
        ms_added = s.sem("ms_added")
        lat_rstd_done = s.sem("lat_rstd_done")
        lat_scaled = s.sem("lat_scaled")
        lat_done = s.sem("lat_done")
        v_high = s.sem("v_high")
        v_low = s.sem("v_low")
        q_ready = s.sem("q_ready")
        q_abs_done = s.sem("q_abs_done")
        q_turned = s.sem("q_turned")
        q_pe_done = s.sem("q_pe_done")
        scored = s.sem("scored")
        masked_done = s.sem("masked_done")
        exp_done = s.sem("exp_done")
        p_turned = s.sem("p_turned")
        p_high = s.sem("p_high")
        p_low = s.sem("p_low")
        summed = s.sem("summed")
        inv_done = s.sem("inv_done")
        o_normed = s.sem("o_normed")
        res_added = s.sem("res_added")
        stats_done = s.sem("stats_done")
        var_done = s.sem("var_done")
        rstd_done = s.sem("rstd_done")
        normed = s.sem("normed")

        CONSTS = 16 * 7

        def exists(seq):
            return not isinstance(seq, int) or 0 <= seq < NSEQ

        def late(seq):
            return not isinstance(seq, int) or seq > 0

        def slot_turns(seq, v):
            return [(i, t) for i, t in enumerate(TURNS) if t[2] == v and turn_exists(t[0], seq)]

        def unit_before(seq, v, back):
            return (seq, 0, v - back) if v >= back else (seq - 1, 1, v + SLOTS - back)

        def heads_of(v):
            return (0, range(HG * v, HG * v + HG), P) if v < 4 else (1, range(2 * v - 8, 2 * v - 6), SEQ)

        X0, CQ0, K0, Q00, X1, CQ1 = 0, 1, 2, 3, 7, 8

        block = ctx.enter_context(nc.Block())

        def over_sequences(eng, slot):
            def body(blk, first, last):
                for par in range(BS):
                    for v in range(SLOTS):
                        slot(BS * blk + par, par, v)
            over_blocks(eng, body)

        @block.sync
        def _(sp):
            sp.dma_start(ident[:, :], ident_dram).then_inc(consts_in, 16)
            sp.dma_start(wl_raw[:, :, :], w_lat.rearrange("(k p) c -> p k c", p=P)).then_inc(consts_in, 16)
            sp.dma_start(mask[:, :], mask_dram).then_inc(consts_in, 16)
            sp.dma_start(lnq[0:QP, :], ln_q).then_inc(consts_in, 16)
            sp.dma_start(lnkv[:, :], ln_kv.partition_broadcast(P)).then_inc(consts_in, 16)
            sp.dma_start(rq[:, :, :, :], rope_q).then_inc(consts_in, 16)
            sp.dma_start(rk[:, :, :, :], rope_k).then_inc(consts_in, 16)
            sp.dma_start(q_rows[0:QP, 1, :, :].rearrange("p h c -> p (h c)"), w_pe).then_inc(pe_in, 16)
            def seq_rows(dram, seq):
                return dram[bass.ds(seq * SEQ, SEQ), :].rearrange("(t p) d -> p t d", p=P)

            sp.dma_start(x_rows[:, :, :], seq_rows(x2, 0)).then_inc(rows_in, 16)
            for g in range(HEADS // HG):
                if g >= 2:
                    sp.wait_ge(multiplied, g - 1)
                sp.dma_start(w_raw[:, g % 2, :, :].rearrange("p h c -> p (h c)"), w_heads[g])\
                    .then_inc(raw_in[g % 2], 16)

            sp.wait_ge(turn_filled, X0 + 1)
            sp.dma_start(x_rows[:, :, :], seq_rows(x2, 1)).then_inc(rows_in, 16)

            def store(seq):
                sp.wait_ge(normed, seq + 1)
                sp.dma_start(seq_rows(x3, seq), x_out[:, :, :]).then_inc(stored, 16)

            def slot(seq, par, v):
                if v == 0 and exists(seq + 2):
                    if late(seq):
                        sp.wait_ge(turn_filled, turns_before(seq - 1, turn_of("x", 0)) + 1)
                    else:
                        sp.wait_ge(turn_filled, X1 + 1)
                    sp.dma_start(x_rows[:, :, :], seq_rows(x2, seq + 2)).then_inc(rows_in, 16)
                if v == 9:
                    if late(seq):
                        sp.wait_ge(res_added, 2 * seq)
                    sp.dma_start(x_res[:, :, :], seq_rows(x2, seq)).then_inc(res_in, 16)
                if v == 11 and late(seq):
                    store(seq - 1)

            over_sequences(sp, slot)
            store(NSEQ - 1)
            sp.wait_ge(stored, 16 * NSEQ)

        @block.gpsimd
        def _(pool):
            nc.gpsimd.memset(minus_half[:, :], -0.5).then_inc(half_set, 1)
            pool.wait_ge(half_set, 1)

            def latent_rstd(n):
                wait_first(pool, squared, n + 1, passed)
                nc.gpsimd.tensor_scalar(mean_sq[:, :], mean_sq[:, :], RMS_EPS, None, ALU.add)\
                    .then_inc(ms_added, 1)
                pool.wait_ge(ms_added, n + 1)
                nc.gpsimd.tensor_tensor(lat_rstd[:, :], mean_sq[:, :], minus_half[:, :], ALU.pow)\
                    .then_inc(lat_rstd_done, 1)

            def rope_sum(n, tile, c):
                pool.wait_ge(q_turned, n + 1)
                nc.gpsimd.tensor_tensor(
                    q_rows[:, tile, 8 * c:8 * c + 8, KVL:KVL + DR],
                    q_cos[:, c, :].rearrange("p (h d) -> p h d", d=DR),
                    q_sin[:, c, :].rearrange("p (h d) -> p h d", d=DR), ALU.add).then_inc(q_pe_done, 1)

            def norm_rstd(seq):
                pool.wait_ge(var_done, seq + 1)
                nc.gpsimd.tensor_tensor(rstd[:, :], var_eps[:, :], minus_half[:, :], ALU.pow)\
                    .then_inc(rstd_done, 1)

            latent_rstd(0)
            latent_rstd(1)
            pool.wait_ge(wpe_low, 2)
            for tile in range(2):
                for c in range(2):
                    rope_sum(2 * tile + c, tile, c)
            latent_rstd(2)
            latent_rstd(3)

            def slot(seq, par, v):
                if v in (2, 3, 6, 7) and exists(seq + 1):
                    tile, c = v // 4, v % 4 - 2
                    if tile == 0:
                        if late(seq):
                            pool.wait_ge(turn_filled, turns_before(seq - 1, turn_of("q0", 3)) + 1)
                        else:
                            pool.wait_ge(turn_filled, Q00 + 4)
                    else:
                        pool.wait_ge(turn_filled, turns_before(seq, turn_of("q1", 3)) + 1)
                    rope_sum(4 * (seq + 1) + 2 * tile + c, tile, c)
                if v in (8, 9) and exists(seq + 2):
                    latent_rstd(2 * (seq + 2) + v - 8)
                if v == 9 and late(seq):
                    norm_rstd(seq - 1)

            over_sequences(pool, slot)
            norm_rstd(NSEQ - 1)

        @block.scalar
        def _(act):
            act.wait_ge(consts_in, CONSTS)
            nc.scalar.activation(wl_part[0][:, :, :], wl_raw[:, :, :], ACT.Copy).then_inc(wl_high, 1)
            act.wait_ge(pe_in, 16)
            for k in range(2):
                nc.scalar.activation(wq_part[0][0:QP, k, HEADS * KVL:],
                                     q_rows[0:QP, 1, 8 * k:8 * k + 8, :].rearrange("p h c -> p (h c)"),
                                     ACT.Copy).then_inc(wpe_high, 1)

            def multiplied_high(g):
                act.wait_ge(multiplied, g + 1)
                nc.scalar.activation(wq_part[0][0:QP, :, g * HG * KVL:(g + 1) * HG * KVL],
                                     score_ps[g % 2][0:QP, :].rearrange("p (k c) -> p k c", k=2), ACT.Copy)
                nc.scalar.activation(wvo_part[0][:, 2 * g:2 * g + 2, :],
                                     pt_ps[g % 2][:, :].rearrange("p (a d) -> p a d", a=2), ACT.Copy)\
                    .then_inc(mult_high, 1)

            def split_turn(kind, index, filled, seq, par):
                act.wait_ge(turn_filled, filled)
                if kind == "x":
                    out, src, scale = xt_part[0][:, :, :], turn_ps[:, :].rearrange("p (k t) -> p k t", k=KD), 1.0
                elif kind == "k":
                    out, src, scale = k_part[0][:, 1 - par, :], turn_ps[:, 0:SEQ], -1.0
                elif kind in ("q0", "q1"):
                    tile = int(kind[1])
                    out, src, scale = q_part[0][:, tile, index * 512:(index + 1) * 512], turn_ps[:, :], 1.0
                elif kind in ("o0", "o_before"):
                    tile = 0 if kind == "o0" else 1
                    out, src, scale = (o_part[0][:, tile, 4 * index:4 * index + 4, :],
                                       turn_ps[:, :].rearrange("p (a t) -> p a t", a=4), 1.0)
                if kind == "cq":
                    for k in range(2):
                        last = nc.scalar.activation(cq_part[0][0:QP, k, :], turn_ps[0:QP, k * SEQ:(k + 1) * SEQ],
                                                    ACT.Copy, scale=lnq[0:QP, k:k + 1])
                    last.then_inc(turn_high, 1)
                else:
                    nc.scalar.activation(out, src, ACT.Copy, scale=scale).then_inc(turn_high, 1)

            def squares_of(n):
                act.wait_ge(lat_ready, n + 1)
                if not (isinstance(n, int) and n == 0):
                    act.wait_ge(lat_rstd_done, n)
                    act.wait_ge(squared, n)
                nc.scalar.activation(squares[:, 0:QLR], proj_ps[:, 0:QLR], ACT.Square, scale=float(QLR) ** -0.5,
                                     accum_out=mean_sq[:, 0:1])
                nc.scalar.activation(squares[:, QLR:], proj_ps[:, QLR:QLR + KVL], ACT.Square,
                                     scale=float(KVL) ** -0.5, accum_out=mean_sq[:, 1:2]).then_inc(squared, 1)

            def q_abs(n, tile, c):
                act.wait_ge(q_ready, n + 1)
                nc.scalar.activation(q_rows[:, tile, 8 * c:8 * c + 8, 0:KVL],
                                     proj_ps[:, :].rearrange("p (h c) -> p h c", c=KVL), ACT.Copy,
                                     scale=float(DN + DR) ** -0.5).then_inc(q_abs_done, 1)

            def values_high(seq, par):
                act.wait_ge(lat_done, 2 * seq + 2)
                nc.scalar.activation(v_part[0][:, par, :, :], k_rows[:, :, 0:KVL], ACT.Copy).then_inc(v_high, 1)

            def exps(seq, v):
                m = SLOTS * seq + v
                tile, heads, keys = heads_of(v)
                act.wait_ge(masked_done, m + 1)
                if v in (0, 4) and late(seq):
                    act.wait_ge(o_normed, 4 * seq - 2 + v // 2)
                wait_reuse(act, p_turned, m, 3)
                for i, h in enumerate(heads):
                    last = nc.scalar.activation(probs[:, v % 3, i * keys:(i + 1) * keys],
                                                masked[:, v % 2, i * keys:(i + 1) * keys], ACT.Exp,
                                                bias=least[:, v % 2, i:i + 1], scale=-1.0,
                                                accum_out=row_sum[:, tile, h:h + 1])
                last.then_inc(exp_done, 1)

            def probs_high(m, v):
                act.wait_ge(p_turned, m + 1)
                wait_reuse(act, summed, m, 2)
                nc.scalar.activation(p_part[0][:, v % 2, :], pt_ps[v % 2][:, :], ACT.Copy).then_inc(p_high, 1)

            split_turn("x", 0, X0 + 1, 0, 0)
            for g in range(HEADS // HG):
                multiplied_high(g)
            squares_of(0)
            squares_of(1)
            split_turn("cq", 0, CQ0 + 1, 0, 0)
            split_turn("k", 0, K0 + 1, 0, 1)
            values_high(0, 0)
            for tile in range(2):
                for c in range(2):
                    if tile == 1 and c == 0:
                        act.wait_ge(wpe_low, 2)
                    q_abs(4 * tile + c, tile, c)
            for g in range(4):
                split_turn("q0", g, Q00 + g + 1, 0, 0)
            split_turn("x", 0, X1 + 1, 0, 0)
            squares_of(2)
            squares_of(3)
            split_turn("cq", 0, CQ1 + 1, 0, 0)

            def slot(seq, par, v):
                of, _, v2 = unit_before(seq, v, 2)
                if exists(of):
                    probs_high(SLOTS * of + v2, v2)
                if v in (8, 9) and exists(seq + 2):
                    squares_of(2 * (seq + 2) + v - 8)
                turns = [(i, kind, index) for i, (kind, index, _) in slot_turns(seq, v) if kind[0] != "y"]
                for i, kind, index in turns[:1]:
                    split_turn(kind, index, turns_before(seq, i) + 1, seq, par)
                exps(seq, v)
                if v in (0, 1, 4, 5) and exists(seq + 1):
                    tile, c = v // 4, v % 4
                    if tile == 1:
                        act.wait_ge(turn_filled, turns_before(seq, turn_of("q1", 3)) + 1)
                    elif late(seq):
                        act.wait_ge(turn_filled, turns_before(seq - 1, turn_of("q0", 3)) + 1)
                    else:
                        act.wait_ge(turn_filled, Q00 + 4)
                    q_abs(8 * (seq + 1) + 4 * tile + c, tile, c)
                if v == 3 and exists(seq + 1):
                    values_high(seq + 1, 1 - par)
                for i, kind, index in turns[1:]:
                    split_turn(kind, index, turns_before(seq, i) + 1, seq, par)

            over_sequences(act, slot)
            for v in (SLOTS - 2, SLOTS - 1):
                probs_high(SLOTS * (NSEQ - 1) + v, v)
            for i, (kind, index, v) in enumerate(TURNS):
                if kind == "o_before":
                    split_turn(kind, index, turns_before(NSEQ, i) + 1, NSEQ, 0)

        @block.vector
        def _(dve):
            dve.wait_ge(consts_in, CONSTS)
            dve.wait_ge(wl_high, 1)
            nc.vector.tensor_tensor(wl_part[1][:, :, :], wl_raw[:, :, :], wl_part[0][:, :, :].bitcast(F32),
                                    ALU.subtract).then_inc(wl_low, 1)
            for k in range(2):
                dve.wait_ge(wpe_high, k + 1)
                nc.vector.tensor_tensor(wq_part[1][0:QP, k, HEADS * KVL:],
                                        q_rows[0:QP, 1, 8 * k:8 * k + 8, :].rearrange("p h c -> p (h c)"),
                                        wq_part[0][0:QP, k, HEADS * KVL:].bitcast(F32), ALU.subtract)\
                    .then_inc(wpe_low, 1)

            def multiplied_low(g):
                dve.wait_ge(mult_high, g + 1)
                cols = slice(g * HG * KVL, (g + 1) * HG * KVL)
                nc.vector.tensor_tensor(wq_part[1][0:QP, :, cols],
                                        score_ps[g % 2][0:QP, :].rearrange("p (k c) -> p k c", k=2),
                                        wq_part[0][0:QP, :, cols].bitcast(F32), ALU.subtract)
                nc.vector.tensor_tensor(wvo_part[1][:, 2 * g:2 * g + 2, :],
                                        pt_ps[g % 2][:, :].rearrange("p (a d) -> p a d", a=2),
                                        wvo_part[0][:, 2 * g:2 * g + 2, :].bitcast(F32), ALU.subtract)\
                    .then_inc(mult_low, 1)

            def split_turn(kind, index, high, seq, par):
                dve.wait_ge(turn_high, high)
                if kind == "cq":
                    for k in range(2):
                        last = nc.vector.scalar_tensor_tensor(
                            cq_part[1][0:QP, k, :], turn_ps[0:QP, k * SEQ:(k + 1) * SEQ], lnq[0:QP, k:k + 1],
                            cq_part[0][0:QP, k, :].bitcast(F32), ALU.mult, ALU.subtract)
                    last.then_inc(turn_read, 1)
                elif kind == "k":
                    nc.vector.scalar_tensor_tensor(k_part[1][:, 1 - par, :], turn_ps[:, 0:SEQ], -1.0,
                                                   k_part[0][:, 1 - par, :].bitcast(F32),
                                                   ALU.mult, ALU.subtract).then_inc(turn_read, 1)
                else:
                    if kind == "x":
                        part, where = xt_part, (slice(None), slice(None), slice(None))
                        src = turn_ps[:, :].rearrange("p (k t) -> p k t", k=KD)
                    elif kind in ("q0", "q1"):
                        part, where = q_part, (slice(None), int(kind[1]), slice(index * 512, (index + 1) * 512))
                        src = turn_ps[:, :]
                    else:
                        tile = 0 if kind == "o0" else 1
                        part, where = o_part, (slice(None), tile, slice(4 * index, 4 * index + 4), slice(None))
                        src = turn_ps[:, :].rearrange("p (a t) -> p a t", a=4)
                    nc.vector.tensor_tensor(part[1][where], src, part[0][where].bitcast(F32), ALU.subtract)\
                        .then_inc(turn_read, 1)

            def latent(n, t):
                dve.wait_ge(lat_rstd_done, n + 1)
                wait_reuse(dve, lat_done, n, 2)
                nc.vector.tensor_scalar(cq_rows[:, t, :], proj_ps[:, 0:QLR], lat_rstd[:, 0:1], None, ALU.mult)
                nc.vector.scalar_tensor_tensor(k_rows[:, t, 0:KVL], proj_ps[:, QLR:QLR + KVL], lat_rstd[:, 1:2],
                                               lnkv[:, :], ALU.mult, ALU.mult)
                at = QLR + KVL
                nc.vector.tensor_tensor(k_turn[:, t, 0, :], proj_ps[:, at:at + DR], rk[:, 0, t, :], ALU.mult)
                for a in range(2):
                    b = at + (1 - a) * (DR // 2)
                    last = nc.vector.tensor_tensor(k_turn[:, t, 1, a * (DR // 2):(a + 1) * (DR // 2)],
                                                   proj_ps[:, b:b + DR // 2],
                                                   rk[:, 1, t, a * (DR // 2):(a + 1) * (DR // 2)], ALU.mult)
                last.then_inc(lat_scaled, 1)
                dve.wait_ge(lat_scaled, n + 1)
                nc.vector.tensor_tensor(k_rows[:, t, KVL:], k_turn[:, t, 0, :], k_turn[:, t, 1, :], ALU.add)\
                    .then_inc(lat_done, 1)

            def values_low(seq, par):
                dve.wait_ge(v_high, seq + 1)
                nc.vector.tensor_tensor(v_part[1][:, par, :, :], k_rows[:, :, 0:KVL],
                                        v_part[0][:, par, :, :].bitcast(F32), ALU.subtract).then_inc(v_low, 1)

            def q_turn(n, ready, tile, c):
                dve.wait_ge(q_ready, ready)
                wait_reuse(dve, q_pe_done, n, 2)
                q = proj_ps[:, :].rearrange("p (h a d) -> p h a d", a=2, d=DR // 2)
                nc.vector.tensor_tensor(q_cos[:, c, :].rearrange("p (h d) -> p h d", d=DR),
                                        proj_ps[:, :].rearrange("p (h d) -> p h d", d=DR),
                                        rq[:, 0, tile:tile + 1, :].to_broadcast([P, 8, DR]), ALU.mult)
                for a in range(2):
                    half = slice(a * (DR // 2), (a + 1) * (DR // 2))
                    last = nc.vector.tensor_tensor(
                        q_sin[:, c, :].rearrange("p (h d) -> p h d", d=DR)[:, :, half], q[:, :, 1 - a, :],
                        rq[:, 1, tile:tile + 1, half].to_broadcast([P, 8, DR // 2]), ALU.mult)
                last.then_inc(q_turned, 1)

            def mask_scores(seq, v):
                m = SLOTS * seq + v
                tile, heads, keys = heads_of(v)
                wait_reuse(dve, exp_done, m, 2)
                wait_first(dve, scored, m + 1, passed)
                for i, h in enumerate(heads):
                    last = nc.vector.tensor_tensor_reduce(
                        out=masked[:, v % 2, i * keys:(i + 1) * keys],
                        in0=score_ps[v % 2][:, i * keys:(i + 1) * keys],
                        in1=mask[:, SEQ - keys:SEQ], scale=1.0, scalar=3.0e38,
                        op0=ALU.add, op1=ALU.min, accum_out=least[:, v % 2, i:i + 1])
                last.then_inc(masked_done, 1)

            def probs_low(m, v):
                dve.wait_ge(p_high, m + 1)
                nc.vector.tensor_tensor(p_part[1][:, v % 2, :], pt_ps[v % 2][:, :],
                                        p_part[0][:, v % 2, :].bitcast(F32), ALU.subtract).then_inc(p_low, 1)

            def normalize(seq, tile, half):
                n = 4 * seq + 2 * tile + half
                unit = SLOTS * seq + (2 * half + 1 if tile == 0 else 4 * half + 7)
                dve.wait_ge(summed, unit + 1)
                if not (isinstance(n, int) and n == 0):
                    dve.wait_ge(o_normed, n)
                nc.vector.reciprocal(row_inv[:, :], row_sum[:, tile, 8 * half:8 * half + 8]).then_inc(inv_done, 1)
                dve.wait_ge(inv_done, n + 1)
                if late(seq):
                    if tile == 0:
                        dve.wait_ge(turn_filled, turns_before(seq - 1, turn_of("o0", half)) + 1)
                    else:
                        dve.wait_ge(turn_filled, turns_before(seq, turn_of("o_before", half)) + 1)
                nc.vector.tensor_tensor(
                    o_rows[:, tile, half * 512:(half + 1) * 512].rearrange("p (h c) -> p h c", c=KVL),
                    o_ps[half][:, :].rearrange("p (h c) -> p h c", c=KVL),
                    row_inv[:, :].rearrange("p (h a) -> p h a", a=1).to_broadcast([P, 8, KVL]), ALU.mult)\
                    .then_inc(o_normed, 1)

            def add_residual(seq, tile, filled):
                dve.wait_ge(turn_filled, filled)
                dve.wait_ge(res_in, 16 * (seq + 1))
                if tile == 0 and late(seq):
                    dve.wait_ge(normed, seq)
                nc.vector.tensor_tensor(y_rows[:, tile, :], turn_ps[:, 0:D], x_res[:, tile, :], ALU.add)\
                    .then_inc(res_added, 1)
                dve.wait_ge(res_added, 2 * seq + tile + 1)
                nc.vector.bn_stats(stats[:, tile, :], y_rows[:, tile, :]).then_inc(turn_read, 1)

            def layer_norm(seq, read):
                wait_first(dve, turn_read, read, passed)
                for t in range(2):
                    last = nc.vector.bn_aggr(moments[:, t, :], stats[:, t, :])
                last.then_inc(stats_done, 1)
                dve.wait_ge(stats_done, seq + 1)
                nc.vector.tensor_scalar(var_eps[:, :], moments[:, :, 1], LN_EPS, None, ALU.add)\
                    .then_inc(var_done, 1)

            def apply_norm(seq):
                dve.wait_ge(rstd_done, seq + 1)
                if late(seq):
                    dve.wait_ge(stored, 16 * seq)
                for t in range(2):
                    last = nc.vector.tensor_scalar(x_out[:, t, :], y_rows[:, t, :], moments[:, t, 0:1],
                                                   rstd[:, t:t + 1], ALU.subtract, ALU.mult)
                last.then_inc(normed, 1)

            split_turn("x", 0, X0 + 1, 0, 0)
            for g in range(HEADS // HG):
                multiplied_low(g)
            latent(0, 0)
            latent(1, 1)
            split_turn("cq", 0, CQ0 + 1, 0, 0)
            split_turn("k", 0, K0 + 1, 0, 1)
            values_low(0, 0)
            for tile in range(2):
                for c in range(2):
                    q_turn(2 * tile + c, 4 * tile + c + 3, tile, c)
            for g in range(4):
                split_turn("q0", g, Q00 + g + 1, 0, 0)
            split_turn("x", 0, X1 + 1, 0, 0)
            latent(2, 0)
            latent(3, 1)
            split_turn("cq", 0, CQ1 + 1, 0, 0)

            def slot(seq, par, v):
                mask_scores(seq, v)
                of, _, v2 = unit_before(seq, v, 2)
                if exists(of):
                    probs_low(SLOTS * of + v2, v2)
                if v == 8 and exists(seq + 2):
                    latent(2 * (seq + 2), 0)
                turns = slot_turns(seq, v)
                for i, (kind, index, _) in turns[:1]:
                    turn(seq, par, i, kind, index)
                if v == 9 and exists(seq + 2):
                    latent(2 * (seq + 2) + 1, 1)
                if v in (2, 3, 6, 7) and exists(seq + 1):
                    tile, c = v // 4, v % 4 - 2
                    n = 2 * tile + c
                    q_turn(4 * (seq + 1) + n, 8 * (seq + 1) + 4 * tile + c + 3, tile, c)
                if v == 3 and late(seq):
                    normalize(seq - 1, 1, 1)
                if v == 5:
                    normalize(seq, 0, 0)
                if v == 3 and exists(seq + 1):
                    values_low(seq + 1, 1 - par)
                if v == 7:
                    normalize(seq, 0, 1)
                if v == 11:
                    normalize(seq, 1, 0)
                if v == 8 and late(seq):
                    layer_norm(seq - 1, turns_before(seq, turn_of("y_before", 0)) + 1)
                if v == 10 and late(seq):
                    apply_norm(seq - 1)
                for i, (kind, index, _) in turns[1:]:
                    turn(seq, par, i, kind, index)

            def turn(seq, par, i, kind, index):
                if kind[0] == "y":
                    of, tile = (seq, 0) if kind == "y0" else (seq - 1, 1)
                    add_residual(of, tile, turns_before(seq, i) + 1)
                else:
                    split_turn(kind, index, turns_before(seq, i, split_only=True) + 1, seq, par)

            over_sequences(dve, slot)
            for v in (SLOTS - 2, SLOTS - 1):
                probs_low(SLOTS * (NSEQ - 1) + v, v)
            normalize(NSEQ - 1, 1, 1)
            for i, (kind, index, v) in enumerate(TURNS):
                if kind == "o_before":
                    split_turn(kind, index, turns_before(NSEQ, i, split_only=True) + 1, NSEQ, 0)
            last_turn = turns_before(NSEQ, turn_of("y_before", 0)) + 1
            add_residual(NSEQ - 1, 1, last_turn)
            layer_norm(NSEQ - 1, last_turn)
            apply_norm(NSEQ - 1)

        @block.tensor
        def _(pe):
            pe.wait_ge(consts_in, CONSTS)

            def take_turn(turn):
                if not (isinstance(turn, int) and turn == 0):
                    pe.wait_ge(turn_read, turn)

            def transpose_x(turn, seq):
                pe.wait_ge(rows_in, 16 * (seq + 1))
                take_turn(turn)
                for k in range(KD):
                    for t in range(2):
                        last = nc.tensor.transpose(turn_ps[:, k * SEQ + t * P:k * SEQ + (t + 1) * P],
                                                   x_rows[:, t, k * P:(k + 1) * P], ident[:, :])
                last.then_inc(turn_filled, 1)

            def latents(n, t):
                for i, (xp, wp) in enumerate(PARTS):
                    for k in range(KD):
                        last = nc.tensor.matmul(proj_ps[:, 0:LATC], xt_part[xp][:, k, t * P:(t + 1) * P],
                                                wl_part[wp][:, k, :], start=(i == 0 and k == 0),
                                                stop=(i == 2 and k == KD - 1))
                last.then_inc(lat_ready, 1)

            def transpose_cq(turn, seq):
                pe.wait_ge(lat_done, 2 * seq + 2)
                take_turn(turn)
                for k in range(2):
                    for t in range(2):
                        last = nc.tensor.transpose(turn_ps[0:QP, k * SEQ + t * P:k * SEQ + (t + 1) * P],
                                                   cq_rows[:, t, k * QP:(k + 1) * QP], ident[:, :])
                last.then_inc(turn_filled, 1)

            def transpose_k(turn, seq):
                pe.wait_ge(lat_done, 2 * seq + 2)
                take_turn(turn)
                for t in range(2):
                    last = nc.tensor.transpose(turn_ps[:, t * P:(t + 1) * P], k_rows[:, t, :], ident[:, :])
                last.then_inc(turn_filled, 1)

            def queries(tile, c):
                for i, (cp, wp) in enumerate(PARTS):
                    for k in range(2):
                        last = nc.tensor.matmul(proj_ps[:, :], cq_part[cp][0:QP, k, tile * P:(tile + 1) * P],
                                                wq_part[wp][0:QP, k, c * 512:(c + 1) * 512],
                                                start=(i == 0 and k == 0), stop=(i == 2 and k == 1))
                last.then_inc(q_ready, 1)

            def transpose_q(turn, seq, tile, g):
                pe.wait_ge(q_abs_done, 4 * seq + 2 * tile + g // 2 + 1)
                pe.wait_ge(q_pe_done, 4 * seq + 2 * tile + g // 2 + 1)
                take_turn(turn)
                for i in range(HG):
                    last = nc.tensor.transpose(turn_ps[:, i * P:(i + 1) * P], q_rows[:, tile, HG * g + i, :],
                                               ident[:, :])
                last.then_inc(turn_filled, 1)

            def transpose_o(turn, seq, tile, half):
                pe.wait_ge(o_normed, 4 * seq + 2 * tile + half + 1)
                take_turn(turn)
                for i in range(4):
                    col = half * 512 + i * P
                    last = nc.tensor.transpose(turn_ps[:, i * P:(i + 1) * P], o_rows[:, tile, col:col + P],
                                               ident[:, :])
                last.then_inc(turn_filled, 1)

            def project_out(turn, tile):
                take_turn(turn)
                for a in range(HEADS // 2):
                    for i, (op, wp) in enumerate(PARTS):
                        last = nc.tensor.matmul(turn_ps[:, 0:D], o_part[op][:, tile, a, :], wvo_part[wp][:, a, :],
                                                start=(a == 0 and i == 0), stop=(a == 7 and i == 2))
                last.then_inc(turn_filled, 1)

            def scores(seq, par, v):
                m = SLOTS * seq + v
                tile, heads, keys = heads_of(v)
                if v == 0:
                    if late(seq):
                        pe.wait_ge(turn_read, turns_before(seq - 1, turn_of("q0", 3)) + 1)
                    else:
                        pe.wait_ge(turn_read, CQ1 + 1)
                elif v >= 4 and v % 2 == 0:
                    pe.wait_ge(turn_read, turns_before(seq, turn_of("q1", v // 2 - 2)) + 1)
                wait_reuse(pe, masked_done, m, 2)
                for i, h in enumerate(heads):
                    for j, (qp, kp) in enumerate(PARTS):
                        last = nc.tensor.matmul(score_ps[v % 2][:, i * keys:(i + 1) * keys],
                                                q_part[qp][:, tile, h * P:(h + 1) * P],
                                                k_part[kp][:, par, 0:keys], start=(j == 0), stop=(j == 2))
                last.then_inc(scored, 1)

            def transpose_probs(m, v):
                pe.wait_ge(exp_done, m + 1)
                wait_reuse(pe, p_low, m, 2)
                for i in range(4):
                    last = nc.tensor.transpose(pt_ps[v % 2][:, i * P:(i + 1) * P],
                                               probs[:, v % 3, i * P:(i + 1) * P], ident[:, :])
                last.then_inc(p_turned, 1)

            def weighted_sums(seq, par, v):
                m = SLOTS * seq + v
                tile, heads, keys = heads_of(v)
                pe.wait_ge(p_low, m + 1)
                if v == 0:
                    pe.wait_ge(v_low, seq + 1)
                half = heads[0] // 8
                if heads[0] % 8 == 0 and not (isinstance(seq, int) and seq == 0 and tile == 0):
                    pe.wait_ge(o_normed, 4 * seq + 2 * tile + half - 1)
                blocks = keys // P
                for i, h in enumerate(heads):
                    for b in range(blocks):
                        for j, (pp, vp) in enumerate(PARTS):
                            at = (i * blocks + b) * P
                            last = nc.tensor.matmul(o_ps[half][:, (h % 8) * KVL:(h % 8 + 1) * KVL],
                                                    p_part[pp][:, v % 2, at:at + P], v_part[vp][:, par, b, :],
                                                    start=(b == 0 and j == 0),
                                                    stop=(b == blocks - 1 and j == 2))
                last.then_inc(summed, 1)

            transpose_x(X0, 0)
            for g in range(HEADS // HG):
                pe.wait_ge(raw_in[g % 2], 16 * (g // 2 + 1))
                if g >= 2:
                    pe.wait_ge(mult_low, g - 1)
                for i in range(HG):
                    raw = w_raw[:, g % 2, i, :]
                    for k in range(2):
                        nc.tensor.matmul(score_ps[g % 2][0:QP, k * SEQ + i * KVL:k * SEQ + (i + 1) * KVL],
                                         raw[:, k * QP:(k + 1) * QP], raw[:, QLR:QLR + KVL],
                                         start=True, stop=True)
                    at = (i % 2) * KVL
                    last = nc.tensor.matmul(pt_ps[g % 2][at:at + KVL, (i // 2) * D:(i // 2 + 1) * D],
                                            raw[:, QLR + KVL:QLR + 2 * KVL], raw[:, QLR + 2 * KVL:],
                                            start=True, stop=True)
                last.then_inc(multiplied, 1)
            pe.wait_ge(turn_read, X0 + 1)
            pe.wait_ge(wl_low, 1)
            latents(0, 0)
            pe.wait_ge(lat_scaled, 1)
            latents(1, 1)
            transpose_cq(CQ0, 0)
            transpose_k(K0, 0)
            pe.wait_ge(turn_read, CQ0 + 1)
            pe.wait_ge(wpe_low, 2)
            pe.wait_ge(mult_low, HEADS // HG)
            for tile in range(2):
                for c in range(4):
                    if c == 0 and tile == 0:
                        pe.wait_ge(lat_scaled, 2)
                    elif c in (1, 2):
                        pe.wait_ge(q_abs_done, 2 * tile + c)
                    else:
                        pe.wait_ge(q_turned, 2 * tile + (1 if c == 3 else 0))
                    queries(tile, c)
            for g in range(4):
                transpose_q(Q00 + g, 0, 0, g)
            transpose_x(X1, 1)
            pe.wait_ge(turn_read, X1 + 1)
            pe.wait_ge(q_turned, 4)
            latents(2, 0)
            pe.wait_ge(lat_scaled, 3)
            latents(3, 1)
            transpose_cq(CQ1, 1)

            def slot(seq, par, v):
                of, _, v2 = unit_before(seq, v, 2)
                if exists(of):
                    transpose_probs(SLOTS * of + v2, v2)
                scores(seq, par, v)
                if v in (8, 9) and exists(seq + 2):
                    if v == 8:
                        pe.wait_ge(turn_read, turns_before(seq, turn_of("x", 0)) + 1)
                        pe.wait_ge(q_turned, 4 * (seq + 2))
                    else:
                        pe.wait_ge(lat_scaled, 2 * (seq + 2) + 1)
                    latents(2 * (seq + 2) + v - 8, v - 8)
                turns = slot_turns(seq, v)
                if v == 11:
                    sums(seq, par, v)
                for i, (kind, index, _) in turns[:1]:
                    turn(seq, par, i, kind, index)
                if v < 8 and exists(seq + 1):
                    tile, c = v // 4, v % 4
                    n = 4 * (seq + 1) + 2 * tile
                    if v == 0:
                        if late(seq):
                            pe.wait_ge(turn_read, turns_before(seq - 1, turn_of("cq", 0)) + 1)
                        else:
                            pe.wait_ge(turn_read, CQ1 + 1)
                        pe.wait_ge(lat_scaled, 2 * (seq + 2))
                    elif c in (1, 2):
                        pe.wait_ge(q_abs_done, n + c)
                    else:
                        pe.wait_ge(q_turned, n + (1 if c == 3 else 0))
                    queries(tile, c)
                if v != 11:
                    sums(seq, par, v)
                for i, (kind, index, _) in turns[1:]:
                    turn(seq, par, i, kind, index)

            def sums(seq, par, v):
                of, back, v3 = unit_before(seq, v, 3)
                if exists(of):
                    weighted_sums(of, (par - back) % 2, v3)

            def turn(seq, par, i, kind, index):
                at = turns_before(seq, i)
                if kind == "q1":
                    transpose_q(at, seq, 1, index)
                elif kind == "q0":
                    transpose_q(at, seq + 1, 0, index)
                elif kind == "k":
                    transpose_k(at, seq + 1)
                elif kind == "x":
                    transpose_x(at, seq + 2)
                elif kind == "cq":
                    transpose_cq(at, seq + 2)
                elif kind == "o_before":
                    transpose_o(at, seq - 1, 1, index)
                elif kind == "o0":
                    transpose_o(at, seq, 0, index)
                else:
                    project_out(at, 0 if kind == "y0" else 1)

            over_sequences(pe, slot)
            for v in (SLOTS - 2, SLOTS - 1):
                transpose_probs(SLOTS * (NSEQ - 1) + v, v)
            for v in range(SLOTS - 3, SLOTS):
                weighted_sums(NSEQ - 1, (NSEQ - 1) % 2, v)
            for i, (kind, index, v) in enumerate(TURNS):
                if kind in ("o_before", "y_before"):
                    turn(NSEQ, 0, i, kind, index)


E = 32
TOPK = 4
NG = 8
GE = E // NG
TOPG = 3
I = 128
SI = 256
SC = SI // P
CAP = -(-5 * TOKENS // (4 * E))
CH2 = CAP // 2
SLOTROWS = E * CAP
ROUTE_SCALE = 2.5
TILES = TOKENS // P
EW = 2 * KD * I + D
PAST_END = 65536.0
ROUTER_LINKS = 32


def moe_phase(nc, ident_dram, router_w, e_bias, counts_dram, earlier_dram, w_experts, w_shared, zero_rows,
              x3, slots_dram, y_dram, out):
    with ExitStack() as ctx:
        s = Scope(nc, ctx, "moe")

        def both(name, shape):
            return [s.sb(name + "_high", shape, F32R), s.sb(name + "_low", shape, F32R)]

        ident = s.sb("ident", [P, P])
        counts = s.sb("counts", [P, E])
        bias = s.sb("bias", [P, BT, E])
        earlier = s.sb("earlier", [P, P], BF16)
        ones = s.sb("ones", [P, P], BF16)
        earlier_f = s.sb("earlier_f", [P, P])
        zeros = s.sb("zeros", [P, D])
        ws_raw = s.sb("ws_raw", [P, 3, KD, SI])
        ws_part = both("ws", [P, 3, KD, SI])
        wr_raw = s.sb("wr_raw", [P, KD, E])
        wr_part = both("wr", [P, KD, E])
        x_out = s.sb("x_out", [P, 2, D])
        x_rows = s.sb("x_rows", [P, 2, BT, D])
        xt_rows = s.sb("xt_rows", [P, BT, D])
        xt_part = both("xt", [P, KD, BLK])
        score = s.sb("score", [P, BT, E])
        choice = s.sb("choice", [P, BT, E])
        pair_max = s.sb("pair_max", [P, BT * NG, 2])
        pair_min = s.sb("pair_min", [P, BT * NG, 2])
        top1 = s.sb("top1", [P, BT * NG])
        low1 = s.sb("low1", [P, BT * NG])
        high2 = s.sb("high2", [P, BT * NG])
        top2 = s.sb("top2", [P, BT * NG])
        group_sum = s.sb("group_sum", [P, BT, NG])
        best = s.sb("best", [P, BT, 8])
        best_at = s.sb("best_at", [P, BT, 8], U32)
        group_at = s.sb("group_at", [P, BT, 8])
        expert_at = s.sb("expert_at", [P, BT, 8])
        in_group = s.sb("in_group", [P, TOPG, BT, NG])
        group_mask = s.sb("group_mask", [P, BT, NG])
        chosen = s.sb("chosen", [P, TOPK, BT, E])
        picked = s.sb("picked", [P, TOPK, BT, E])
        pair_sum = s.sb("pair_sum", [P, 2, BT, E])
        member = s.sb("member", [P, BT, E], BF16)
        pair_member = s.sb("pair_member", [P, 2, E])
        block_member = s.sb("block_member", [P, E])
        members = s.sb("members", [P, E], BF16)
        members_f = s.sb("members_f", [P, E])
        weight_k = s.sb("weight_k", [P, BT, TOPK])
        place_k = s.sb("place_k", [P, BT, TOPK])
        weight_sum = s.sb("weight_sum", [P, BT])
        weight_inv = s.sb("weight_inv", [P, BT])
        full = s.sb("full", [P, BT, TOPK])
        slot_f = s.sb("slot_f", [P, BT, TOPK])
        slot_now = s.sb("slot_now", [P, BT * TOPK], U32)
        slot_at = s.sb("slot_at", [P, TILES, TOPK], U32)
        gather_now = s.sb("gather_now", [P, 2, TOPK], U32)
        weight = s.sb("weight", [P, TILES * TOPK])
        gate = s.sb("gate", [P, 2, BLK])
        hidden = s.sb("hidden", [P, 2, BLK])
        h_part = both("h", [P, 2, BLK])
        total = s.sb("total", [P, TILES, D])
        w_raw = s.sb("w_raw", [P, 2, EW])
        w_part = both("w", [P, 2, EW])
        e_rows = s.sb("e_rows", [CH2, 2, 2, D])
        e_part = both("e", [P, 2, KD, CAP])
        e_gate = s.sb("e_gate", [P, 2, CAP])
        e_hidden = s.sb("e_hidden", [P, 2, CAP])
        eh_part = both("eh", [P, 2, CAP])
        y_rows = s.sb("y_rows", [CH2, 2, 2, D])
        y_in = s.sb("y_in", [P, 2, TOPK, D])
        stats = s.sb("stats", [P, 2, 6])
        moments = s.sb("moments", [P, 2, 2])
        minus_half = s.sb("minus_half", [P, 2])
        var_eps = s.sb("var_eps", [P, 2])
        rstd = s.sb("rstd", [P, 2])
        xt_ps = [s.ps("xt0"), s.ps("xt1")]
        hid_ps = [[s.ps("gate0"), s.ps("up0")], [s.ps("gate1"), s.ps("up1")]]
        route_ps = s.ps("route")

        consts_in = s.sem("consts_in")
        passed = s.sem("passed")
        zero_set = s.sem("zero_set")
        slots_zeroed = s.sem("slots_zeroed")
        consts_set = s.sem("consts_set")
        ws_high = s.sem("ws_high")
        ws_low = s.sem("ws_low")
        rows_in = s.sem("rows_in")
        xt_in = s.sem("xt_in")
        transposed = s.sem("transposed")
        xt_high = s.sem("xt_high")
        xt_low = s.sem("xt_low")
        logits_done = s.sem("logits_done")
        score_done = s.sem("score_done")
        chain = s.sem("router_chain")
        member_done = s.sem("member_done")
        places_done = s.sem("places_done")
        places_read = s.sem("places_read")
        slots_done = s.sem("slots_done")
        scattered = s.sem("scattered")
        gate_ready = s.sem("gate_ready")
        up_ready = s.sem("up_ready")
        gate_done = s.sem("gate_done")
        hidden_done = s.sem("hidden_done")
        h_high = s.sem("h_high")
        h_low = s.sem("h_low")
        shared_done = s.sem("shared_done")
        total_done = s.sem("total_done")
        raw_in = [s.sem("raw_in0"), s.sem("raw_in1")]
        w_high = s.sem("w_high_done")
        w_low = s.sem("w_low_done")
        slots_in = [s.sem("slots_in0"), s.sem("slots_in1")]
        e_turned = s.sem("e_turned")
        e_high = s.sem("e_high_done")
        e_low = s.sem("e_low_done")
        e_gate_ready = s.sem("e_gate_ready")
        e_up_ready = s.sem("e_up_ready")
        e_gate_done = s.sem("e_gate_done")
        e_hidden_done = s.sem("e_hidden_done")
        eh_high = s.sem("eh_high_done")
        eh_low = s.sem("eh_low_done")
        y_ready = s.sem("y_ready")
        y_copied = s.sem("y_copied")
        y_stored = [s.sem("y_stored0"), s.sem("y_stored1")]
        y_cleared = s.sem("y_cleared")
        gather_set = s.sem("gather_set")
        gathered = [s.sem("gathered0"), s.sem("gathered1")]
        added = s.sem("added")
        stats_done = s.sem("stats_done")
        var_done = s.sem("var_done")
        rstd_done = s.sem("rstd_done")
        normed = s.sem("normed")
        stored = s.sem("stored")

        CONSTS = 16 * (4 + BT + 2)
        PAIRS = TILES // 2

        def late(n):
            return not isinstance(n, int) or n > 0

        def over(eng, count, body):
            body(0)
            with eng.Fori(1, count - 1) as i:
                body(i)
            body(count - 1)

        def slot_rows(dram, e):
            return dram[bass.ds(e * CAP, CAP), :].rearrange("(a p) d -> p a d", p=CH2)

        block = ctx.enter_context(nc.Block())

        @block.sync
        def _(sp):
            sp.dma_start(ident[:, :], ident_dram).then_inc(consts_in, 16)
            sp.dma_start(counts[:, :], counts_dram).then_inc(consts_in, 16)
            sp.dma_start(earlier_f[:, :], earlier_dram).then_inc(consts_in, 16)
            sp.dma_start(ws_raw[:, :, :, :].rearrange("p a k c -> p (a k c)"), w_shared).then_inc(consts_in, 16)
            sp.dma_start(wr_raw[:, :, :], router_w.rearrange("(k p) e -> p k e", p=P)).then_inc(consts_in, 16)
            sp.dma_start(zeros[:, :], zero_rows).then_inc(consts_in, 16)
            for j in range(BT):
                sp.dma_start(bias[:, j, :], e_bias.partition_broadcast(P)).then_inc(consts_in, 16)
            sp.wait_ge(consts_in, CONSTS)
            for a in range(SLOTROWS // P):
                sp.dma_start(slots_dram[a * P:(a + 1) * P, :], zeros[:, :]).then_inc(slots_zeroed, 16)

            def load(blk):
                if late(blk):
                    sp.wait_ge(transposed, blk)
                sp.dma_start(xt_rows[:, :, :], rows(x3, blk)).then_inc(xt_in, 16)
                if late(blk):
                    wait_first(sp, total_done, blk, passed)
                    wait_first(sp, scattered, 16 * BT * TOPK * blk, passed)
                sp.dma_start(x_rows[:, 0, :, :], rows(x3, blk)).then_inc(rows_in, 16)

            over(sp, NB, load)

            def load_w(e, par):
                if late(e) and not (isinstance(e, int) and e < 2):
                    sp.wait_ge(w_high, e - 1)
                    sp.wait_ge(w_low, e - 1)
                sp.dma_start(w_raw[:, par, :], w_experts[bass.ds(e, 1), :, :].rearrange("a p c -> (a p) c"))\
                    .then_inc(raw_in[par], 16)

            def load_slots(e, par):
                if not (isinstance(e, int) and e < 2):
                    sp.wait_ge(e_turned, e - 1)
                sp.dma_start(e_rows[:, par, :, :], slot_rows(slots_dram, e)).then_inc(slots_in[par], 16)

            def store_y(e, par):
                sp.wait_ge(y_copied, e + 1)
                sp.dma_start(slot_rows(y_dram, e), y_rows[:, par, :, :]).then_inc(y_stored[par], 16)

            load_w(0, 0)
            load_w(1, 1)
            sp.wait_ge(scattered, 16 * TOPK * TILES)
            load_slots(0, 0)
            load_slots(1, 1)

            def experts(i):
                for par in range(2):
                    e = 2 * i + par
                    if not (isinstance(i, int) and i == E // 2 - 1):
                        load_w(e + 2, par)
                        load_slots(e + 2, par)
                    store_y(e, par)

            over(sp, E // 2, experts)

            def store(i):
                sp.wait_ge(normed, i + 1)
                sp.dma_start(out[bass.ds(i * 2 * P, 2 * P), :].rearrange("(t p) d -> p t d", p=P),
                             x_out[:, :, :]).then_inc(stored, 16)

            over(sp, PAIRS, store)
            sp.wait_ge(stored, 16 * PAIRS)

        @block.gpsimd
        def _(pool):
            nc.gpsimd.memset(minus_half[:, :], -0.5).then_inc(consts_set, 1)
            pool.wait_ge(consts_set, 1)
            pool.wait_ge(slots_zeroed, 16 * (SLOTROWS // P))

            def scatter(blk):
                pool.wait_ge(slots_done, blk + 1)
                wait_first(pool, rows_in, 16 * (blk + 1), passed)
                for j in range(BT):
                    for k in range(TOPK):
                        nc.gpsimd.indirect_dma_start(
                            slots_dram, bass.IndirectOffsetOnAxis(slot_now[:, j * TOPK + k:j * TOPK + k + 1], 0),
                            x_rows[:, 0, j, :], None, bounds_check=SLOTROWS - 1, oob_is_err=False)\
                            .then_inc(scattered, 16)

            over(pool, NB, scatter)

            pool.wait_ge(y_stored[0], 16 * (E // 2))
            pool.wait_ge(y_stored[1], 16 * (E // 2))
            pool.wait_ge(y_cleared, 2)

            def gather(i):
                for t in range(2):
                    if late(i):
                        pool.wait_ge(added, 2 * i + t - 1)
                    nc.gpsimd.tensor_copy(gather_now[:, t, :], slot_at[:, bass.ds(2 * i + t, 1), :]
                                          .rearrange("p a k -> p (a k)")).then_inc(gather_set, 1)
                    wait_first(pool, gather_set, 2 * i + t + 1, passed)
                    for k in range(TOPK):
                        nc.gpsimd.indirect_dma_start(
                            y_in[:, t, k, :], None, y_dram,
                            bass.IndirectOffsetOnAxis(gather_now[:, t, k:k + 1], 0),
                            bounds_check=SLOTROWS - 1, oob_is_err=False).then_inc(gathered[t], 16)
                if late(i):
                    rsqrt(i - 1)

            def rsqrt(i):
                pool.wait_ge(var_done, i + 1)
                nc.gpsimd.tensor_tensor(rstd[:, :], var_eps[:, :], minus_half[:, :], ALU.pow)\
                    .then_inc(rstd_done, 1)

            over(pool, PAIRS, gather)
            rsqrt(PAIRS - 1)

        @block.scalar
        def _(act):
            act.wait_ge(consts_in, CONSTS)
            nc.scalar.activation(ws_part[0][:, :, :, :], ws_raw[:, :, :, :], ACT.Copy)
            nc.scalar.activation(wr_part[0][:, :, :], wr_raw[:, :, :], ACT.Copy).then_inc(ws_high, 1)

            def tokens(blk):
                act.wait_ge(transposed, blk + 1)
                if late(blk):
                    act.wait_ge(up_ready, SC * blk)
                for k in range(KD):
                    nc.scalar.activation(xt_part[0][:, k, :], xt_ps[k][:, :], ACT.Copy).then_inc(xt_high, 1)
                act.wait_ge(logits_done, blk + 1)
                if late(blk):
                    act.wait_ge(slots_done, blk)
                nc.scalar.activation(score[:, :, :], route_ps[:, 0:BT * E].rearrange("p (t e) -> p t e", e=E),
                                     ACT.Sigmoid).then_inc(score_done, 1)
                for c in range(SC):
                    act.wait_ge(gate_ready, SC * blk + c + 1)
                    if late(blk):
                        act.wait_ge(hidden_done, SC * (blk - 1) + c + 1)
                    nc.scalar.activation(gate[:, c, :], hid_ps[c][0][:, :], ACT.Silu).then_inc(gate_done, 1)
                for c in range(SC):
                    act.wait_ge(hidden_done, SC * blk + c + 1)
                    if late(blk):
                        act.wait_ge(shared_done, blk)
                    nc.scalar.activation(h_part[0][:, c, :], hidden[:, c, :], ACT.Copy).then_inc(h_high, 1)

            over(act, NB, tokens)

            def weights(e, par):
                act.wait_ge(raw_in[par], 8 * (e - par) + 16)
                if not (isinstance(e, int) and e < 2):
                    act.wait_ge(y_ready, e - 1)
                nc.scalar.activation(w_part[0][:, par, :], w_raw[:, par, :], ACT.Copy).then_inc(w_high, 1)

            def experts(i):
                for par in range(2):
                    e = 2 * i + par
                    weights(e, par)
                    act.wait_ge(e_turned, e + 1)
                    if not (isinstance(e, int) and e < 2):
                        act.wait_ge(e_up_ready, e - 1)
                    nc.scalar.activation(e_part[0][:, par, :, :],
                                         xt_ps[par][:, 0:KD * CAP].rearrange("p (k c) -> p k c", c=CAP),
                                         ACT.Copy).then_inc(e_high, 1)
                    act.wait_ge(e_gate_ready, e + 1)
                    if not (isinstance(e, int) and e < 2):
                        act.wait_ge(e_hidden_done, e - 1)
                    nc.scalar.activation(e_gate[:, par, :], hid_ps[par][0][:, 0:CAP], ACT.Silu)\
                        .then_inc(e_gate_done, 1)
                    act.wait_ge(e_hidden_done, e + 1)
                    if not (isinstance(e, int) and e < 2):
                        act.wait_ge(y_ready, e - 1)
                    nc.scalar.activation(eh_part[0][:, par, :], e_hidden[:, par, :], ACT.Copy).then_inc(eh_high, 1)

            over(act, E // 2, experts)

        @block.vector
        def _(dve):
            dve.wait_ge(consts_in, CONSTS)
            nc.vector.memset(ones[:, :], 1.0)
            nc.vector.memset(members[:, :], 0.0)
            nc.vector.memset(members_f[:, :], 0.0)
            nc.vector.memset(y_in[:, :, :, :], 0.0).then_inc(y_cleared, 2)
            nc.vector.tensor_copy(earlier[:, :], earlier_f[:, :])
            dve.wait_ge(ws_high, 1)
            nc.vector.tensor_tensor(ws_part[1][:, :, :, :], ws_raw[:, :, :, :],
                                    ws_part[0][:, :, :, :].bitcast(F32), ALU.subtract)
            nc.vector.tensor_tensor(wr_part[1][:, :, :], wr_raw[:, :, :], wr_part[0][:, :, :].bitcast(F32),
                                    ALU.subtract).then_inc(ws_low, 1)

            def router(blk):
                base = ROUTER_LINKS * blk
                links = [0]

                def link(instruction):
                    links[0] += 1
                    instruction.then_inc(chain, 1)
                    wait_first(dve, chain, base + links[0], passed)

                v = nc.vector
                dve.wait_ge(score_done, blk + 1)
                link(v.tensor_tensor(choice[:, :, :], score[:, :, :], bias[:, :, :], ALU.add))
                fours = choice[:, :, :].rearrange("p t (g a b) -> p (t g) a b", a=2, b=2)
                v.tensor_tensor(pair_max[:, :, :], fours[:, :, :, 0], fours[:, :, :, 1], ALU.max)
                link(v.tensor_tensor(pair_min[:, :, :], fours[:, :, :, 0], fours[:, :, :, 1], ALU.min))
                v.tensor_tensor(top1[:, :], pair_max[:, :, 0], pair_max[:, :, 1], ALU.max)
                v.tensor_tensor(low1[:, :], pair_max[:, :, 0], pair_max[:, :, 1], ALU.min)
                link(v.tensor_tensor(high2[:, :], pair_min[:, :, 0], pair_min[:, :, 1], ALU.max))
                link(v.tensor_tensor(top2[:, :], low1[:, :], high2[:, :], ALU.max))
                link(v.tensor_tensor(group_sum[:, :, :].rearrange("p t g -> p (t g)"), top1[:, :], top2[:, :],
                                     ALU.add))
                for j in range(BT):
                    last = v.max(best[:, j, :], group_sum[:, j, :])
                link(last)
                for j in range(BT):
                    last = v.max_index(best_at[:, j, :], best[:, j, :], group_sum[:, j, :])
                link(last)
                link(v.tensor_copy(group_at[:, :, :], best_at[:, :, :]))
                for g in range(TOPG):
                    last = v.tensor_tensor(in_group[:, g, :, :],
                                           counts[:, 0:NG].rearrange("p (a g) -> p a g", a=1)
                                           .to_broadcast([P, BT, NG]),
                                           group_at[:, :, g:g + 1].to_broadcast([P, BT, NG]), ALU.is_equal)
                link(last)
                link(v.tensor_tensor(group_mask[:, :, :], in_group[:, 0, :, :], in_group[:, 1, :, :], ALU.add))
                link(v.tensor_tensor(group_mask[:, :, :], group_mask[:, :, :], in_group[:, 2, :, :], ALU.add))
                link(v.tensor_tensor(choice[:, :, :].rearrange("p t (g e) -> p (t g) e", e=GE),
                                     choice[:, :, :].rearrange("p t (g e) -> p (t g) e", e=GE),
                                     group_mask[:, :, :].rearrange("p t (g a) -> p (t g) a", a=1)
                                     .to_broadcast([P, BT * NG, GE]), ALU.mult))
                link(v.tensor_scalar(choice[:, :, :], choice[:, :, :], 0.0, None, ALU.add))
                for j in range(BT):
                    last = v.max(best[:, j, :], choice[:, j, :])
                link(last)
                for j in range(BT):
                    last = v.max_index(best_at[:, j, :], best[:, j, :], choice[:, j, :])
                link(last)
                link(v.tensor_copy(expert_at[:, :, :], best_at[:, :, :]))
                for k in range(TOPK):
                    last = v.tensor_tensor(chosen[:, k, :, :],
                                           counts[:, :].rearrange("p (a e) -> p a e", a=1)
                                           .to_broadcast([P, BT, E]),
                                           expert_at[:, :, k:k + 1].to_broadcast([P, BT, E]), ALU.is_equal)
                link(last)
                link(v.tensor_tensor(pair_sum[:, :, :, :], chosen[:, 0:2, :, :], chosen[:, 2:4, :, :], ALU.add))
                v.tensor_tensor(member[:, :, :], pair_sum[:, 0, :, :], pair_sum[:, 1, :, :], ALU.add)\
                    .then_inc(member_done, 1)
                for k in range(TOPK):
                    last = v.tensor_tensor(picked[:, k, :, :], chosen[:, k, :, :], score[:, :, :], ALU.mult)
                link(last)
                link(v.tensor_reduce(weight_k[:, :, :].rearrange("p t k -> p k t"), picked[:, :, :, :],
                                     axis=AX.X, op=ALU.add))
                link(v.tensor_reduce(weight_sum[:, :], weight_k[:, :, :], axis=AX.X, op=ALU.add))
                link(v.tensor_scalar(weight_sum[:, :], weight_sum[:, :], 1e-20, None, ALU.add))
                link(v.reciprocal(weight_inv[:, :], weight_sum[:, :]))
                link(v.tensor_tensor(weight_k[:, :, :], weight_k[:, :, :],
                                     weight_inv[:, :].rearrange("p (t a) -> p t a", a=1)
                                     .to_broadcast([P, BT, TOPK]), ALU.mult))
                dve.wait_ge(places_done, blk + 1)
                places = route_ps[:, BT * E:2 * BT * E].rearrange("p (t e) -> p t e", e=E)
                for k in range(TOPK):
                    last = v.tensor_tensor(picked[:, k, :, :], chosen[:, k, :, :], places, ALU.mult)
                last.then_inc(places_read, 1)
                dve.wait_ge(places_read, blk + 1)
                link(v.tensor_reduce(place_k[:, :, :].rearrange("p t k -> p k t"), picked[:, :, :, :],
                                     axis=AX.X, op=ALU.add))
                link(v.tensor_scalar(full[:, :, :], place_k[:, :, :], float(CAP), None, ALU.is_ge))
                link(v.scalar_tensor_tensor(slot_f[:, :, :], expert_at[:, :, 0:TOPK], float(CAP),
                                            place_k[:, :, :], ALU.mult, ALU.add))
                link(v.scalar_tensor_tensor(slot_f[:, :, :], full[:, :, :], PAST_END, slot_f[:, :, :],
                                            ALU.mult, ALU.add))
                link(v.tensor_scalar(full[:, :, :], full[:, :, :], -ROUTE_SCALE, ROUTE_SCALE, ALU.mult, ALU.add))
                v.tensor_tensor(weight[:, bass.ds(blk * BT * TOPK, BT * TOPK)],
                                weight_k[:, :, :].rearrange("p t k -> p (t k)"),
                                full[:, :, :].rearrange("p t k -> p (t k)"), ALU.mult)
                link(v.tensor_tensor(pair_member[:, :, :], member[:, 0:2, :], member[:, 2:4, :], ALU.add))
                link(v.tensor_tensor(block_member[:, :], pair_member[:, 0, :], pair_member[:, 1, :], ALU.add))
                link(v.tensor_tensor(members_f[:, :], members_f[:, :], block_member[:, :], ALU.add))
                v.tensor_copy(members[:, :], members_f[:, :])
                if late(blk):
                    dve.wait_ge(scattered, 16 * BT * TOPK * blk)
                v.tensor_copy(slot_now[:, :], slot_f[:, :, :].rearrange("p t k -> p (t k)"))
                v.tensor_copy(slot_at[:, bass.ds(blk * BT, BT), :], slot_f[:, :, :]).then_inc(slots_done, 1)
                assert links[0] == ROUTER_LINKS, links[0]

            def tokens(blk):
                for k in range(KD):
                    dve.wait_ge(xt_high, KD * blk + k + 1)
                    nc.vector.tensor_tensor(xt_part[1][:, k, :], xt_ps[k][:, :],
                                            xt_part[0][:, k, :].bitcast(F32), ALU.subtract).then_inc(xt_low, 1)
                router(blk)
                for c in range(SC):
                    dve.wait_ge(up_ready, SC * blk + c + 1)
                    dve.wait_ge(gate_done, SC * blk + c + 1)
                    if late(blk):
                        dve.wait_ge(h_low, SC * (blk - 1) + c + 1)
                    nc.vector.tensor_tensor(hidden[:, c, :], hid_ps[c][1][:, :], gate[:, c, :], ALU.mult)\
                        .then_inc(hidden_done, 1)
                for c in range(SC):
                    dve.wait_ge(h_high, SC * blk + c + 1)
                    nc.vector.tensor_tensor(h_part[1][:, c, :], hidden[:, c, :],
                                            h_part[0][:, c, :].bitcast(F32), ALU.subtract).then_inc(h_low, 1)
                dve.wait_ge(shared_done, blk + 1)
                dve.wait_ge(rows_in, 16 * (blk + 1))
                for h in range(2):
                    last = nc.vector.tensor_tensor(
                        total[:, bass.ds(blk * BT + 2 * h, 2), :],
                        xt_ps[h][:, :].rearrange("p (t d) -> p t d", d=D),
                        x_rows[:, 0, 2 * h:2 * h + 2, :], ALU.add)
                last.then_inc(total_done, 1)

            over(dve, NB, tokens)

            def experts(i):
                for par in range(2):
                    e = 2 * i + par
                    dve.wait_ge(w_high, e + 1)
                    nc.vector.tensor_tensor(w_part[1][:, par, :], w_raw[:, par, :],
                                            w_part[0][:, par, :].bitcast(F32), ALU.subtract).then_inc(w_low, 1)
                    dve.wait_ge(e_high, e + 1)
                    nc.vector.tensor_tensor(e_part[1][:, par, :, :],
                                            xt_ps[par][:, 0:KD * CAP].rearrange("p (k c) -> p k c", c=CAP),
                                            e_part[0][:, par, :, :].bitcast(F32), ALU.subtract).then_inc(e_low, 1)
                    dve.wait_ge(e_up_ready, e + 1)
                    dve.wait_ge(e_gate_done, e + 1)
                    if not (isinstance(e, int) and e < 2):
                        dve.wait_ge(eh_low, e - 1)
                    nc.vector.tensor_tensor(e_hidden[:, par, :], hid_ps[par][1][:, 0:CAP], e_gate[:, par, :],
                                            ALU.mult).then_inc(e_hidden_done, 1)
                    dve.wait_ge(eh_high, e + 1)
                    nc.vector.tensor_tensor(eh_part[1][:, par, :], e_hidden[:, par, :],
                                            eh_part[0][:, par, :].bitcast(F32), ALU.subtract).then_inc(eh_low, 1)
                    dve.wait_ge(y_ready, e + 1)
                    if not (isinstance(e, int) and e < 2):
                        dve.wait_ge(y_stored[par], 8 * (e - par))
                    nc.vector.tensor_copy(y_rows[:, par, :, :],
                                          route_ps[0:CH2, :].rearrange("p (a d) -> p a d", a=2))\
                        .then_inc(y_copied, 1)

            over(dve, E // 2, experts)

            def combine(i):
                for k in range(TOPK):
                    for t in range(2):
                        if k == 0:
                            dve.wait_ge(gathered[t], 16 * TOPK * (i + 1))
                        else:
                            dve.wait_ge(chain, NB * ROUTER_LINKS + 8 * i + 2 * (k - 1) + t + 1)
                        row = total[:, bass.ds(2 * i + t, 1), :].rearrange("p a d -> p (a d)")
                        last = nc.vector.scalar_tensor_tensor(
                            row, y_in[:, t, k, :], weight[:, bass.ds((2 * i + t) * TOPK + k, 1)], row, ALU.mult, ALU.add)
                        last.then_inc(chain, 1)
                wait_first(dve, chain, NB * ROUTER_LINKS + 8 * i + 8, passed)
                for t in range(2):
                    row = total[:, bass.ds(2 * i + t, 1), :].rearrange("p a d -> p (a d)")
                    nc.vector.bn_stats(stats[:, t, :], row).then_inc(added, 1)
                if late(i):
                    dve.wait_ge(normed, i)
                wait_first(dve, added, 2 * i + 2, passed)
                for t in range(2):
                    last = nc.vector.bn_aggr(moments[:, t, :], stats[:, t, :])
                last.then_inc(stats_done, 1)
                dve.wait_ge(stats_done, i + 1)
                nc.vector.tensor_scalar(var_eps[:, :], moments[:, :, 1], LN_EPS, None, ALU.add)\
                    .then_inc(var_done, 1)
                dve.wait_ge(rstd_done, i + 1)
                if late(i):
                    dve.wait_ge(stored, 16 * i)
                for t in range(2):
                    row = total[:, bass.ds(2 * i + t, 1), :].rearrange("p a d -> p (a d)")
                    last = nc.vector.tensor_scalar(x_out[:, t, :], row, moments[:, t, 0:1], rstd[:, t:t + 1],
                                                   ALU.subtract, ALU.mult)
                last.then_inc(normed, 1)

            over(dve, PAIRS, combine)

        @block.tensor
        def _(pe):
            pe.wait_ge(consts_in, CONSTS)

            def turn(blk):
                pe.wait_ge(xt_in, 16 * (blk + 1))
                if late(blk):
                    pe.wait_ge(total_done, blk)
                for k in range(KD):
                    for j in range(BT):
                        last = nc.tensor.transpose(xt_ps[k][:, j * P:(j + 1) * P],
                                                   xt_rows[:, j, k * P:(k + 1) * P], ident[:, :])
                last.then_inc(transposed, 1)

            def tokens(blk):
                turn(blk)
                pe.wait_ge(xt_low, KD * (blk + 1))
                if not late(blk):
                    pe.wait_ge(ws_low, 1)
                if late(blk):
                    pe.wait_ge(score_done, blk)
                    pe.wait_ge(places_read, blk)
                for j in range(BT):
                    for i, (xp, wp) in enumerate(PARTS):
                        for k in range(KD):
                            last = nc.tensor.matmul(route_ps[:, j * E:(j + 1) * E],
                                                    xt_part[xp][:, k, j * P:(j + 1) * P], wr_part[wp][:, k, :],
                                                    start=(i == 0 and k == 0), stop=(i == 2 and k == KD - 1))
                last.then_inc(logits_done, 1)
                for c in range(SC):
                    for b, (ready, read) in enumerate(((gate_ready, gate_done), (up_ready, hidden_done))):
                        if late(blk):
                            pe.wait_ge(read, SC * (blk - 1) + c + 1)
                        for i, (wp, xp) in enumerate(PARTS):
                            for k in range(KD):
                                last = nc.tensor.matmul(hid_ps[c][b][:, :],
                                                        ws_part[wp][:, b, k, c * P:(c + 1) * P],
                                                        xt_part[xp][:, k, :],
                                                        start=(i == 0 and k == 0), stop=(i == 2 and k == KD - 1))
                        last.then_inc(ready, 1)
                pe.wait_ge(member_done, blk + 1)
                pe.wait_ge(score_done, blk + 1)
                for j in range(BT):
                    place = route_ps[:, (BT + j) * E:(BT + j + 1) * E]
                    nc.tensor.matmul(place, ones[:, :], members[:, :], start=True, stop=False)
                    for b in range(j):
                        nc.tensor.matmul(place, ones[:, :], member[:, b, :], start=False, stop=False)
                    last = nc.tensor.matmul(place, earlier[:, :], member[:, j, :], start=False, stop=True)
                last.then_inc(places_done, 1)
                pe.wait_ge(h_low, SC * (blk + 1))
                for j in range(BT):
                    for c in range(SC):
                        for i, (hp, wp) in enumerate(PARTS):
                            last = nc.tensor.matmul(xt_ps[j // 2][:, (j % 2) * D:(j % 2 + 1) * D],
                                                    h_part[hp][:, c, j * P:(j + 1) * P], ws_part[wp][:, 2, c, :],
                                                    start=(c == 0 and i == 0), stop=(c == SC - 1 and i == 2))
                last.then_inc(shared_done, 1)

            over(pe, NB, tokens)
            pe.wait_ge(total_done, NB)

            def experts(i):
                for par in range(2):
                    e = 2 * i + par
                    early = isinstance(e, int) and e < 2
                    pe.wait_ge(slots_in[par], 8 * (e - par) + 16)
                    if not early:
                        pe.wait_ge(e_low, e - 1)
                    for k in range(KD):
                        for a in range(2):
                            at = k * CAP + a * CH2
                            last = nc.tensor.transpose(xt_ps[par][:, at:at + CH2],
                                                       e_rows[:, par, a, k * P:(k + 1) * P],
                                                       ident[0:CH2, 0:CH2])
                    last.then_inc(e_turned, 1)
                    pe.wait_ge(e_low, e + 1)
                    pe.wait_ge(w_low, e + 1)
                    for b, (ready, read) in enumerate(((e_gate_ready, e_gate_done), (e_up_ready, e_hidden_done))):
                        if not early:
                            pe.wait_ge(read, e - 1)
                        for i2, (wp, xp) in enumerate(PARTS):
                            for k in range(KD):
                                col = (b * KD + k) * I
                                last = nc.tensor.matmul(hid_ps[par][b][:, 0:CAP], w_part[wp][:, par, col:col + I],
                                                        e_part[xp][:, par, k, :],
                                                        start=(i2 == 0 and k == 0), stop=(i2 == 2 and k == KD - 1))
                        last.then_inc(ready, 1)
                    pe.wait_ge(eh_low, e + 1)
                    if not (isinstance(e, int) and e == 0):
                        pe.wait_ge(y_copied, e)
                    for a in range(2):
                        for i2, (hp, wp) in enumerate(PARTS):
                            last = nc.tensor.matmul(route_ps[0:CH2, a * D:(a + 1) * D],
                                                    eh_part[hp][:, par, a * CH2:(a + 1) * CH2],
                                                    w_part[wp][:, par, 2 * KD * I:EW],
                                                    start=(i2 == 0), stop=(i2 == 2))
                    last.then_inc(y_ready, 1)

            over(pe, E // 2, experts)


def rwkv_attention_moe_program(nc, a, out):
    x1 = nc.dram_tensor("x1", (TOKENS, D), F32).ap()
    x2 = nc.dram_tensor("x2", (TOKENS, D), F32).ap()
    x3 = nc.dram_tensor("x3", (TOKENS, D), F32).ap()
    slots = nc.dram_tensor("slots", (SLOTROWS, D), F32).ap()
    slots_out = nc.dram_tensor("slots_out", (SLOTROWS, D), F32).ap()
    rwkv_phase(nc, a["x_t"], a["x"], a["rkvo"], a["decay"], a["first"], a["mixes"], x1)
    ffn_phase(nc, a["ident"], a["ffn_gate_up"], a["ffn_down"], a["ffn_s_gate_up"], a["ffn_s_down"], x1, x2)
    attention_phase(nc, a["ident"], a["mla_latent"], a["mla_heads"], a["mla_pe"], a["mla_ln_q"], a["mla_ln_kv"],
                    a["rope_q"], a["rope_k"], a["mask"], x2, x3)
    moe_phase(nc, a["ident"], a["router_w"], a["e_bias"], a["counts"], a["earlier"], a["experts"], a["shared"],
              a["zeros"], x3, slots, slots_out, out)


def constants():
    inv = np.float32(1.0) / np.float32(10000.0) ** (np.arange(0, DR, 2, dtype=np.float32) / np.float32(DR))
    angle = np.outer(np.arange(SEQ, dtype=np.float32), inv.astype(np.float32)).astype(np.float32)
    cos = np.cos(np.concatenate([angle, angle], 1))
    sin = np.sin(np.concatenate([-angle, angle], 1))
    rope = np.stack([cos, sin]).reshape(2, 2, P, DR).transpose(2, 0, 1, 3).astype(np.float32)
    later = np.triu(np.ones((P, P), np.float32), 1)
    return {
        "ident": np.eye(P, dtype=np.float32),
        "rope_k": rope,
        "rope_q": rope * np.float32((DN + DR) ** -0.5),
        "mask": np.concatenate([np.zeros((P, P), np.float32), later * np.float32(MASKED)], 1),
        "counts": np.tile(np.arange(E, dtype=np.float32), (P, 1)),
        "earlier": later,
        "zeros": np.zeros((P, D), np.float32),
    }


def layouts(t):
    x = t["L0_attn_hidden_states"].reshape(TOKENS, D)

    def by_chunk(w):
        return w.reshape(CH, P, KD, P).transpose(0, 3, 2, 1).reshape(CH, P, D)

    def by_part(w):
        return w.reshape(KD, P, -1).transpose(1, 0, 2)

    qb = t["L1_attn_w_qb"].reshape(HEADS, DN + DR, QLR)
    kvb = t["L1_attn_w_kvb"].reshape(HEADS, DN + DV, KVL)
    heads = np.concatenate([qb[:, :DN], kvb[:, :DN], kvb[:, DN:],
                            t["L1_attn_w_o"].T.reshape(HEADS, DV, D)], 2)
    scales = np.zeros((2, HPAD), np.float32)
    scales[0, :HID] = t["L0_ffn_s_gate"]
    scales[1, :HID] = t["L0_ffn_s_up"]
    gate_up = [t[f"L1_ffn_W_{w}"].reshape(E, KD, P, I).transpose(0, 2, 1, 3).reshape(E, P, KD * I)
               for w in ("gate", "up")]
    return {
        "x": x,
        "x_t": x.T,
        "rkvo": np.concatenate([by_chunk(t[f"L0_attn_W{q}"]) for q in "rkv"]
                               + [t["L0_attn_Wo"].T.reshape(CH, P, D)], 2),
        "decay": t["L0_attn_time_decay"].T,
        "first": t["L0_attn_time_first"].T,
        "mixes": np.stack([t[f"L0_attn_time_mix_{q}"].reshape(KD, P) for q in "rkv"]).reshape(3 * KD, P).T,
        "ffn_gate_up": np.stack([t["L0_ffn_wq_gate"].T, t["L0_ffn_wq_up"].T]),
        "ffn_down": t["L0_ffn_wq_down"].T,
        "ffn_s_gate_up": scales.reshape(2, HC, P).transpose(2, 0, 1),
        "ffn_s_down": t["L0_ffn_s_down"],
        "mla_latent": np.concatenate([t["L1_attn_w_qa"], t["L1_attn_w_kva"]]).T,
        "mla_heads": heads.reshape(HEADS // HG, HG, P, MLAC).transpose(0, 2, 1, 3).reshape(HEADS // HG, P, -1),
        "mla_pe": qb[:, DN:].reshape(HEADS * DR, QLR).T.reshape(2, QP, -1).transpose(1, 0, 2).reshape(QP, -1),
        "mla_ln_q": t["L1_attn_q_a_ln_w"].reshape(2, QP).T,
        "mla_ln_kv": t["L1_attn_kv_a_ln_w"],
        "router_w": t["L1_ffn_router_w"].T,
        "e_bias": t["L1_ffn_e_bias"],
        "experts": np.concatenate(gate_up + [t["L1_ffn_W_down"]], 2),
        "shared": np.stack([by_part(t[f"L1_ffn_shared_{w}"].T) for w in ("gate", "up", "down")], 1)
        .reshape(P, -1),
    }


def kernel(**inputs):
    import concourse.bacc as bacc
    from concourse.bass_utils import run_bass_kernel_spmd

    nc = bacc.Bacc("TRN2", target_bir_lowering=False, num_devices=1)
    laid = {**layouts({k: np.asarray(v) for k, v in inputs.items()}), **constants()}
    arrays = {f"in_{k}": np.ascontiguousarray(v) for k, v in laid.items()}
    aps = {k: nc.dram_tensor(f"in_{k}", arrays[f"in_{k}"].shape, mybir.dt.from_np(arrays[f"in_{k}"].dtype),
                             kind="ExternalInput").ap() for k in laid}
    out = nc.dram_tensor("out", (TOKENS, D), F32, kind="ExternalOutput").ap()
    rwkv_attention_moe_program(nc, aps, out)
    r = run_bass_kernel_spmd(nc, [arrays], core_ids=[0])
    return r.results[0]["out"].reshape(TOKENS // SEQ, SEQ, D)
```

```python
import numpy as np
import concourse.bass as bass
from concourse import mybir
from contextlib import ExitStack

F32 = mybir.dt.float32
F32R = mybir.dt.float32r
BF16 = mybir.dt.bfloat16
U32 = mybir.dt.uint32
I32 = mybir.dt.int32
ALU = mybir.AluOpType
ACT = mybir.ActivationFunctionType
AX = mybir.AxisListType

P = 128
D = 256
KD = D // P
SEQ = 256
TOKENS = 16 * SEQ
BLK = 512
BS = BLK // SEQ
BT = BLK // P
NB = TOKENS // BLK
LN_EPS = 1e-5

HH, HL, LH = (0, 0), (0, 1), (1, 0)
PARTS = (HH, HL, LH)


def over_blocks(eng, body):
    body(0, first=True, last=False)
    with eng.Fori(1, NB - 1) as blk:
        body(blk, first=False, last=False)
    body(NB - 1, first=False, last=True)


def over_block_pairs(eng, body):
    body(0, first=True, last=False, par=0)
    with eng.Fori(0, (NB - 2) // 2) as i:
        body(2 * i + 1, first=False, last=False, par=1)
        body(2 * i + 2, first=False, last=False, par=0)
    body(NB - 1, first=False, last=True, par=1)


def wait_reuse(eng, sem, n, depth):
    if isinstance(n, int) and n < depth:
        return
    eng.wait_ge(sem, n - depth + 1)


def wait_first(eng, sem, value, passed):
    eng.wait_ge(sem, value)
    eng.sem_inc(passed, 1)


class Scope:

    def __init__(self, nc, ctx, phase):
        self.nc, self.ctx, self.phase = nc, ctx, phase
        self.sems = []
        ctx.callback(self.clear)

    def clear(self):
        self.nc.clear_and_free_semaphores(self.sems)
        self.nc.all_engine_barrier()

    def sb(self, name, shape, dt=F32):
        return self.ctx.enter_context(self.nc.sbuf_tensor(f"{self.phase}_{name}", shape, dt))

    def ps(self, name):
        return self.ctx.enter_context(self.nc.psum_tensor(f"{self.phase}_{name}", [P, 512], F32))

    def sem(self, name):
        self.sems.append(self.nc.alloc_semaphore(name=f"{self.phase}_{name}"))
        return self.sems[-1]


def rows(dram, blk):
    return dram[bass.ds(blk * BLK, BLK), :].rearrange("(j p) d -> p j d", p=P)


CH = 16
WCOLS = 3 * D + D


def rwkv_phase(nc, x_t, x_tok, w_rkvo, decay, first_u, mixes, x1):
    with ExitStack() as ctx:
        s = Scope(nc, ctx, "rwkv")
        w_part = [s.sb("w_high", [P, CH, WCOLS], F32R), s.sb("w_low", [P, CH, WCOLS], F32R)]
        w_raw = s.sb("w_raw", [P, 2, WCOLS])
        decay_w = s.sb("decay_w", [P, CH])
        decay_e = s.sb("decay_e", [P, CH])
        bonus_u = s.sb("bonus_u", [P, CH])
        mix = s.sb("mix", [P, 3 * KD])
        mix_rest = s.sb("mix_rest", [P, 3 * KD])
        x_in = s.sb("x_in", [P, KD, BS, SEQ + 1])
        mixed = s.sb("mixed", [P, 3, KD, BLK])
        m_part = [s.sb("m_high", [P, 3, KD, BLK], F32R), s.sb("m_low", [P, 3, KD, BLK], F32R)]
        gate = s.sb("gate", [P, 2, BLK])
        key = s.sb("key", [P, 2, BLK])
        kv = s.sb("kv", [P, BLK])
        state = s.sb("state", [P, BS, SEQ + 1])
        o_part = [s.sb("o_high", [P, 2, BLK], F32R), s.sb("o_low", [P, 2, BLK], F32R)]
        x_res = s.sb("x_res", [P, BT, D])
        stats = s.sb("stats", [P, BT, 6])
        moments = s.sb("moments", [P, BT, 2])
        minus_half = s.sb("minus_half", [P, BT])
        var_eps = s.sb("var_eps", [P, BT])
        rstd = s.sb("rstd", [P, BT])
        proj_ps = [[s.ps(f"{q}{i}") for q in ("r", "k", "v")] for i in range(2)]
        out_ps = [s.ps("out0"), s.ps("out1")]

        consts_in = s.sem("consts_in")
        passed = s.sem("passed")
        raw_in = [s.sem("raw_in0"), s.sem("raw_in1")]
        w_high_done = s.sem("w_high_done")
        w_low_done = s.sem("w_low_done")
        x_in_done = s.sem("x_in_done")
        res_in = s.sem("res_in")
        stored = s.sem("stored")
        zeroed = s.sem("zeroed")
        decay_exp = s.sem("decay_exp")
        decay_done = s.sem("decay_done")
        rest_done = s.sem("rest_done")
        shift_scaled = s.sem("shift_scaled")
        mixed_done = s.sem("mixed_done")
        m_high_done = s.sem("m_high_done")
        m_low_done = s.sem("m_low_done")
        projected = [s.sem(f"{q}_projected") for q in ("r", "k", "v")]
        gate_done = s.sem("gate_done")
        key_done = s.sem("key_done")
        kv_done = s.sem("kv_done")
        scan_done = s.sem("scan_done")
        wkv_done = s.sem("wkv_done")
        gated_done = s.sem("gated_done")
        o_high_done = s.sem("o_high_done")
        o_low_done = s.sem("o_low_done")
        step_out_done = s.sem("step_out_done")
        res_added = s.sem("res_added")
        stats_done = s.sem("stats_done")
        var_done = s.sem("var_done")
        rstd_done = s.sem("rstd_done")
        normed = s.sem("normed")

        def x_now(k):
            return x_in[:, k, :, 1:SEQ + 1]

        def x_before(k):
            return x_in[:, k, :, 0:SEQ]

        block = ctx.enter_context(nc.Block())

        @block.sync
        def _(sp):
            sp.dma_start(decay_e[:, :], decay).then_inc(consts_in, 16)
            sp.dma_start(bonus_u[:, :], first_u).then_inc(consts_in, 16)
            sp.dma_start(mix[:, :], mixes).then_inc(consts_in, 16)

            def load_x(blk):
                for k in range(KD):
                    sp.dma_start(x_now(k), x_t[k * P:(k + 1) * P, bass.ds(blk * BLK, BLK)]
                                 .rearrange("p (s t) -> p s t", s=BS)).then_inc(x_in_done, 16)

            def load_w(c):
                if c >= 2:
                    sp.wait_ge(w_high_done, c - 1)
                    sp.wait_ge(w_low_done, c - 1)
                sp.dma_start(w_raw[:, c % 2, :], w_rkvo[c]).then_inc(raw_in[c % 2], 16)

            sp.wait_ge(zeroed, 1)
            load_x(0)
            for c in range(4):
                load_w(c)

            def body(blk, first, last):
                if not first:
                    sp.wait_ge(stored, 16 * blk)
                sp.dma_start(x_res[:, :, :], rows(x_tok, blk)).then_inc(res_in, 16)
                if not last:
                    sp.wait_ge(shift_scaled, 3 * blk + 3)
                    sp.wait_ge(mixed_done, 3 * blk + 3)
                    load_x(blk + 1)
                if first:
                    for c in range(4, CH):
                        load_w(c)
                sp.wait_ge(normed, blk + 1)
                sp.dma_start(rows(x1, blk), x_res[:, :, :]).then_inc(stored, 16)

            over_blocks(sp, body)
            sp.wait_ge(stored, 16 * NB)

        @block.gpsimd
        def _(pool):
            nc.gpsimd.memset(minus_half[:, :], -0.5)
            nc.gpsimd.memset(x_in[:, :, :, 0:1], 0.0).then_inc(zeroed, 1)

            def body(blk, first, last):
                for c in range(CH):
                    n = CH * blk + c
                    pool.wait_ge(gate_done, n + 1)
                    pool.wait_ge(wkv_done, n + 1)
                    nc.gpsimd.tensor_tensor(gate[:, c % 2, :], key[:, c % 2, :], gate[:, c % 2, :],
                                            ALU.mult).then_inc(gated_done, 1)
                    if c == 2 and not first:
                        rsqrt(blk - 1)

            def rsqrt(blk):
                pool.wait_ge(var_done, blk + 1)
                nc.gpsimd.tensor_tensor(rstd[:, :], var_eps[:, :], minus_half[:, :], ALU.pow)\
                    .then_inc(rstd_done, 1)

            over_blocks(pool, body)
            rsqrt(NB - 1)

        @block.scalar
        def _(act):
            act.wait_ge(consts_in, 48)
            nc.scalar.activation(decay_e[:, :], decay_e[:, :], ACT.Exp).then_inc(decay_exp, 1)
            act.wait_ge(decay_exp, 1)
            nc.scalar.activation(decay_w[:, :], decay_e[:, :], ACT.Exp, scale=-1.0)\
                .then_inc(decay_done, 1)

            def shift_scale(blk, q):
                act.wait_ge(x_in_done, 32 * (blk + 1))
                if not (isinstance(blk, int) and blk == 0):
                    act.wait_ge(m_high_done, 3 * blk)
                    act.wait_ge(m_low_done, 3 * blk)
                for k in range(KD):
                    last = nc.scalar.activation(mixed[:, q, k, :].rearrange("p (s t) -> p s t", s=BS),
                                                x_before(k), ACT.Copy,
                                                scale=mix_rest[:, q * KD + k:q * KD + k + 1])
                last.then_inc(shift_scaled, 1)

            def m_high(blk, q):
                act.wait_ge(mixed_done, 3 * blk + q + 1)
                if not (isinstance(blk, int) and blk == 0):
                    act.wait_ge(projected[q], CH * blk)
                nc.scalar.activation(m_part[0][:, q, :, :], mixed[:, q, :, :], ACT.Copy)\
                    .then_inc(m_high_done, 1)

            def w_high(c):
                act.wait_ge(raw_in[c % 2], 16 * (c // 2 + 1))
                nc.scalar.activation(w_part[0][:, c, :], w_raw[:, c % 2, :], ACT.Copy)\
                    .then_inc(w_high_done, 1)

            def o_high(n, c):
                act.wait_ge(gated_done, n + 1)
                wait_reuse(act, step_out_done, n, 2)
                nc.scalar.activation(o_part[0][:, c % 2, :], gate[:, c % 2, :], ACT.Copy)\
                    .then_inc(o_high_done, 1)

            act.wait_ge(rest_done, 1)
            for q in range(3):
                shift_scale(0, q)
            for q in range(3):
                m_high(0, q)
            for c in range(3):
                w_high(c)

            def body(blk, first, last):
                for c in range(CH):
                    n = CH * blk + c
                    act.wait_ge(projected[0], n + 1)
                    wait_reuse(act, o_high_done, n, 2)
                    wait_reuse(act, o_low_done, n, 2)
                    nc.scalar.activation(gate[:, c % 2, :], proj_ps[c % 2][0][:, :], ACT.Sigmoid)\
                        .then_inc(gate_done, 1)
                    if c == CH - 1 and not last:
                        m_high(blk + 1, 0)
                    act.wait_ge(projected[1], n + 1)
                    wait_reuse(act, gated_done, n, 2)
                    nc.scalar.activation(key[:, c % 2, :], proj_ps[c % 2][1][:, :], ACT.Copy)\
                        .then_inc(key_done, 1)
                    if c == CH - 1 and not last:
                        m_high(blk + 1, 1)
                        m_high(blk + 1, 2)
                    if not (first and c == 0):
                        o_high(n - 1, c - 1)
                    if first and c + 3 < CH:
                        w_high(c + 3)
                    if 4 <= c < 7 and not last:
                        shift_scale(blk + 1, c - 4)

            over_blocks(act, body)
            o_high(CH * NB - 1, CH - 1)

        @block.vector
        def _(dve):
            dve.wait_ge(consts_in, 48)
            nc.vector.tensor_scalar(mix_rest[:, :], mix[:, :], -1.0, 1.0, ALU.mult, ALU.add)\
                .then_inc(rest_done, 1)
            nc.vector.memset(state[:, :, 0:1], 0.0)
            dve.wait_ge(decay_done, 1)

            def mix_now(blk, q):
                dve.wait_ge(shift_scaled, 3 * blk + q + 1)
                for k in range(KD):
                    m = mixed[:, q, k, :].rearrange("p (s t) -> p s t", s=BS)
                    last = nc.vector.scalar_tensor_tensor(m, x_now(k), mix[:, q * KD + k:q * KD + k + 1],
                                                          m, ALU.mult, ALU.add)
                last.then_inc(mixed_done, 1)

            def m_low(blk, q):
                dve.wait_ge(m_high_done, 3 * blk + q + 1)
                nc.vector.tensor_tensor(m_part[1][:, q, :, :], mixed[:, q, :, :],
                                        m_part[0][:, q, :, :].bitcast(F32), ALU.subtract)\
                    .then_inc(m_low_done, 1)

            def w_low(c):
                dve.wait_ge(w_high_done, c + 1)
                nc.vector.tensor_tensor(w_part[1][:, c, :], w_raw[:, c % 2, :],
                                        w_part[0][:, c, :].bitcast(F32), ALU.subtract)\
                    .then_inc(w_low_done, 1)

            def o_low(n, c):
                dve.wait_ge(o_high_done, n + 1)
                nc.vector.tensor_tensor(o_part[1][:, c % 2, :], gate[:, c % 2, :],
                                        o_part[0][:, c % 2, :].bitcast(F32), ALU.subtract)\
                    .then_inc(o_low_done, 1)

            def layer_norm(blk):
                dve.wait_ge(step_out_done, CH * (blk + 1))
                dve.wait_ge(res_in, 16 * (blk + 1))
                for h in range(2):
                    last = nc.vector.tensor_tensor(x_res[:, 2 * h:2 * h + 2, :],
                                                   out_ps[h][:, :].rearrange("p (j d) -> p j d", d=D),
                                                   x_res[:, 2 * h:2 * h + 2, :], ALU.add)
                last.then_inc(res_added, 1)
                dve.wait_ge(res_added, blk + 1)
                for j in range(BT):
                    last = nc.vector.bn_stats(stats[:, j, :], x_res[:, j, :])
                last.then_inc(stats_done, 1)
                wait_first(dve, stats_done, 2 * blk + 1, passed)
                for j in range(BT):
                    last = nc.vector.bn_aggr(moments[:, j, :], stats[:, j, :])
                last.then_inc(stats_done, 1)
                dve.wait_ge(stats_done, 2 * blk + 2)
                nc.vector.tensor_scalar(var_eps[:, :], moments[:, :, 1], LN_EPS, None, ALU.add)\
                    .then_inc(var_done, 1)

            def apply_norm(blk):
                dve.wait_ge(rstd_done, blk + 1)
                for j in range(BT):
                    last = nc.vector.tensor_scalar(x_res[:, j, :], x_res[:, j, :], moments[:, j, 0:1],
                                                   rstd[:, j:j + 1], ALU.subtract, ALU.mult)
                last.then_inc(normed, 1)

            for q in range(3):
                mix_now(0, q)
            for q in range(3):
                m_low(0, q)
            for c in range(3):
                w_low(c)

            def body(blk, first, last):
                for c in range(CH):
                    n = CH * blk + c
                    if c == CH - 1 and not last:
                        m_low(blk + 1, 0)
                    dve.wait_ge(projected[2], n + 1)
                    dve.wait_ge(key_done, n + 1)
                    wait_reuse(dve, wkv_done, n, 1)
                    nc.vector.tensor_tensor(kv[:, :], proj_ps[c % 2][2][:, :], key[:, c % 2, :],
                                            ALU.mult).then_inc(kv_done, 1)
                    dve.wait_ge(kv_done, n + 1)
                    for q in range(BS):
                        last_scan = nc.vector.tensor_tensor_scan(
                            out=state[:, q, 1:SEQ + 1],
                            data0=decay_w[:, c:c + 1].to_broadcast([P, SEQ]),
                            data1=kv[:, q * SEQ:(q + 1) * SEQ], initial=0.0,
                            op0=ALU.mult, op1=ALU.add)
                    last_scan.then_inc(scan_done, 1)
                    dve.wait_ge(scan_done, n + 1)
                    nc.vector.scalar_tensor_tensor(key[:, c % 2, :].rearrange("p (s t) -> p s t", s=BS),
                                                   kv[:, :].rearrange("p (s t) -> p s t", s=BS),
                                                   bonus_u[:, c:c + 1], state[:, :, 0:SEQ],
                                                   ALU.mult, ALU.add).then_inc(wkv_done, 1)
                    if c == CH - 1 and not last:
                        m_low(blk + 1, 1)
                        m_low(blk + 1, 2)
                    if not (first and c == 0):
                        o_low(n - 1, c - 1)
                    if first and c + 3 < CH:
                        w_low(c + 3)
                    if c == 1 and not first:
                        layer_norm(blk - 1)
                    if c == 3 and not first:
                        apply_norm(blk - 1)
                    if 5 <= c < 8 and not last:
                        mix_now(blk + 1, c - 5)

            over_blocks(dve, body)
            o_low(CH * NB - 1, CH - 1)
            layer_norm(NB - 1)
            apply_norm(NB - 1)

        @block.tensor
        def _(pe):
            def project(blk, c, first):
                n = CH * blk + c
                if first:
                    pe.wait_ge(w_high_done, c + 1)
                    pe.wait_ge(w_low_done, c + 1)
                for q, read in enumerate((gate_done, key_done, kv_done)):
                    if c == 0:
                        pe.wait_ge(m_high_done, 3 * blk + q + 1)
                        pe.wait_ge(m_low_done, 3 * blk + q + 1)
                    wait_reuse(pe, read, n, 2)
                    for i, (wp, mp) in enumerate(PARTS):
                        for k in range(KD):
                            col = (q * KD + k) * P
                            last = nc.tensor.matmul(proj_ps[c % 2][q][:, :],
                                                    w_part[wp][:, c, col:col + P],
                                                    m_part[mp][:, q, k, :],
                                                    start=(i == 0 and k == 0),
                                                    stop=(i == 2 and k == KD - 1))
                    last.then_inc(projected[q], 1)

            def step_out(blk, c):
                n = CH * blk + c
                pe.wait_ge(o_high_done, n + 1)
                pe.wait_ge(o_low_done, n + 1)
                if c == 0 and not (isinstance(blk, int) and blk == 0):
                    pe.wait_ge(res_added, blk)
                for j in range(BT):
                    for i, (op, wp) in enumerate(PARTS):
                        last = nc.tensor.matmul(out_ps[j // 2][:, (j % 2) * D:(j % 2 + 1) * D],
                                                o_part[op][:, c % 2, j * P:(j + 1) * P],
                                                w_part[wp][:, c, 3 * D:4 * D],
                                                start=(c == 0 and i == 0 and j % 2 == 0),
                                                stop=(c == CH - 1 and i == 2),
                                                skip_group_check=True)
                last.then_inc(step_out_done, 1)

            def body(blk, first, last):
                for c in range(CH):
                    project(blk, c, first)
                    if c >= 2:
                        step_out(blk, c - 2)
                    elif not first:
                        step_out(blk - 1, CH - 2 + c)

            over_blocks(pe, body)
            step_out(NB - 1, CH - 2)
            step_out(NB - 1, CH - 1)


HID = 704
HC = -(-HID // P)
HPAD = HC * P
HTAIL = HID - (HC - 1) * P
ZERO_POINT = 128.0


def ffn_phase(nc, ident_dram, wq_gate_up, wq_down, s_gate_up, s_down, x1, x2):
    with ExitStack() as ctx:
        s = Scope(nc, ctx, "ffn")
        ident = s.sb("ident", [P, P])
        code = s.sb("code", [P, 2, KD, HID], I32)
        code_down = s.sb("code_down", [P, HC, D], I32)
        centred = s.sb("centred", [P, 2, KD, HID])
        centred_down = s.sb("centred_down", [P, HC, D])
        w_part = [s.sb("w_high", [P, 2, KD, HPAD], F32R), s.sb("w_low", [P, 2, KD, HPAD], F32R)]
        wd_part = [s.sb("wd_high", [P, HC, D], F32R), s.sb("wd_low", [P, HC, D], F32R)]
        scale_hid = s.sb("scale_hid", [P, 2, HC])
        scale_out = s.sb("scale_out", [P, 2, D])
        x_rows = s.sb("x_rows", [P, BT, D])
        x_res = s.sb("x_res", [P, BT, D])
        xt_part = [s.sb("xt_high", [P, 2, KD, BLK], F32R), s.sb("xt_low", [P, 2, KD, BLK], F32R)]
        gate = s.sb("gate", [P, 2, BLK])
        hidden = s.sb("hidden", [P, 2, BLK])
        h_part = [s.sb("h_high", [P, 2, BLK], F32R), s.sb("h_low", [P, 2, BLK], F32R)]
        y_rows = s.sb("y_rows", [P, BT, D])
        x_out = s.sb("x_out", [P, BT, D])
        stats = s.sb("stats", [P, BT, 6])
        moments = s.sb("moments", [P, BT, 2])
        minus_half = s.sb("minus_half", [P, BT])
        var_eps = s.sb("var_eps", [P, BT])
        rstd = s.sb("rstd", [P, BT])
        hid_ps = [[s.ps(f"{q}{i}") for q in ("gate", "up")] for i in range(2)]
        out_ps = [s.ps("out0"), s.ps("out1")]
        xt_ps = [s.ps("xt0"), s.ps("xt1")]

        codes_in = s.sem("codes_in")
        consts_in = s.sem("consts_in")
        passed = s.sem("passed")
        rows_in = s.sem("rows_in")
        res_in = s.sem("res_in")
        stored = s.sem("stored")
        padded = s.sem("padded")
        half_set = s.sem("half_set")
        centred_done = s.sem("centred_done")
        w_high_done = s.sem("w_high_done")
        w_low_done = s.sem("w_low_done")
        transposed = s.sem("transposed")
        xt_high_done = s.sem("xt_high_done")
        xt_low_done = s.sem("xt_low_done")
        gate_ready = s.sem("gate_ready")
        up_ready = s.sem("up_ready")
        gate_done = s.sem("gate_done")
        hidden_done = s.sem("hidden_done")
        h_high_done = s.sem("h_high_done")
        h_low_done = s.sem("h_low_done")
        step_out_done = s.sem("step_out_done")
        scaled = s.sem("scaled")
        res_added = s.sem("res_added")
        stats_done = s.sem("stats_done")
        var_done = s.sem("var_done")
        rstd_done = s.sem("rstd_done")
        normed = s.sem("normed")

        block = ctx.enter_context(nc.Block())

        @block.sync
        def _(sp):
            sp.dma_start(ident[:, :], ident_dram).then_inc(consts_in, 16)
            sp.dma_start(x_rows[:, :, :], rows(x1, 0)).then_inc(rows_in, 16)
            for i in range(2):
                sp.dma_start(code[:, i, :, :], wq_gate_up[i].rearrange("(k p) h -> p k h", p=P))\
                    .then_inc(codes_in, 16)
            sp.dma_start(code_down[:, 0:HC - 1, :],
                         wq_down[0:(HC - 1) * P, :].rearrange("(c p) d -> p c d", p=P)).then_inc(codes_in, 16)
            sp.dma_start(code_down[0:HTAIL, HC - 1, :], wq_down[(HC - 1) * P:HID, :]).then_inc(codes_in, 16)
            sp.dma_start(scale_hid[:, :, :], s_gate_up).then_inc(consts_in, 16)
            for i in range(2):
                sp.dma_start(scale_out[:, i, :], s_down.partition_broadcast(P)).then_inc(consts_in, 16)

            def store(blk):
                sp.wait_ge(normed, blk + 1)
                sp.dma_start(rows(x2, blk), x_out[:, :, :]).then_inc(stored, 16)

            def body(blk, first, last):
                if not last:
                    sp.wait_ge(transposed, blk + 1)
                    sp.dma_start(x_rows[:, :, :], rows(x1, blk + 1)).then_inc(rows_in, 16)
                if not first:
                    sp.wait_ge(res_added, blk)
                sp.dma_start(x_res[:, :, :], rows(x1, blk)).then_inc(res_in, 16)
                if not first:
                    store(blk - 1)

            over_blocks(sp, body)
            store(NB - 1)
            sp.wait_ge(stored, 16 * NB)

        @block.gpsimd
        def _(pool):
            nc.gpsimd.memset(minus_half[:, :], -0.5).then_inc(half_set, 1)
            pool.wait_ge(half_set, 1)

            def body(blk, first, last):
                pool.wait_ge(var_done, blk + 1)
                nc.gpsimd.tensor_tensor(rstd[:, :], var_eps[:, :], minus_half[:, :], ALU.pow)\
                    .then_inc(rstd_done, 1)

            over_blocks(pool, body)

        @block.scalar
        def _(act):
            def w_high(part):
                act.wait_ge(centred_done, part + 1)
                if part < 2 * KD:
                    i, k = part // KD, part % KD
                    out, src = w_part[0][:, i, k, 0:HID], centred[:, i, k, :]
                else:
                    out, src = wd_part[0][:, :, :], centred_down[:, :, :]
                nc.scalar.activation(out, src, ACT.Copy).then_inc(w_high_done, 1)

            def xt_high(blk, par):
                act.wait_ge(transposed, blk + 1)
                if not (isinstance(blk, int) and blk < 2):
                    act.wait_ge(up_ready, HC * (blk - 1))
                for k in range(KD):
                    nc.scalar.activation(xt_part[0][:, par, k, :], xt_ps[k][:, :], ACT.Copy)\
                        .then_inc(xt_high_done, 1)

            def h_high(n, j):
                act.wait_ge(hidden_done, n + 1)
                wait_reuse(act, step_out_done, n, 2)
                nc.scalar.activation(h_part[0][:, j % 2, :], hidden[:, j % 2, :], ACT.Copy)\
                    .then_inc(h_high_done, 1)

            for part in range(2 * KD + 1):
                w_high(part)
            xt_high(0, 0)

            def body(blk, first, last, par):
                for j in range(HC):
                    n = HC * blk + j
                    act.wait_ge(gate_ready, n + 1)
                    wait_reuse(act, hidden_done, n, 2)
                    nc.scalar.activation(gate[:, j % 2, :], hid_ps[j % 2][0][:, :], ACT.Silu,
                                         scale=scale_hid[:, 0, j:j + 1]).then_inc(gate_done, 1)
                    if j == 4 and not last:
                        xt_high(blk + 1, 1 - par)
                    if not (first and j == 0):
                        h_high(n - 1, (j - 1) % 2)

            over_block_pairs(act, body)
            h_high(HC * NB - 1, HC - 1)

        @block.vector
        def _(dve):
            nc.vector.memset(code_down[HTAIL:P, HC - 1, :], int(ZERO_POINT)).then_inc(padded, 1)
            for i in range(2):
                nc.vector.memset(w_part[i][:, :, :, HID:HPAD].bitcast(F32), 0.0).then_inc(padded, 1)
            dve.wait_ge(codes_in, 64)
            dve.wait_ge(padded, 1)
            for part in range(2 * KD + 1):
                if part < 2 * KD:
                    i, k = part // KD, part % KD
                    out, src = centred[:, i, k, :], code[:, i, k, :]
                else:
                    out, src = centred_down[:, :, :], code_down[:, :, :]
                nc.vector.tensor_scalar(out, src, -ZERO_POINT, None, ALU.add).then_inc(centred_done, 1)
            for part in range(2 * KD + 1):
                dve.wait_ge(w_high_done, part + 1)
                if part < 2 * KD:
                    i, k = part // KD, part % KD
                    out, src, high = (w_part[1][:, i, k, 0:HID], centred[:, i, k, :],
                                      w_part[0][:, i, k, 0:HID])
                else:
                    out, src, high = wd_part[1][:, :, :], centred_down[:, :, :], wd_part[0][:, :, :]
                nc.vector.tensor_tensor(out, src, high.bitcast(F32), ALU.subtract).then_inc(w_low_done, 1)

            def xt_low(blk, par):
                for k in range(KD):
                    dve.wait_ge(xt_high_done, KD * blk + k + 1)
                    nc.vector.tensor_tensor(xt_part[1][:, par, k, :], xt_ps[k][:, :],
                                            xt_part[0][:, par, k, :].bitcast(F32), ALU.subtract)\
                        .then_inc(xt_low_done, 1)

            def h_low(n, j):
                dve.wait_ge(h_high_done, n + 1)
                nc.vector.tensor_tensor(h_part[1][:, j % 2, :], hidden[:, j % 2, :],
                                        h_part[0][:, j % 2, :].bitcast(F32), ALU.subtract)\
                    .then_inc(h_low_done, 1)

            def layer_norm(blk):
                dve.wait_ge(step_out_done, HC * (blk + 1))
                if not (isinstance(blk, int) and blk == 0):
                    dve.wait_ge(normed, blk)
                for h in range(2):
                    last = nc.vector.tensor_tensor(y_rows[:, 2 * h:2 * h + 2, :],
                                                   out_ps[h][:, :].rearrange("p (j d) -> p j d", d=D),
                                                   scale_out[:, :, :], ALU.mult)
                last.then_inc(scaled, 1)
                dve.wait_ge(scaled, blk + 1)
                dve.wait_ge(res_in, 16 * (blk + 1))
                nc.vector.tensor_tensor(y_rows[:, :, :], y_rows[:, :, :], x_res[:, :, :], ALU.add).then_inc(res_added, 1)
                dve.wait_ge(res_added, blk + 1)
                for j in range(BT):
                    last = nc.vector.bn_stats(stats[:, j, :], y_rows[:, j, :])
                last.then_inc(stats_done, 1)
                wait_first(dve, stats_done, 2 * blk + 1, passed)
                for j in range(BT):
                    last = nc.vector.bn_aggr(moments[:, j, :], stats[:, j, :])
                last.then_inc(stats_done, 1)
                dve.wait_ge(stats_done, 2 * blk + 2)
                nc.vector.tensor_scalar(var_eps[:, :], moments[:, :, 1], LN_EPS, None, ALU.add)\
                    .then_inc(var_done, 1)

            def apply_norm(blk):
                dve.wait_ge(rstd_done, blk + 1)
                if not (isinstance(blk, int) and blk == 0):
                    dve.wait_ge(stored, 16 * blk)
                for j in range(BT):
                    last = nc.vector.tensor_scalar(x_out[:, j, :], y_rows[:, j, :], moments[:, j, 0:1],
                                                   rstd[:, j:j + 1], ALU.subtract, ALU.mult)
                last.then_inc(normed, 1)

            xt_low(0, 0)
            dve.wait_ge(consts_in, 16 * 4)

            def body(blk, first, last, par):
                for j in range(HC):
                    n = HC * blk + j
                    dve.wait_ge(up_ready, n + 1)
                    dve.wait_ge(gate_done, n + 1)
                    wait_reuse(dve, h_low_done, n, 2)
                    nc.vector.scalar_tensor_tensor(hidden[:, j % 2, :], hid_ps[j % 2][1][:, :],
                                                   scale_hid[:, 1, j:j + 1], gate[:, j % 2, :],
                                                   ALU.mult, ALU.mult).then_inc(hidden_done, 1)
                    if j == 4 and not last:
                        xt_low(blk + 1, 1 - par)
                    if not (first and j == 0):
                        h_low(n - 1, (j - 1) % 2)
                    if j == 1 and not first:
                        layer_norm(blk - 1)
                    if j == 2 and not first:
                        apply_norm(blk - 1)

            over_block_pairs(dve, body)
            h_low(HC * NB - 1, HC - 1)
            layer_norm(NB - 1)
            apply_norm(NB - 1)

        @block.tensor
        def _(pe):
            def transpose_rows(blk):
                pe.wait_ge(rows_in, 16 * (blk + 1))
                if not (isinstance(blk, int) and blk == 0):
                    pe.wait_ge(xt_low_done, KD * blk)
                for k in range(KD):
                    for j in range(BT):
                        last = nc.tensor.transpose(
                            xt_ps[k][:, j * P:(j + 1) * P],
                            x_rows[:, j, k * P:(k + 1) * P],
                            ident[:, :])
                last.then_inc(transposed, 1)

            def project(blk, j, first, par):
                n = HC * blk + j
                if j == 0:
                    pe.wait_ge(xt_high_done, KD * (blk + 1))
                    pe.wait_ge(xt_low_done, KD * (blk + 1))
                for i, (ready, read) in enumerate(((gate_ready, gate_done), (up_ready, hidden_done))):
                    if first and j == 0:
                        pe.wait_ge(w_high_done, KD * (i + 1))
                        pe.wait_ge(w_low_done, KD * (i + 1))
                        pe.wait_ge(padded, 3)
                    wait_reuse(pe, read, n, 2)
                    for q, (wp, xp) in enumerate(PARTS):
                        for k in range(KD):
                            last = nc.tensor.matmul(hid_ps[j % 2][i][:, :],
                                                    w_part[wp][:, i, k, j * P:(j + 1) * P],
                                                    xt_part[xp][:, par, k, :],
                                                    start=(q == 0 and k == 0),
                                                    stop=(q == 2 and k == KD - 1))
                    last.then_inc(ready, 1)

            def step_out(blk, j):
                n = HC * blk + j
                pe.wait_ge(h_high_done, n + 1)
                pe.wait_ge(h_low_done, n + 1)
                if isinstance(blk, int) and blk == 0:
                    if j == 0:
                        pe.wait_ge(w_high_done, 2 * KD + 1)
                        pe.wait_ge(w_low_done, 2 * KD + 1)
                elif j == 0:
                    pe.wait_ge(scaled, blk)
                for t in range(BT):
                    for i, (hp, wp) in enumerate(PARTS):
                        last = nc.tensor.matmul(out_ps[t // 2][:, (t % 2) * D:(t % 2 + 1) * D],
                                                h_part[hp][:, j % 2, t * P:(t + 1) * P],
                                                wd_part[wp][:, j, :],
                                                start=(j == 0 and i == 0 and t % 2 == 0),
                                                stop=(j == HC - 1 and i == 2),
                                                skip_group_check=True)
                last.then_inc(step_out_done, 1)

            pe.wait_ge(consts_in, 16 * 4)
            transpose_rows(0)

            def body(blk, first, last, par):
                for j in range(HC):
                    project(blk, j, first, par)
                    if j >= 2:
                        step_out(blk, j - 2)
                    elif not first:
                        step_out(blk - 1, HC - 2 + j)
                    if j == 3 and not last:
                        transpose_rows(blk + 1)

            over_block_pairs(pe, body)
            step_out(NB - 1, HC - 2)
            step_out(NB - 1, HC - 1)


NSEQ = TOKENS // SEQ
HEADS = 16
QLR = 192
QP = QLR // 2
KVL = 64
DN = 128
DR = 64
DV = 128
LATC = QLR + KVL + DR
RMS_EPS = 1e-6
SLOTS = 12
MLAC = QLR + KVL + KVL + D
HG = 4
MASKED = 1e30

TURNS = (("q1", 0, 0), ("o_before", 0, 0), ("q1", 1, 1), ("q1", 2, 2), ("k", 0, 2), ("q1", 3, 3),
         ("q0", 0, 4), ("o_before", 1, 4), ("q0", 1, 5), ("x", 0, 6), ("q0", 2, 6), ("q0", 3, 7),
         ("y_before", 0, 8), ("o0", 0, 9), ("o0", 1, 10), ("cq", 0, 10), ("y0", 0, 11))
FIRST_TURNS = 9


def turn_exists(kind, seq):
    if not isinstance(seq, int):
        return True
    if kind in ("o_before", "y_before"):
        return seq >= 1
    return seq + {"q0": 1, "k": 1, "x": 2, "cq": 2}.get(kind, 0) < NSEQ


def turns_before(seq, i, split_only=False):
    def counts(t, of):
        return turn_exists(t[0], of) and not (split_only and t[0][0] == "y")
    if not isinstance(seq, int):
        each = sum(counts(t, 1) for t in TURNS)
        return each * (seq - 1) + turns_before(1, i, split_only)
    done = sum(counts(t, of) for of in range(seq) for t in TURNS)
    return FIRST_TURNS + done + sum(counts(t, seq) for t in TURNS[:i])


def turn_of(kind, index):
    return next(i for i, t in enumerate(TURNS) if t[:2] == (kind, index))


def attention_phase(nc, ident_dram, w_lat, w_heads, w_pe, ln_q, ln_kv, rope_q, rope_k, mask_dram, x2, x3):
    with ExitStack() as ctx:
        s = Scope(nc, ctx, "mla")

        def both(name, shape):
            return [s.sb(name + "_high", shape, F32R), s.sb(name + "_low", shape, F32R)]

        ident = s.sb("ident", [P, P])
        mask = s.sb("mask", [P, SEQ])
        lnq = s.sb("lnq", [P, 2])
        lnkv = s.sb("lnkv", [P, KVL])
        rq = s.sb("rq", [P, 2, 2, DR])
        rk = s.sb("rk", [P, 2, 2, DR])
        w_raw = s.sb("w_raw", [P, 2, HG, MLAC])
        wl_raw = s.sb("wl_raw", [P, KD, LATC])
        wl_part = both("wl", [P, KD, LATC])
        wq_part = both("wq", [P, 2, 2 * HEADS * DR])
        wvo_part = both("wvo", [P, HEADS // 2, D])
        x_rows = s.sb("x_rows", [P, 2, D])
        x_res = s.sb("x_res", [P, 2, D])
        xt_part = both("xt", [P, KD, SEQ])
        squares = s.sb("squares", [P, QLR + KVL])
        mean_sq = s.sb("mean_sq", [P, 2])
        lat_rstd = s.sb("lat_rstd", [P, 2])
        cq_rows = s.sb("cq_rows", [P, 2, QLR])
        k_rows = s.sb("k_rows", [P, 2, KVL + DR])
        k_turn = s.sb("k_turn", [P, 2, 2, DR])
        cq_part = both("cq", [P, 2, SEQ])
        k_part = both("k", [P, 2, SEQ])
        v_part = both("v", [P, 2, 2, KVL])
        q_rows = s.sb("q_rows", [P, 2, HEADS, KVL + DR])
        q_cos = s.sb("q_cos", [P, 2, 512])
        q_sin = s.sb("q_sin", [P, 2, 512])
        q_part = both("q", [P, 2, HEADS * P])
        masked = s.sb("masked", [P, 2, 512])
        least = s.sb("least", [P, 2, HG])
        probs = s.sb("probs", [P, 3, 512])
        row_sum = s.sb("row_sum", [P, 2, HEADS])
        row_inv = s.sb("row_inv", [P, 8])
        p_part = both("p", [P, 2, 512])
        o_rows = s.sb("o_rows", [P, 2, HEADS * KVL])
        o_part = both("o", [P, 2, HEADS // 2, P])
        y_rows = s.sb("y_rows", [P, 2, D])
        x_out = s.sb("x_out", [P, 2, D])
        stats = s.sb("stats", [P, 2, 6])
        moments = s.sb("moments", [P, 2, 2])
        minus_half = s.sb("minus_half", [P, 2])
        var_eps = s.sb("var_eps", [P, 2])
        rstd = s.sb("rstd", [P, 2])
        score_ps = [s.ps("score0"), s.ps("score1")]
        pt_ps = [s.ps("pt0"), s.ps("pt1")]
        o_ps = [s.ps("o0"), s.ps("o1")]
        proj_ps = s.ps("proj")
        turn_ps = s.ps("turn")

        consts_in = s.sem("consts_in")
        passed = s.sem("passed")
        pe_in = s.sem("pe_in")
        raw_in = [s.sem("raw_in0"), s.sem("raw_in1")]
        rows_in = s.sem("rows_in")
        res_in = s.sem("res_in")
        stored = s.sem("stored")
        half_set = s.sem("half_set")
        wl_high = s.sem("wl_high")
        wl_low = s.sem("wl_low")
        wpe_high = s.sem("wpe_high")
        wpe_low = s.sem("wpe_low")
        multiplied = s.sem("multiplied")
        mult_high = s.sem("mult_high")
        mult_low = s.sem("mult_low")
        turn_filled = s.sem("turn_filled")
        turn_high = s.sem("turn_high")
        turn_read = s.sem("turn_read")
        lat_ready = s.sem("lat_ready")
        squared = s.sem("squared")
        ms_added = s.sem("ms_added")
        lat_rstd_done = s.sem("lat_rstd_done")
        lat_scaled = s.sem("lat_scaled")
        lat_done = s.sem("lat_done")
        v_high = s.sem("v_high")
        v_low = s.sem("v_low")
        q_ready = s.sem("q_ready")
        q_abs_done = s.sem("q_abs_done")
        q_turned = s.sem("q_turned")
        q_pe_done = s.sem("q_pe_done")
        scored = s.sem("scored")
        masked_done = s.sem("masked_done")
        exp_done = s.sem("exp_done")
        p_turned = s.sem("p_turned")
        p_high = s.sem("p_high")
        p_low = s.sem("p_low")
        summed = s.sem("summed")
        inv_done = s.sem("inv_done")
        o_normed = s.sem("o_normed")
        res_added = s.sem("res_added")
        stats_done = s.sem("stats_done")
        var_done = s.sem("var_done")
        rstd_done = s.sem("rstd_done")
        normed = s.sem("normed")

        CONSTS = 16 * 7

        def exists(seq):
            return not isinstance(seq, int) or 0 <= seq < NSEQ

        def late(seq):
            return not isinstance(seq, int) or seq > 0

        def slot_turns(seq, v):
            return [(i, t) for i, t in enumerate(TURNS) if t[2] == v and turn_exists(t[0], seq)]

        def unit_before(seq, v, back):
            return (seq, 0, v - back) if v >= back else (seq - 1, 1, v + SLOTS - back)

        def heads_of(v):
            return (0, range(HG * v, HG * v + HG), P) if v < 4 else (1, range(2 * v - 8, 2 * v - 6), SEQ)

        X0, CQ0, K0, X1, Q00, CQ1 = 0, 1, 2, 3, 4, 8
        LAT_PS = [proj_ps, o_ps[0], pt_ps[1], proj_ps]
        QUERY_PS = [o_ps[1], score_ps[0], score_ps[1], pt_ps[0], o_ps[0], o_ps[1], score_ps[0], score_ps[1]]

        block = ctx.enter_context(nc.Block())

        def over_sequences(eng, slot):
            def body(blk, first, last):
                for par in range(BS):
                    for v in range(SLOTS):
                        slot(BS * blk + par, par, v)
            over_blocks(eng, body)

        @block.sync
        def _(sp):
            sp.dma_start(ident[:, :], ident_dram).then_inc(consts_in, 16)
            sp.dma_start(wl_raw[:, :, :], w_lat.rearrange("(k p) c -> p k c", p=P)).then_inc(consts_in, 16)
            sp.dma_start(mask[:, :], mask_dram).then_inc(consts_in, 16)
            sp.dma_start(lnq[0:QP, :], ln_q).then_inc(consts_in, 16)
            sp.dma_start(lnkv[:, :], ln_kv.partition_broadcast(P)).then_inc(consts_in, 16)
            sp.dma_start(rq[:, :, :, :], rope_q).then_inc(consts_in, 16)
            sp.dma_start(rk[:, :, :, :], rope_k).then_inc(consts_in, 16)
            sp.dma_start(q_rows[0:QP, 1, :, :].rearrange("p h c -> p (h c)"), w_pe).then_inc(pe_in, 16)
            def seq_rows(dram, seq):
                return dram[bass.ds(seq * SEQ, SEQ), :].rearrange("(t p) d -> p t d", p=P)

            sp.dma_start(x_rows[:, :, :], seq_rows(x2, 0)).then_inc(rows_in, 16)
            for g in range(HEADS // HG):
                if g >= 2:
                    sp.wait_ge(multiplied, g - 1)
                sp.dma_start(w_raw[:, g % 2, :, :].rearrange("p h c -> p (h c)"), w_heads[g])\
                    .then_inc(raw_in[g % 2], 16)

            sp.wait_ge(turn_filled, X0 + 1)
            sp.dma_start(x_rows[:, :, :], seq_rows(x2, 1)).then_inc(rows_in, 16)

            def store(seq):
                sp.wait_ge(normed, seq + 1)
                sp.dma_start(seq_rows(x3, seq), x_out[:, :, :]).then_inc(stored, 16)

            def slot(seq, par, v):
                if v == 0 and exists(seq + 2):
                    if late(seq):
                        sp.wait_ge(turn_filled, turns_before(seq - 1, turn_of("x", 0)) + 1)
                    else:
                        sp.wait_ge(turn_filled, X1 + 1)
                    sp.dma_start(x_rows[:, :, :], seq_rows(x2, seq + 2)).then_inc(rows_in, 16)
                if v == 9:
                    if late(seq):
                        sp.wait_ge(res_added, 2 * seq)
                    sp.dma_start(x_res[:, :, :], seq_rows(x2, seq)).then_inc(res_in, 16)
                if v == 11 and late(seq):
                    store(seq - 1)

            over_sequences(sp, slot)
            store(NSEQ - 1)
            sp.wait_ge(stored, 16 * NSEQ)

        @block.gpsimd
        def _(pool):
            nc.gpsimd.memset(minus_half[:, :], -0.5).then_inc(half_set, 1)
            pool.wait_ge(half_set, 1)

            def latent_rstd(n):
                wait_first(pool, squared, n + 1, passed)
                nc.gpsimd.tensor_scalar(mean_sq[:, :], mean_sq[:, :], RMS_EPS, None, ALU.add)\
                    .then_inc(ms_added, 1)
                pool.wait_ge(ms_added, n + 1)
                if isinstance(n, int) and 0 < n < 4:
                    pool.wait_ge(lat_scaled, n)
                nc.gpsimd.tensor_tensor(lat_rstd[:, :], mean_sq[:, :], minus_half[:, :], ALU.pow)\
                    .then_inc(lat_rstd_done, 1)

            def rope_sum(n, tile, c):
                pool.wait_ge(q_turned, n + 1)
                nc.gpsimd.tensor_tensor(
                    q_rows[:, tile, 8 * c:8 * c + 8, KVL:KVL + DR],
                    q_cos[:, c, :].rearrange("p (h d) -> p h d", d=DR),
                    q_sin[:, c, :].rearrange("p (h d) -> p h d", d=DR), ALU.add).then_inc(q_pe_done, 1)

            def norm_rstd(seq):
                pool.wait_ge(var_done, seq + 1)
                nc.gpsimd.tensor_tensor(rstd[:, :], var_eps[:, :], minus_half[:, :], ALU.pow)\
                    .then_inc(rstd_done, 1)

            latent_rstd(0)
            latent_rstd(1)
            pool.wait_ge(wpe_low, 2)
            for c in range(2):
                rope_sum(c, 0, c)
            latent_rstd(2)
            latent_rstd(3)
            for c in range(2):
                rope_sum(2 + c, 1, c)

            def slot(seq, par, v):
                if v in (2, 3, 6, 7) and exists(seq + 1):
                    tile, c = v // 4, v % 4 - 2
                    if tile == 0:
                        if late(seq):
                            pool.wait_ge(turn_filled, turns_before(seq - 1, turn_of("q0", 3)) + 1)
                        else:
                            pool.wait_ge(turn_filled, Q00 + 4)
                    else:
                        pool.wait_ge(turn_filled, turns_before(seq, turn_of("q1", 3)) + 1)
                    rope_sum(4 * (seq + 1) + 2 * tile + c, tile, c)
                if v in (8, 9) and exists(seq + 2):
                    latent_rstd(2 * (seq + 2) + v - 8)
                if v == 9 and late(seq):
                    norm_rstd(seq - 1)

            over_sequences(pool, slot)
            norm_rstd(NSEQ - 1)

        @block.scalar
        def _(act):
            act.wait_ge(consts_in, CONSTS)
            nc.scalar.activation(wl_part[0][:, :, :], wl_raw[:, :, :], ACT.Copy).then_inc(wl_high, 1)
            act.wait_ge(pe_in, 16)
            for k in range(2):
                nc.scalar.activation(wq_part[0][0:QP, k, HEADS * KVL:],
                                     q_rows[0:QP, 1, 8 * k:8 * k + 8, :].rearrange("p h c -> p (h c)"),
                                     ACT.Copy).then_inc(wpe_high, 1)

            def multiplied_high(g):
                act.wait_ge(multiplied, g + 1)
                nc.scalar.activation(wq_part[0][0:QP, :, g * HG * KVL:(g + 1) * HG * KVL],
                                     score_ps[g % 2][0:QP, :].rearrange("p (k c) -> p k c", k=2), ACT.Copy)
                nc.scalar.activation(wvo_part[0][:, 2 * g:2 * g + 2, :],
                                     pt_ps[g % 2][:, :].rearrange("p (a d) -> p a d", a=2), ACT.Copy)\
                    .then_inc(mult_high, 1)

            def split_turn(kind, index, filled, seq, par):
                act.wait_ge(turn_filled, filled)
                if kind == "x":
                    out, src, scale = xt_part[0][:, :, :], turn_ps[:, :].rearrange("p (k t) -> p k t", k=KD), 1.0
                elif kind == "k":
                    out, src, scale = k_part[0][:, 1 - par, :], turn_ps[:, 0:SEQ], -1.0
                elif kind in ("q0", "q1"):
                    tile = int(kind[1])
                    out, src, scale = q_part[0][:, tile, index * 512:(index + 1) * 512], turn_ps[:, :], 1.0
                elif kind in ("o0", "o_before"):
                    tile = 0 if kind == "o0" else 1
                    out, src, scale = (o_part[0][:, tile, 4 * index:4 * index + 4, :],
                                       turn_ps[:, :].rearrange("p (a t) -> p a t", a=4), 1.0)
                if kind == "cq":
                    for k in range(2):
                        last = nc.scalar.activation(cq_part[0][0:QP, k, :], turn_ps[0:QP, k * SEQ:(k + 1) * SEQ],
                                                    ACT.Copy, scale=lnq[0:QP, k:k + 1])
                    last.then_inc(turn_high, 1)
                else:
                    nc.scalar.activation(out, src, ACT.Copy, scale=scale).then_inc(turn_high, 1)

            def squares_of(n, ps=proj_ps):
                act.wait_ge(lat_ready, n + 1)
                if not (isinstance(n, int) and n == 0):
                    act.wait_ge(lat_rstd_done, n)
                    act.wait_ge(squared, n)
                nc.scalar.activation(squares[:, 0:QLR], ps[:, 0:QLR], ACT.Square, scale=float(QLR) ** -0.5,
                                     accum_out=mean_sq[:, 0:1])
                nc.scalar.activation(squares[:, QLR:], ps[:, QLR:QLR + KVL], ACT.Square,
                                     scale=float(KVL) ** -0.5, accum_out=mean_sq[:, 1:2]).then_inc(squared, 1)

            def q_abs(n, tile, c, ps=proj_ps):
                act.wait_ge(q_ready, n + 1)
                nc.scalar.activation(q_rows[:, tile, 8 * c:8 * c + 8, 0:KVL],
                                     ps[:, :].rearrange("p (h c) -> p h c", c=KVL), ACT.Copy,
                                     scale=float(DN + DR) ** -0.5).then_inc(q_abs_done, 1)

            def values_high(seq, par):
                act.wait_ge(lat_done, 2 * seq + 2)
                nc.scalar.activation(v_part[0][:, par, :, :], k_rows[:, :, 0:KVL], ACT.Copy).then_inc(v_high, 1)

            def exps(seq, v):
                m = SLOTS * seq + v
                tile, heads, keys = heads_of(v)
                act.wait_ge(masked_done, m + 1)
                if v in (0, 4) and late(seq):
                    act.wait_ge(o_normed, 4 * seq - 2 + v // 2)
                wait_reuse(act, p_turned, m, 3)
                for i, h in enumerate(heads):
                    last = nc.scalar.activation(probs[:, v % 3, i * keys:(i + 1) * keys],
                                                masked[:, v % 2, i * keys:(i + 1) * keys], ACT.Exp,
                                                bias=least[:, v % 2, i:i + 1], scale=-1.0,
                                                accum_out=row_sum[:, tile, h:h + 1])
                last.then_inc(exp_done, 1)

            def probs_high(m, v):
                act.wait_ge(p_turned, m + 1)
                wait_reuse(act, summed, m, 2)
                nc.scalar.activation(p_part[0][:, v % 2, :], pt_ps[v % 2][:, :], ACT.Copy).then_inc(p_high, 1)

            split_turn("x", 0, X0 + 1, 0, 0)
            multiplied_high(0)
            multiplied_high(1)
            squares_of(0, LAT_PS[0])
            squares_of(1, LAT_PS[1])
            multiplied_high(2)
            multiplied_high(3)
            split_turn("cq", 0, CQ0 + 1, 0, 0)
            split_turn("k", 0, K0 + 1, 0, 1)
            values_high(0, 0)
            split_turn("x", 0, X1 + 1, 0, 0)
            for c in range(2):
                q_abs(c, 0, c, QUERY_PS[c])
            squares_of(2, LAT_PS[2])
            squares_of(3, LAT_PS[3])
            act.wait_ge(wpe_low, 2)
            for c in range(2):
                q_abs(4 + c, 1, c, QUERY_PS[4 + c])
            for g in range(4):
                split_turn("q0", g, Q00 + g + 1, 0, 0)
            split_turn("cq", 0, CQ1 + 1, 0, 0)

            def slot(seq, par, v):
                of, _, v2 = unit_before(seq, v, 2)
                if exists(of):
                    probs_high(SLOTS * of + v2, v2)
                if v in (8, 9) and exists(seq + 2):
                    squares_of(2 * (seq + 2) + v - 8)
                turns = [(i, kind, index) for i, (kind, index, _) in slot_turns(seq, v) if kind[0] != "y"]
                for i, kind, index in turns[:1]:
                    split_turn(kind, index, turns_before(seq, i) + 1, seq, par)
                exps(seq, v)
                if v in (0, 1, 4, 5) and exists(seq + 1):
                    tile, c = v // 4, v % 4
                    if tile == 1:
                        act.wait_ge(turn_filled, turns_before(seq, turn_of("q1", 3)) + 1)
                    elif late(seq):
                        act.wait_ge(turn_filled, turns_before(seq - 1, turn_of("q0", 3)) + 1)
                    else:
                        act.wait_ge(turn_filled, Q00 + 4)
                    q_abs(8 * (seq + 1) + 4 * tile + c, tile, c)
                if v == 3 and exists(seq + 1):
                    values_high(seq + 1, 1 - par)
                for i, kind, index in turns[1:]:
                    split_turn(kind, index, turns_before(seq, i) + 1, seq, par)

            over_sequences(act, slot)
            for v in (SLOTS - 2, SLOTS - 1):
                probs_high(SLOTS * (NSEQ - 1) + v, v)
            for i, (kind, index, v) in enumerate(TURNS):
                if kind == "o_before":
                    split_turn(kind, index, turns_before(NSEQ, i) + 1, NSEQ, 0)

        @block.vector
        def _(dve):
            dve.wait_ge(consts_in, CONSTS)
            dve.wait_ge(wl_high, 1)
            nc.vector.tensor_tensor(wl_part[1][:, :, :], wl_raw[:, :, :], wl_part[0][:, :, :].bitcast(F32),
                                    ALU.subtract).then_inc(wl_low, 1)
            for k in range(2):
                dve.wait_ge(wpe_high, k + 1)
                nc.vector.tensor_tensor(wq_part[1][0:QP, k, HEADS * KVL:],
                                        q_rows[0:QP, 1, 8 * k:8 * k + 8, :].rearrange("p h c -> p (h c)"),
                                        wq_part[0][0:QP, k, HEADS * KVL:].bitcast(F32), ALU.subtract)\
                    .then_inc(wpe_low, 1)

            def multiplied_low(g):
                dve.wait_ge(mult_high, g + 1)
                cols = slice(g * HG * KVL, (g + 1) * HG * KVL)
                nc.vector.tensor_tensor(wq_part[1][0:QP, :, cols],
                                        score_ps[g % 2][0:QP, :].rearrange("p (k c) -> p k c", k=2),
                                        wq_part[0][0:QP, :, cols].bitcast(F32), ALU.subtract)
                nc.vector.tensor_tensor(wvo_part[1][:, 2 * g:2 * g + 2, :],
                                        pt_ps[g % 2][:, :].rearrange("p (a d) -> p a d", a=2),
                                        wvo_part[0][:, 2 * g:2 * g + 2, :].bitcast(F32), ALU.subtract)\
                    .then_inc(mult_low, 1)

            def split_turn(kind, index, high, seq, par):
                dve.wait_ge(turn_high, high)
                if kind == "cq":
                    for k in range(2):
                        last = nc.vector.scalar_tensor_tensor(
                            cq_part[1][0:QP, k, :], turn_ps[0:QP, k * SEQ:(k + 1) * SEQ], lnq[0:QP, k:k + 1],
                            cq_part[0][0:QP, k, :].bitcast(F32), ALU.mult, ALU.subtract)
                    last.then_inc(turn_read, 1)
                elif kind == "k":
                    nc.vector.scalar_tensor_tensor(k_part[1][:, 1 - par, :], turn_ps[:, 0:SEQ], -1.0,
                                                   k_part[0][:, 1 - par, :].bitcast(F32),
                                                   ALU.mult, ALU.subtract).then_inc(turn_read, 1)
                else:
                    if kind == "x":
                        part, where = xt_part, (slice(None), slice(None), slice(None))
                        src = turn_ps[:, :].rearrange("p (k t) -> p k t", k=KD)
                    elif kind in ("q0", "q1"):
                        part, where = q_part, (slice(None), int(kind[1]), slice(index * 512, (index + 1) * 512))
                        src = turn_ps[:, :]
                    else:
                        tile = 0 if kind == "o0" else 1
                        part, where = o_part, (slice(None), tile, slice(4 * index, 4 * index + 4), slice(None))
                        src = turn_ps[:, :].rearrange("p (a t) -> p a t", a=4)
                    nc.vector.tensor_tensor(part[1][where], src, part[0][where].bitcast(F32), ALU.subtract)\
                        .then_inc(turn_read, 1)

            def latent(n, t, ps=proj_ps):
                dve.wait_ge(lat_rstd_done, n + 1)
                wait_reuse(dve, lat_done, n, 2)
                nc.vector.tensor_scalar(cq_rows[:, t, :], ps[:, 0:QLR], lat_rstd[:, 0:1], None, ALU.mult)
                nc.vector.scalar_tensor_tensor(k_rows[:, t, 0:KVL], ps[:, QLR:QLR + KVL], lat_rstd[:, 1:2],
                                               lnkv[:, :], ALU.mult, ALU.mult)
                at = QLR + KVL
                nc.vector.tensor_tensor(k_turn[:, t, 0, :], ps[:, at:at + DR], rk[:, 0, t, :], ALU.mult)
                for a in range(2):
                    b = at + (1 - a) * (DR // 2)
                    last = nc.vector.tensor_tensor(k_turn[:, t, 1, a * (DR // 2):(a + 1) * (DR // 2)],
                                                   ps[:, b:b + DR // 2],
                                                   rk[:, 1, t, a * (DR // 2):(a + 1) * (DR // 2)], ALU.mult)
                last.then_inc(lat_scaled, 1)
                dve.wait_ge(lat_scaled, n + 1)
                nc.vector.tensor_tensor(k_rows[:, t, KVL:], k_turn[:, t, 0, :], k_turn[:, t, 1, :], ALU.add)\
                    .then_inc(lat_done, 1)

            def values_low(seq, par):
                dve.wait_ge(v_high, seq + 1)
                nc.vector.tensor_tensor(v_part[1][:, par, :, :], k_rows[:, :, 0:KVL],
                                        v_part[0][:, par, :, :].bitcast(F32), ALU.subtract).then_inc(v_low, 1)

            def q_turn(n, ready, tile, c, ps=proj_ps):
                dve.wait_ge(q_ready, ready)
                wait_reuse(dve, q_pe_done, n, 2)
                q = ps[:, :].rearrange("p (h a d) -> p h a d", a=2, d=DR // 2)
                nc.vector.tensor_tensor(q_cos[:, c, :].rearrange("p (h d) -> p h d", d=DR),
                                        ps[:, :].rearrange("p (h d) -> p h d", d=DR),
                                        rq[:, 0, tile:tile + 1, :].to_broadcast([P, 8, DR]), ALU.mult)
                for a in range(2):
                    half = slice(a * (DR // 2), (a + 1) * (DR // 2))
                    last = nc.vector.tensor_tensor(
                        q_sin[:, c, :].rearrange("p (h d) -> p h d", d=DR)[:, :, half], q[:, :, 1 - a, :],
                        rq[:, 1, tile:tile + 1, half].to_broadcast([P, 8, DR // 2]), ALU.mult)
                last.then_inc(q_turned, 1)

            def mask_scores(seq, v):
                m = SLOTS * seq + v
                tile, heads, keys = heads_of(v)
                wait_reuse(dve, exp_done, m, 2)
                wait_first(dve, scored, m + 1, passed)
                for i, h in enumerate(heads):
                    last = nc.vector.tensor_tensor_reduce(
                        out=masked[:, v % 2, i * keys:(i + 1) * keys],
                        in0=score_ps[v % 2][:, i * keys:(i + 1) * keys],
                        in1=mask[:, SEQ - keys:SEQ], scale=1.0, scalar=3.0e38,
                        op0=ALU.add, op1=ALU.min, accum_out=least[:, v % 2, i:i + 1])
                last.then_inc(masked_done, 1)

            def probs_low(m, v):
                dve.wait_ge(p_high, m + 1)
                nc.vector.tensor_tensor(p_part[1][:, v % 2, :], pt_ps[v % 2][:, :],
                                        p_part[0][:, v % 2, :].bitcast(F32), ALU.subtract).then_inc(p_low, 1)

            def normalize(seq, tile, half):
                n = 4 * seq + 2 * tile + half
                unit = SLOTS * seq + (2 * half + 1 if tile == 0 else 4 * half + 7)
                dve.wait_ge(summed, unit + 1)
                if not (isinstance(n, int) and n == 0):
                    dve.wait_ge(o_normed, n)
                nc.vector.reciprocal(row_inv[:, :], row_sum[:, tile, 8 * half:8 * half + 8]).then_inc(inv_done, 1)
                dve.wait_ge(inv_done, n + 1)
                if late(seq):
                    if tile == 0:
                        dve.wait_ge(turn_filled, turns_before(seq - 1, turn_of("o0", half)) + 1)
                    else:
                        dve.wait_ge(turn_filled, turns_before(seq, turn_of("o_before", half)) + 1)
                nc.vector.tensor_tensor(
                    o_rows[:, tile, half * 512:(half + 1) * 512].rearrange("p (h c) -> p h c", c=KVL),
                    o_ps[half][:, :].rearrange("p (h c) -> p h c", c=KVL),
                    row_inv[:, :].rearrange("p (h a) -> p h a", a=1).to_broadcast([P, 8, KVL]), ALU.mult)\
                    .then_inc(o_normed, 1)

            def add_residual(seq, tile, filled):
                dve.wait_ge(turn_filled, filled)
                dve.wait_ge(res_in, 16 * (seq + 1))
                if tile == 0 and late(seq):
                    dve.wait_ge(normed, seq)
                nc.vector.tensor_tensor(y_rows[:, tile, :], turn_ps[:, 0:D], x_res[:, tile, :], ALU.add)\
                    .then_inc(res_added, 1)
                dve.wait_ge(res_added, 2 * seq + tile + 1)
                nc.vector.bn_stats(stats[:, tile, :], y_rows[:, tile, :]).then_inc(turn_read, 1)

            def layer_norm(seq, read):
                wait_first(dve, turn_read, read, passed)
                for t in range(2):
                    last = nc.vector.bn_aggr(moments[:, t, :], stats[:, t, :])
                last.then_inc(stats_done, 1)
                dve.wait_ge(stats_done, seq + 1)
                nc.vector.tensor_scalar(var_eps[:, :], moments[:, :, 1], LN_EPS, None, ALU.add)\
                    .then_inc(var_done, 1)

            def apply_norm(seq):
                dve.wait_ge(rstd_done, seq + 1)
                if late(seq):
                    dve.wait_ge(stored, 16 * seq)
                for t in range(2):
                    last = nc.vector.tensor_scalar(x_out[:, t, :], y_rows[:, t, :], moments[:, t, 0:1],
                                                   rstd[:, t:t + 1], ALU.subtract, ALU.mult)
                last.then_inc(normed, 1)

            split_turn("x", 0, X0 + 1, 0, 0)
            multiplied_low(0)
            multiplied_low(1)
            latent(0, 0, LAT_PS[0])
            latent(1, 1, LAT_PS[1])
            multiplied_low(2)
            multiplied_low(3)
            split_turn("cq", 0, CQ0 + 1, 0, 0)
            split_turn("k", 0, K0 + 1, 0, 1)
            values_low(0, 0)
            split_turn("x", 0, X1 + 1, 0, 0)
            for c in range(2):
                q_turn(c, c + 3, 0, c, QUERY_PS[2 + c])
            latent(2, 0, LAT_PS[2])
            latent(3, 1, LAT_PS[3])
            for c in range(2):
                q_turn(2 + c, c + 7, 1, c, QUERY_PS[6 + c])
            for g in range(4):
                split_turn("q0", g, Q00 + g + 1, 0, 0)
            split_turn("cq", 0, CQ1 + 1, 0, 0)

            def slot(seq, par, v):
                mask_scores(seq, v)
                of, _, v2 = unit_before(seq, v, 2)
                if exists(of):
                    probs_low(SLOTS * of + v2, v2)
                if v == 8 and exists(seq + 2):
                    latent(2 * (seq + 2), 0)
                turns = slot_turns(seq, v)
                for i, (kind, index, _) in turns[:1]:
                    turn(seq, par, i, kind, index)
                if v == 9 and exists(seq + 2):
                    latent(2 * (seq + 2) + 1, 1)
                if v in (2, 3, 6, 7) and exists(seq + 1):
                    tile, c = v // 4, v % 4 - 2
                    n = 2 * tile + c
                    q_turn(4 * (seq + 1) + n, 8 * (seq + 1) + 4 * tile + c + 3, tile, c)
                if v == 3 and late(seq):
                    normalize(seq - 1, 1, 1)
                if v == 5:
                    normalize(seq, 0, 0)
                if v == 3 and exists(seq + 1):
                    values_low(seq + 1, 1 - par)
                if v == 7:
                    normalize(seq, 0, 1)
                if v == 11:
                    normalize(seq, 1, 0)
                if v == 8 and late(seq):
                    layer_norm(seq - 1, turns_before(seq, turn_of("y_before", 0)) + 1)
                if v == 10 and late(seq):
                    apply_norm(seq - 1)
                for i, (kind, index, _) in turns[1:]:
                    turn(seq, par, i, kind, index)

            def turn(seq, par, i, kind, index):
                if kind[0] == "y":
                    of, tile = (seq, 0) if kind == "y0" else (seq - 1, 1)
                    add_residual(of, tile, turns_before(seq, i) + 1)
                else:
                    split_turn(kind, index, turns_before(seq, i, split_only=True) + 1, seq, par)

            over_sequences(dve, slot)
            for v in (SLOTS - 2, SLOTS - 1):
                probs_low(SLOTS * (NSEQ - 1) + v, v)
            normalize(NSEQ - 1, 1, 1)
            for i, (kind, index, v) in enumerate(TURNS):
                if kind == "o_before":
                    split_turn(kind, index, turns_before(NSEQ, i, split_only=True) + 1, NSEQ, 0)
            last_turn = turns_before(NSEQ, turn_of("y_before", 0)) + 1
            add_residual(NSEQ - 1, 1, last_turn)
            layer_norm(NSEQ - 1, last_turn)
            apply_norm(NSEQ - 1)

        @block.tensor
        def _(pe):
            pe.wait_ge(consts_in, CONSTS)

            def take_turn(turn):
                if not (isinstance(turn, int) and turn == 0):
                    pe.wait_ge(turn_read, turn)

            def transpose_x(turn, seq):
                pe.wait_ge(rows_in, 16 * (seq + 1))
                take_turn(turn)
                for k in range(KD):
                    for t in range(2):
                        last = nc.tensor.transpose(turn_ps[:, k * SEQ + t * P:k * SEQ + (t + 1) * P],
                                                   x_rows[:, t, k * P:(k + 1) * P], ident[:, :])
                last.then_inc(turn_filled, 1)

            def latents(n, t, ps=proj_ps):
                for i, (xp, wp) in enumerate(PARTS):
                    for k in range(KD):
                        last = nc.tensor.matmul(ps[:, 0:LATC], xt_part[xp][:, k, t * P:(t + 1) * P],
                                                wl_part[wp][:, k, :], start=(i == 0 and k == 0),
                                                stop=(i == 2 and k == KD - 1))
                last.then_inc(lat_ready, 1)

            def transpose_cq(turn, seq):
                pe.wait_ge(lat_done, 2 * seq + 2)
                take_turn(turn)
                for k in range(2):
                    for t in range(2):
                        last = nc.tensor.transpose(turn_ps[0:QP, k * SEQ + t * P:k * SEQ + (t + 1) * P],
                                                   cq_rows[:, t, k * QP:(k + 1) * QP], ident[:, :])
                last.then_inc(turn_filled, 1)

            def transpose_k(turn, seq):
                pe.wait_ge(lat_done, 2 * seq + 2)
                take_turn(turn)
                for t in range(2):
                    last = nc.tensor.transpose(turn_ps[:, t * P:(t + 1) * P], k_rows[:, t, :], ident[:, :])
                last.then_inc(turn_filled, 1)

            def queries(tile, c, ps=proj_ps):
                for i, (cp, wp) in enumerate(PARTS):
                    for k in range(2):
                        last = nc.tensor.matmul(ps[:, :], cq_part[cp][0:QP, k, tile * P:(tile + 1) * P],
                                                wq_part[wp][0:QP, k, c * 512:(c + 1) * 512],
                                                start=(i == 0 and k == 0), stop=(i == 2 and k == 1))
                last.then_inc(q_ready, 1)

            def transpose_q(turn, seq, tile, g):
                pe.wait_ge(q_abs_done, 4 * seq + 2 * tile + g // 2 + 1)
                pe.wait_ge(q_pe_done, 4 * seq + 2 * tile + g // 2 + 1)
                take_turn(turn)
                for i in range(HG):
                    last = nc.tensor.transpose(turn_ps[:, i * P:(i + 1) * P], q_rows[:, tile, HG * g + i, :],
                                               ident[:, :])
                last.then_inc(turn_filled, 1)

            def transpose_o(turn, seq, tile, half):
                pe.wait_ge(o_normed, 4 * seq + 2 * tile + half + 1)
                take_turn(turn)
                for i in range(4):
                    col = half * 512 + i * P
                    last = nc.tensor.transpose(turn_ps[:, i * P:(i + 1) * P], o_rows[:, tile, col:col + P],
                                               ident[:, :])
                last.then_inc(turn_filled, 1)

            def project_out(turn, tile):
                take_turn(turn)
                for a in range(HEADS // 2):
                    for i, (op, wp) in enumerate(PARTS):
                        last = nc.tensor.matmul(turn_ps[:, 0:D], o_part[op][:, tile, a, :], wvo_part[wp][:, a, :],
                                                start=(a == 0 and i == 0), stop=(a == 7 and i == 2))
                last.then_inc(turn_filled, 1)

            def scores(seq, par, v):
                m = SLOTS * seq + v
                tile, heads, keys = heads_of(v)
                if v == 0:
                    if late(seq):
                        pe.wait_ge(turn_read, turns_before(seq - 1, turn_of("q0", 3)) + 1)
                    else:
                        pe.wait_ge(turn_read, CQ1 + 1)
                elif v >= 4 and v % 2 == 0:
                    pe.wait_ge(turn_read, turns_before(seq, turn_of("q1", v // 2 - 2)) + 1)
                wait_reuse(pe, masked_done, m, 2)
                for i, h in enumerate(heads):
                    for j, (qp, kp) in enumerate(PARTS):
                        last = nc.tensor.matmul(score_ps[v % 2][:, i * keys:(i + 1) * keys],
                                                q_part[qp][:, tile, h * P:(h + 1) * P],
                                                k_part[kp][:, par, 0:keys], start=(j == 0), stop=(j == 2))
                last.then_inc(scored, 1)

            def transpose_probs(m, v):
                pe.wait_ge(exp_done, m + 1)
                wait_reuse(pe, p_low, m, 2)
                for i in range(4):
                    last = nc.tensor.transpose(pt_ps[v % 2][:, i * P:(i + 1) * P],
                                               probs[:, v % 3, i * P:(i + 1) * P], ident[:, :])
                last.then_inc(p_turned, 1)

            def weighted_sums(seq, par, v):
                m = SLOTS * seq + v
                tile, heads, keys = heads_of(v)
                pe.wait_ge(p_low, m + 1)
                if v == 0:
                    pe.wait_ge(v_low, seq + 1)
                half = heads[0] // 8
                if heads[0] % 8 == 0 and not (isinstance(seq, int) and seq == 0 and tile == 0):
                    pe.wait_ge(o_normed, 4 * seq + 2 * tile + half - 1)
                blocks = keys // P
                for i, h in enumerate(heads):
                    for b in range(blocks):
                        for j, (pp, vp) in enumerate(PARTS):
                            at = (i * blocks + b) * P
                            last = nc.tensor.matmul(o_ps[half][:, (h % 8) * KVL:(h % 8 + 1) * KVL],
                                                    p_part[pp][:, v % 2, at:at + P], v_part[vp][:, par, b, :],
                                                    start=(b == 0 and j == 0),
                                                    stop=(b == blocks - 1 and j == 2))
                last.then_inc(summed, 1)

            def multiply(g):
                pe.wait_ge(raw_in[g % 2], 16 * (g // 2 + 1))
                if g >= 2:
                    pe.wait_ge(mult_low, g - 1)
                for i in range(HG):
                    raw = w_raw[:, g % 2, i, :]
                    for k in range(2):
                        nc.tensor.matmul(score_ps[g % 2][0:QP, k * SEQ + i * KVL:k * SEQ + (i + 1) * KVL],
                                         raw[:, k * QP:(k + 1) * QP], raw[:, QLR:QLR + KVL],
                                         start=True, stop=True)
                    at = (i % 2) * KVL
                    last = nc.tensor.matmul(pt_ps[g % 2][at:at + KVL, (i // 2) * D:(i // 2 + 1) * D],
                                            raw[:, QLR + KVL:QLR + 2 * KVL], raw[:, QLR + 2 * KVL:],
                                            start=True, stop=True)
                last.then_inc(multiplied, 1)

            transpose_x(X0, 0)
            multiply(0)
            multiply(1)
            pe.wait_ge(turn_read, X0 + 1)
            pe.wait_ge(wl_low, 1)
            latents(0, 0, LAT_PS[0])
            latents(1, 1, LAT_PS[1])
            multiply(2)
            multiply(3)
            transpose_cq(CQ0, 0)
            transpose_k(K0, 0)
            transpose_x(X1, 1)
            pe.wait_ge(turn_read, CQ0 + 1)
            pe.wait_ge(wpe_low, 2)
            pe.wait_ge(mult_low, HEADS // HG)
            for c in range(4):
                queries(0, c, QUERY_PS[c])
            pe.wait_ge(turn_read, X1 + 1)
            latents(2, 0, LAT_PS[2])
            latents(3, 1, LAT_PS[3])
            for c in range(4):
                if c in (1, 2):
                    pe.wait_ge(q_abs_done, c)
                elif c == 3:
                    pe.wait_ge(q_turned, 1)
                queries(1, c, QUERY_PS[4 + c])
            for g in range(4):
                transpose_q(Q00 + g, 0, 0, g)
            transpose_cq(CQ1, 1)

            def slot(seq, par, v):
                of, _, v2 = unit_before(seq, v, 2)
                if exists(of):
                    transpose_probs(SLOTS * of + v2, v2)
                scores(seq, par, v)
                if v in (8, 9) and exists(seq + 2):
                    if v == 8:
                        pe.wait_ge(turn_read, turns_before(seq, turn_of("x", 0)) + 1)
                        pe.wait_ge(q_turned, 4 * (seq + 2))
                    else:
                        pe.wait_ge(lat_scaled, 2 * (seq + 2) + 1)
                    latents(2 * (seq + 2) + v - 8, v - 8)
                turns = slot_turns(seq, v)
                if v == 11:
                    sums(seq, par, v)
                for i, (kind, index, _) in turns[:1]:
                    turn(seq, par, i, kind, index)
                if v < 8 and exists(seq + 1):
                    tile, c = v // 4, v % 4
                    n = 4 * (seq + 1) + 2 * tile
                    if v == 0:
                        if late(seq):
                            pe.wait_ge(turn_read, turns_before(seq - 1, turn_of("cq", 0)) + 1)
                        else:
                            pe.wait_ge(turn_read, CQ1 + 1)
                        pe.wait_ge(lat_scaled, 2 * (seq + 2))
                    elif c in (1, 2):
                        pe.wait_ge(q_abs_done, n + c)
                    else:
                        pe.wait_ge(q_turned, n + (1 if c == 3 else 0))
                    queries(tile, c)
                if v != 11:
                    sums(seq, par, v)
                for i, (kind, index, _) in turns[1:]:
                    turn(seq, par, i, kind, index)

            def sums(seq, par, v):
                of, back, v3 = unit_before(seq, v, 3)
                if exists(of):
                    weighted_sums(of, (par - back) % 2, v3)

            def turn(seq, par, i, kind, index):
                at = turns_before(seq, i)
                if kind == "q1":
                    transpose_q(at, seq, 1, index)
                elif kind == "q0":
                    transpose_q(at, seq + 1, 0, index)
                elif kind == "k":
                    transpose_k(at, seq + 1)
                elif kind == "x":
                    transpose_x(at, seq + 2)
                elif kind == "cq":
                    transpose_cq(at, seq + 2)
                elif kind == "o_before":
                    transpose_o(at, seq - 1, 1, index)
                elif kind == "o0":
                    transpose_o(at, seq, 0, index)
                else:
                    project_out(at, 0 if kind == "y0" else 1)

            over_sequences(pe, slot)
            for v in (SLOTS - 2, SLOTS - 1):
                transpose_probs(SLOTS * (NSEQ - 1) + v, v)
            for v in range(SLOTS - 3, SLOTS):
                weighted_sums(NSEQ - 1, (NSEQ - 1) % 2, v)
            for i, (kind, index, v) in enumerate(TURNS):
                if kind in ("o_before", "y_before"):
                    turn(NSEQ, 0, i, kind, index)


E = 32
TOPK = 4
NG = 8
GE = E // NG
TOPG = 3
I = 128
SI = 256
SC = SI // P
CAP = -(-5 * TOKENS // (4 * E))
CH2 = CAP // 2
SLOTROWS = E * CAP
ROUTE_SCALE = 2.5
TILES = TOKENS // P
RING = 4
EIN = 2 * KD * I
EW = EIN + D
PAST_END = 65536.0
ROUTER_LINKS = 32


def moe_phase(nc, ident_dram, router_w, e_bias, counts_dram, earlier_dram, w_experts, w_shared, zero_rows,
              x3, slots_dram, y_dram, out):
    with ExitStack() as ctx:
        s = Scope(nc, ctx, "moe")

        def both(name, shape):
            return [s.sb(name + "_high", shape, F32R), s.sb(name + "_low", shape, F32R)]

        ident = s.sb("ident", [P, P])
        counts = s.sb("counts", [P, E])
        bias = s.sb("bias", [P, BT, E])
        earlier = s.sb("earlier", [P, P], BF16)
        ones = s.sb("ones", [P, P], BF16)
        earlier_f = s.sb("earlier_f", [P, P])
        zeros = s.sb("zeros", [P, D])
        ws_raw = s.sb("ws_raw", [P, 3, KD, SI])
        ws_part = both("ws", [P, 3, KD, SI])
        wr_raw = s.sb("wr_raw", [P, KD, E])
        wr_part = both("wr", [P, KD, E])
        x_out = s.sb("x_out", [P, 2, 2, D])
        x_rows = s.sb("x_rows", [P, 2, BT, D])
        xt_rows = s.sb("xt_rows", [P, BT, D])
        xt_part = both("xt", [P, KD, BLK])
        score = s.sb("score", [P, BT, E])
        choice = s.sb("choice", [P, BT, E])
        pair_max = s.sb("pair_max", [P, BT * NG, 2])
        pair_min = s.sb("pair_min", [P, BT * NG, 2])
        top1 = s.sb("top1", [P, BT * NG])
        low1 = s.sb("low1", [P, BT * NG])
        high2 = s.sb("high2", [P, BT * NG])
        top2 = s.sb("top2", [P, BT * NG])
        group_sum = s.sb("group_sum", [P, BT, NG])
        best = s.sb("best", [P, BT, 8])
        best_at = s.sb("best_at", [P, BT, 8], U32)
        group_at = s.sb("group_at", [P, BT, 8])
        expert_at = s.sb("expert_at", [P, BT, 8])
        in_group = s.sb("in_group", [P, TOPG, BT, NG])
        group_mask = s.sb("group_mask", [P, BT, NG])
        chosen = s.sb("chosen", [P, TOPK, BT, E])
        picked = s.sb("picked", [P, TOPK, BT, E])
        pair_sum = s.sb("pair_sum", [P, 2, BT, E])
        member = s.sb("member", [P, BT, E], BF16)
        pair_member = s.sb("pair_member", [P, 2, E])
        block_member = s.sb("block_member", [P, E])
        members = s.sb("members", [P, E], BF16)
        members_f = s.sb("members_f", [P, E])
        weight_k = s.sb("weight_k", [P, BT, TOPK])
        place_k = s.sb("place_k", [P, BT, TOPK])
        weight_sum = s.sb("weight_sum", [P, BT])
        weight_inv = s.sb("weight_inv", [P, BT])
        full = s.sb("full", [P, BT, TOPK])
        slot_f = s.sb("slot_f", [P, BT, TOPK])
        slot_now = s.sb("slot_now", [P, 2, BT * TOPK], U32)
        slot_at = s.sb("slot_at", [P, TILES, TOPK], U32)
        gather_now = s.sb("gather_now", [P, RING, 2 * TOPK], U32)
        weight = s.sb("weight", [P, TILES * TOPK])
        gate = s.sb("gate", [P, 2, BLK])
        hidden = s.sb("hidden", [P, 2, BLK])
        h_part = both("h", [P, 2, BLK])
        total = s.sb("total", [P, TILES, D])
        w_raw = s.sb("w_raw", [P, RING, EW])
        w_part = both("w", [P, 2, EW])
        e_rows = s.sb("e_rows", [CH2, RING, 2, D])
        e_part = both("e", [P, 2, KD, CAP])
        e_gate = s.sb("e_gate", [P, 2, CAP])
        e_hidden = s.sb("e_hidden", [P, 2, CAP])
        eh_part = both("eh", [P, 2, CAP])
        y_rows = s.sb("y_rows", [CH2, RING, 2, D])
        y_in = s.sb("y_in", [P, RING, 2, TOPK, D])
        stats = s.sb("stats", [P, 2, 2, 6])
        moments = s.sb("moments", [P, 2, 2, 2])
        minus_half = s.sb("minus_half", [P, 2])
        var_eps = s.sb("var_eps", [P, 2, 2])
        rstd = s.sb("rstd", [P, 2, 2])
        xt_ps = [s.ps("xt0"), s.ps("xt1")]
        hid_ps = [[s.ps("gate0"), s.ps("up0")], [s.ps("gate1"), s.ps("up1")]]
        route_ps = s.ps("route")
        place_ps = s.ps("place")

        consts_in = s.sem("consts_in")
        passed = s.sem("passed")
        zero_set = s.sem("zero_set")
        slots_zeroed = s.sem("slots_zeroed")
        consts_set = s.sem("consts_set")
        ws_high = s.sem("ws_high")
        ws_low = s.sem("ws_low")
        rows_in = [s.sem("rows_in0"), s.sem("rows_in1")]
        xt_in = s.sem("xt_in")
        transposed = s.sem("transposed")
        xt_high = s.sem("xt_high")
        xt_low = s.sem("xt_low")
        logits_done = s.sem("logits_done")
        score_done = s.sem("score_done")
        chain = s.sem("router_chain")
        member_done = s.sem("member_done")
        places_done = s.sem("places_done")
        places_read = s.sem("places_read")
        slots_done = s.sem("slots_done")
        scattered = [s.sem("scattered0"), s.sem("scattered1")]
        gate_ready = s.sem("gate_ready")
        up_ready = s.sem("up_ready")
        gate_done = s.sem("gate_done")
        hidden_done = s.sem("hidden_done")
        h_high = s.sem("h_high")
        h_low = s.sem("h_low")
        shared_done = s.sem("shared_done")
        total_done = s.sem("total_done")
        raw_in = [s.sem(f"raw_in{r}") for r in range(RING)]
        in_high = s.sem("in_high_done")
        in_low = s.sem("in_low_done")
        down_high = s.sem("down_high_done")
        down_low = s.sem("down_low_done")
        slots_in = [s.sem(f"slots_in{r}") for r in range(RING)]
        e_turned = s.sem("e_turned")
        e_high = s.sem("e_high_done")
        e_low = s.sem("e_low_done")
        e_gate_ready = s.sem("e_gate_ready")
        e_up_ready = s.sem("e_up_ready")
        e_gate_done = s.sem("e_gate_done")
        e_hidden_done = s.sem("e_hidden_done")
        eh_high = s.sem("eh_high_done")
        eh_low = s.sem("eh_low_done")
        y_ready = s.sem("y_ready")
        y_copied = s.sem("y_copied")
        y_stored = [s.sem(f"y_stored{r}") for r in range(RING)]
        y_cleared = s.sem("y_cleared")
        gather_set = s.sem("gather_set")
        gathered = [s.sem(f"gathered{r}") for r in range(RING)]
        added = s.sem("added")
        stats_done = s.sem("stats_done")
        var_done = s.sem("var_done")
        rstd_done = s.sem("rstd_done")
        normed = s.sem("normed")
        stored = [s.sem("stored0"), s.sem("stored1")]

        CONSTS = 16 * (4 + BT + 2)
        PAIRS = TILES // 2

        def late(n):
            return not isinstance(n, int) or n > 0

        def over(eng, count, body):
            body(0)
            with eng.Fori(1, count - 1) as i:
                body(i)
            body(count - 1)

        def blocks(eng, body):
            def pair(i):
                for par in range(2):
                    body(2 * i + par, i, par)
            over(eng, NB // 2, pair)

        def rings(eng, count, body):
            def ring(i):
                for r in range(RING):
                    body(RING * i + r, i, r)
            over(eng, count // RING, ring)

        def ring_of(i, r, ahead):
            i = i + (r + ahead) // RING
            r = (r + ahead) % RING
            return RING * i + r, i, r

        def is_expert(e):
            return not isinstance(e, int) or 0 <= e < E

        def second(n):
            return not isinstance(n, int) or n >= 2

        def slot_rows(dram, e):
            return dram[bass.ds(e * CAP, CAP), :].rearrange("(a p) d -> p a d", p=CH2)

        block = ctx.enter_context(nc.Block())

        @block.sync
        def _(sp):
            sp.dma_start(ident[:, :], ident_dram).then_inc(consts_in, 16)
            sp.dma_start(counts[:, :], counts_dram).then_inc(consts_in, 16)
            sp.dma_start(earlier_f[:, :], earlier_dram).then_inc(consts_in, 16)
            sp.dma_start(ws_raw[:, :, :, :].rearrange("p a k c -> p (a k c)"), w_shared).then_inc(consts_in, 16)
            sp.dma_start(wr_raw[:, :, :], router_w.rearrange("(k p) e -> p k e", p=P)).then_inc(consts_in, 16)
            sp.dma_start(zeros[:, :], zero_rows).then_inc(consts_in, 16)
            for j in range(BT):
                sp.dma_start(bias[:, j, :], e_bias.partition_broadcast(P)).then_inc(consts_in, 16)
            def load_w(e, i, r):
                if not (isinstance(e, int) and e < RING):
                    sp.wait_ge(in_low, e - RING + 1)
                    sp.wait_ge(down_low, e - RING + 1)
                sp.dma_start(w_raw[:, r, :], w_experts[bass.ds(e, 1), :, :].rearrange("a p c -> (a p) c"))\
                    .then_inc(raw_in[r], 16)

            def load(blk, i, par):
                if late(blk):
                    sp.wait_ge(transposed, blk)
                sp.dma_start(xt_rows[:, :, :], rows(x3, blk)).then_inc(xt_in, 16)
                if second(blk):
                    wait_first(sp, total_done, blk - 1, passed)
                    wait_first(sp, scattered[par], 16 * BT * TOPK * i, passed)
                sp.dma_start(x_rows[:, par, :, :], rows(x3, blk)).then_inc(rows_in[par], 16)
                if isinstance(blk, int) and blk == 0:
                    sp.wait_ge(consts_in, CONSTS)
                    for a in range(SLOTROWS // P):
                        sp.dma_start(slots_dram[a * P:(a + 1) * P, :], zeros[:, :]).then_inc(slots_zeroed, 16)

            blocks(sp, load)

            def load_slots(e, i, r):
                if not (isinstance(e, int) and e < RING):
                    sp.wait_ge(e_turned, e - RING + 1)
                sp.dma_start(e_rows[:, r, :, :], slot_rows(slots_dram, e)).then_inc(slots_in[r], 16)

            def store_y(e, i, r):
                sp.wait_ge(y_copied, e + 1)
                sp.dma_start(slot_rows(y_dram, e), y_rows[:, r, :, :]).then_inc(y_stored[r], 16)

            for e in range(RING):
                load_w(e, 0, e)
            for par in range(2):
                sp.wait_ge(scattered[par], 16 * BT * TOPK * (NB // 2))
            for e in range(RING):
                load_slots(e, 0, e)

            def experts(e, i, r):
                if is_expert(e + RING):
                    load_w(e + RING, i + 1, r)
                    load_slots(e + RING, i + 1, r)
                if late(e):
                    store_y(*ring_of(i, r, -1))

            rings(sp, E, experts)
            store_y(E - 1, E // RING - 1, RING - 1)

            def store(n, i, r):
                sp.wait_ge(normed, n + 1)
                sp.dma_start(out[bass.ds(n * 2 * P, 2 * P), :].rearrange("(t p) d -> p t d", p=P),
                             x_out[:, r % 2, :, :]).then_inc(stored[r % 2], 16)

            rings(sp, PAIRS, store)
            sp.wait_ge(stored[0], 16 * (PAIRS // 2))
            sp.wait_ge(stored[1], 16 * (PAIRS // 2))

        @block.gpsimd
        def _(pool):
            nc.gpsimd.memset(minus_half[:, :], -0.5).then_inc(consts_set, 1)
            pool.wait_ge(consts_set, 1)
            pool.wait_ge(slots_zeroed, 16 * (SLOTROWS // P))

            def scatter(blk, i, par):
                pool.wait_ge(slots_done, blk + 1)
                wait_first(pool, rows_in[par], 16 * (i + 1), passed)
                for j in range(BT):
                    for k in range(TOPK):
                        nc.gpsimd.indirect_dma_start(
                            slots_dram,
                            bass.IndirectOffsetOnAxis(slot_now[:, par, j * TOPK + k:j * TOPK + k + 1], 0),
                            x_rows[:, par, j, :], None, bounds_check=SLOTROWS - 1, oob_is_err=False)\
                            .then_inc(scattered[par], 16)

            blocks(pool, scatter)

            for r in range(RING):
                pool.wait_ge(y_stored[r], 16 * (E // RING))
            pool.wait_ge(y_cleared, 2)

            def gather(n, i, r):
                if not (isinstance(n, int) and n < RING):
                    pool.wait_ge(added, 2 * (n - RING) + 2)
                nc.gpsimd.tensor_copy(gather_now[:, r, :], slot_at[:, bass.ds(2 * n, 2), :]
                                      .rearrange("p a k -> p (a k)")).then_inc(gather_set, 1)
                wait_first(pool, gather_set, n + 1, passed)
                for k in range(TOPK):
                    for t in range(2):
                        at = t * TOPK + k
                        nc.gpsimd.indirect_dma_start(
                            y_in[:, r, t, k, :], None, y_dram,
                            bass.IndirectOffsetOnAxis(gather_now[:, r, at:at + 1], 0),
                            bounds_check=SLOTROWS - 1, oob_is_err=False).then_inc(gathered[r], 16)
                if late(n):
                    rsqrt(n - 1, (r - 1) % 2)

            def rsqrt(n, par):
                pool.wait_ge(var_done, n + 1)
                nc.gpsimd.tensor_tensor(rstd[:, par, :], var_eps[:, par, :], minus_half[:, :], ALU.pow)\
                    .then_inc(rstd_done, 1)

            rings(pool, PAIRS, gather)
            rsqrt(PAIRS - 1, (PAIRS - 1) % 2)

        @block.scalar
        def _(act):
            act.wait_ge(consts_in, CONSTS)
            nc.scalar.activation(ws_part[0][:, :, :, :], ws_raw[:, :, :, :], ACT.Copy)
            nc.scalar.activation(wr_part[0][:, :, :], wr_raw[:, :, :], ACT.Copy).then_inc(ws_high, 1)

            def x_high(blk):
                act.wait_ge(transposed, blk + 1)
                if late(blk):
                    act.wait_ge(up_ready, SC * blk)
                for k in range(KD):
                    nc.scalar.activation(xt_part[0][:, k, :], hid_ps[k][0][:, :], ACT.Copy).then_inc(xt_high, 1)

            def scores(blk):
                act.wait_ge(logits_done, blk + 1)
                if late(blk):
                    act.wait_ge(slots_done, blk)
                nc.scalar.activation(score[:, :, :], route_ps[:, 0:BT * E].rearrange("p (t e) -> p t e", e=E),
                                     ACT.Sigmoid).then_inc(score_done, 1)

            x_high(0)
            scores(0)

            def tokens(blk, i, par):
                for c in range(SC):
                    act.wait_ge(gate_ready, SC * blk + c + 1)
                    if late(blk):
                        act.wait_ge(hidden_done, SC * (blk - 1) + c + 1)
                    nc.scalar.activation(gate[:, c, :], hid_ps[c][0][:, :], ACT.Silu).then_inc(gate_done, 1)
                if not (isinstance(blk, int) and blk == NB - 1):
                    x_high(blk + 1)
                for c in range(SC):
                    act.wait_ge(hidden_done, SC * blk + c + 1)
                    if late(blk):
                        act.wait_ge(shared_done, blk)
                    nc.scalar.activation(h_part[0][:, c, :], hidden[:, c, :], ACT.Copy).then_inc(h_high, 1)
                if not (isinstance(blk, int) and blk == NB - 1):
                    scores(blk + 1)

            blocks(act, tokens)

            def expert_in(e, i, r):
                act.wait_ge(raw_in[r], 16 * (i + 1))
                if second(e):
                    act.wait_ge(e_up_ready, e - 1)
                nc.scalar.activation(w_part[0][:, r % 2, 0:EIN], w_raw[:, r, 0:EIN], ACT.Copy)\
                    .then_inc(in_high, 1)
                act.wait_ge(e_turned, e + 1)
                nc.scalar.activation(e_part[0][:, r % 2, :, :],
                                     xt_ps[r % 2][:, 0:KD * CAP].rearrange("p (k c) -> p k c", c=CAP),
                                     ACT.Copy).then_inc(e_high, 1)

            def expert_hidden(e, par, r):
                act.wait_ge(e_gate_ready, e + 1)
                if second(e):
                    act.wait_ge(e_hidden_done, e - 1)
                nc.scalar.activation(e_gate[:, par, :], hid_ps[par][0][:, 0:CAP], ACT.Silu)\
                    .then_inc(e_gate_done, 1)
                if second(e):
                    act.wait_ge(y_ready, e - 1)
                nc.scalar.activation(w_part[0][:, par, EIN:], w_raw[:, r, EIN:], ACT.Copy).then_inc(down_high, 1)
                act.wait_ge(e_hidden_done, e + 1)
                nc.scalar.activation(eh_part[0][:, par, :], e_hidden[:, par, :], ACT.Copy).then_inc(eh_high, 1)

            def expert_out(e, i, r):
                act.wait_ge(y_ready, e + 1)
                if not (isinstance(e, int) and e < RING):
                    act.wait_ge(y_stored[r], 16 * i)
                nc.scalar.activation(y_rows[:, r, :, :], route_ps[0:CH2, :].rearrange("p (a d) -> p a d", a=2),
                                     ACT.Copy).then_inc(y_copied, 1)

            expert_in(0, 0, 0)

            def experts(e, i, r):
                if is_expert(e + 1):
                    expert_in(*ring_of(i, r, 1))
                expert_hidden(e, r % 2, r)
                if late(e):
                    expert_out(*ring_of(i, r, -1))

            rings(act, E, experts)
            expert_out(E - 1, E // RING - 1, RING - 1)

        @block.vector
        def _(dve):
            dve.wait_ge(consts_in, CONSTS)
            nc.vector.memset(ones[:, :], 1.0)
            nc.vector.memset(members[:, :], 0.0)
            nc.vector.memset(members_f[:, :], 0.0)
            nc.vector.tensor_copy(earlier[:, :], earlier_f[:, :])
            dve.wait_ge(ws_high, 1)
            nc.vector.tensor_tensor(ws_part[1][:, :, :, :], ws_raw[:, :, :, :],
                                    ws_part[0][:, :, :, :].bitcast(F32), ALU.subtract)
            nc.vector.tensor_tensor(wr_part[1][:, :, :], wr_raw[:, :, :], wr_part[0][:, :, :].bitcast(F32),
                                    ALU.subtract).then_inc(ws_low, 1)

            def router(blk, i, par):
                base = ROUTER_LINKS * blk
                links = [0]

                def link(instruction):
                    links[0] += 1
                    instruction.then_inc(chain, 1)
                    wait_first(dve, chain, base + links[0], passed)

                v = nc.vector
                dve.wait_ge(score_done, blk + 1)
                link(v.tensor_tensor(choice[:, :, :], score[:, :, :], bias[:, :, :], ALU.add))
                fours = choice[:, :, :].rearrange("p t (g a b) -> p (t g) a b", a=2, b=2)
                v.tensor_tensor(pair_max[:, :, :], fours[:, :, :, 0], fours[:, :, :, 1], ALU.max)
                link(v.tensor_tensor(pair_min[:, :, :], fours[:, :, :, 0], fours[:, :, :, 1], ALU.min))
                v.tensor_tensor(top1[:, :], pair_max[:, :, 0], pair_max[:, :, 1], ALU.max)
                v.tensor_tensor(low1[:, :], pair_max[:, :, 0], pair_max[:, :, 1], ALU.min)
                link(v.tensor_tensor(high2[:, :], pair_min[:, :, 0], pair_min[:, :, 1], ALU.max))
                link(v.tensor_tensor(top2[:, :], low1[:, :], high2[:, :], ALU.max))
                link(v.tensor_tensor(group_sum[:, :, :].rearrange("p t g -> p (t g)"), top1[:, :], top2[:, :],
                                     ALU.add))
                for j in range(BT):
                    last = v.max(best[:, j, :], group_sum[:, j, :])
                link(last)
                for j in range(BT):
                    last = v.max_index(best_at[:, j, :], best[:, j, :], group_sum[:, j, :])
                link(last)
                link(v.tensor_copy(group_at[:, :, :], best_at[:, :, :]))
                for g in range(TOPG):
                    last = v.tensor_tensor(in_group[:, g, :, :],
                                           counts[:, 0:NG].rearrange("p (a g) -> p a g", a=1)
                                           .to_broadcast([P, BT, NG]),
                                           group_at[:, :, g:g + 1].to_broadcast([P, BT, NG]), ALU.is_equal)
                link(last)
                link(v.tensor_tensor(group_mask[:, :, :], in_group[:, 0, :, :], in_group[:, 1, :, :], ALU.add))
                link(v.tensor_tensor(group_mask[:, :, :], group_mask[:, :, :], in_group[:, 2, :, :], ALU.add))
                link(v.tensor_tensor(choice[:, :, :].rearrange("p t (g e) -> p (t g) e", e=GE),
                                     choice[:, :, :].rearrange("p t (g e) -> p (t g) e", e=GE),
                                     group_mask[:, :, :].rearrange("p t (g a) -> p (t g) a", a=1)
                                     .to_broadcast([P, BT * NG, GE]), ALU.mult))
                link(v.tensor_scalar(choice[:, :, :], choice[:, :, :], 0.0, None, ALU.add))
                for j in range(BT):
                    last = v.max(best[:, j, :], choice[:, j, :])
                link(last)
                for j in range(BT):
                    last = v.max_index(best_at[:, j, :], best[:, j, :], choice[:, j, :])
                link(last)
                link(v.tensor_copy(expert_at[:, :, :], best_at[:, :, :]))
                shared_hidden(blk)
                for k in range(TOPK):
                    last = v.tensor_tensor(chosen[:, k, :, :],
                                           counts[:, :].rearrange("p (a e) -> p a e", a=1)
                                           .to_broadcast([P, BT, E]),
                                           expert_at[:, :, k:k + 1].to_broadcast([P, BT, E]), ALU.is_equal)
                link(last)
                link(v.tensor_tensor(pair_sum[:, :, :, :], chosen[:, 0:2, :, :], chosen[:, 2:4, :, :], ALU.add))
                v.tensor_tensor(member[:, :, :], pair_sum[:, 0, :, :], pair_sum[:, 1, :, :], ALU.add)\
                    .then_inc(member_done, 1)
                for k in range(TOPK):
                    last = v.tensor_tensor(picked[:, k, :, :], chosen[:, k, :, :], score[:, :, :], ALU.mult)
                link(last)
                link(v.tensor_reduce(weight_k[:, :, :].rearrange("p t k -> p k t"), picked[:, :, :, :],
                                     axis=AX.X, op=ALU.add))
                link(v.tensor_reduce(weight_sum[:, :], weight_k[:, :, :], axis=AX.X, op=ALU.add))
                link(v.tensor_scalar(weight_sum[:, :], weight_sum[:, :], 1e-20, None, ALU.add))
                link(v.reciprocal(weight_inv[:, :], weight_sum[:, :]))
                link(v.tensor_tensor(weight_k[:, :, :], weight_k[:, :, :],
                                     weight_inv[:, :].rearrange("p (t a) -> p t a", a=1)
                                     .to_broadcast([P, BT, TOPK]), ALU.mult))
                if not (isinstance(blk, int) and blk == NB - 1):
                    x_low(blk + 1)
                shared_low(blk)
                dve.wait_ge(places_done, blk + 1)
                places = place_ps[:, 0:BT * E].rearrange("p (t e) -> p t e", e=E)
                for k in range(TOPK):
                    last = v.tensor_tensor(picked[:, k, :, :], chosen[:, k, :, :], places, ALU.mult)
                last.then_inc(places_read, 1)
                dve.wait_ge(places_read, blk + 1)
                link(v.tensor_reduce(place_k[:, :, :].rearrange("p t k -> p k t"), picked[:, :, :, :],
                                     axis=AX.X, op=ALU.add))
                link(v.tensor_scalar(full[:, :, :], place_k[:, :, :], float(CAP), None, ALU.is_ge))
                link(v.scalar_tensor_tensor(slot_f[:, :, :], expert_at[:, :, 0:TOPK], float(CAP),
                                            place_k[:, :, :], ALU.mult, ALU.add))
                link(v.scalar_tensor_tensor(slot_f[:, :, :], full[:, :, :], PAST_END, slot_f[:, :, :],
                                            ALU.mult, ALU.add))
                link(v.tensor_scalar(full[:, :, :], full[:, :, :], -ROUTE_SCALE, ROUTE_SCALE, ALU.mult, ALU.add))
                v.tensor_tensor(weight[:, bass.ds(blk * BT * TOPK, BT * TOPK)],
                                weight_k[:, :, :].rearrange("p t k -> p (t k)"),
                                full[:, :, :].rearrange("p t k -> p (t k)"), ALU.mult)
                link(v.tensor_tensor(pair_member[:, :, :], member[:, 0:2, :], member[:, 2:4, :], ALU.add))
                link(v.tensor_tensor(block_member[:, :], pair_member[:, 0, :], pair_member[:, 1, :], ALU.add))
                link(v.tensor_tensor(members_f[:, :], members_f[:, :], block_member[:, :], ALU.add))
                v.tensor_copy(members[:, :], members_f[:, :])
                if second(blk):
                    dve.wait_ge(scattered[par], 16 * BT * TOPK * i)
                v.tensor_copy(slot_now[:, par, :], slot_f[:, :, :].rearrange("p t k -> p (t k)"))
                v.tensor_copy(slot_at[:, bass.ds(blk * BT, BT), :], slot_f[:, :, :]).then_inc(slots_done, 1)
                assert links[0] == ROUTER_LINKS, links[0]

            def x_low(blk):
                for k in range(KD):
                    dve.wait_ge(xt_high, KD * blk + k + 1)
                    nc.vector.tensor_tensor(xt_part[1][:, k, :], hid_ps[k][0][:, :],
                                            xt_part[0][:, k, :].bitcast(F32), ALU.subtract).then_inc(xt_low, 1)

            def shared_hidden(blk):
                for c in range(SC):
                    dve.wait_ge(up_ready, SC * blk + c + 1)
                    dve.wait_ge(gate_done, SC * blk + c + 1)
                    if late(blk):
                        dve.wait_ge(h_low, SC * (blk - 1) + c + 1)
                    nc.vector.tensor_tensor(hidden[:, c, :], hid_ps[c][1][:, :], gate[:, c, :], ALU.mult)\
                        .then_inc(hidden_done, 1)

            def shared_low(blk):
                for c in range(SC):
                    dve.wait_ge(h_high, SC * blk + c + 1)
                    nc.vector.tensor_tensor(h_part[1][:, c, :], hidden[:, c, :],
                                            h_part[0][:, c, :].bitcast(F32), ALU.subtract).then_inc(h_low, 1)

            x_low(0)

            def tokens(blk, i, par):
                router(blk, i, par)
                dve.wait_ge(shared_done, blk + 1)
                dve.wait_ge(rows_in[par], 16 * (i + 1))
                for h in range(2):
                    last = nc.vector.tensor_tensor(
                        total[:, bass.ds(blk * BT + 2 * h, 2), :],
                        xt_ps[h][:, :].rearrange("p (t d) -> p t d", d=D),
                        x_rows[:, par, 2 * h:2 * h + 2, :], ALU.add)
                last.then_inc(total_done, 1)

            blocks(dve, tokens)

            def expert_in(e, i, r):
                dve.wait_ge(in_high, e + 1)
                nc.vector.tensor_tensor(w_part[1][:, r % 2, 0:EIN], w_raw[:, r, 0:EIN],
                                        w_part[0][:, r % 2, 0:EIN].bitcast(F32), ALU.subtract).then_inc(in_low, 1)
                dve.wait_ge(e_high, e + 1)
                nc.vector.tensor_tensor(e_part[1][:, r % 2, :, :],
                                        xt_ps[r % 2][:, 0:KD * CAP].rearrange("p (k c) -> p k c", c=CAP),
                                        e_part[0][:, r % 2, :, :].bitcast(F32), ALU.subtract).then_inc(e_low, 1)

            def expert_hidden(e, par, r):
                dve.wait_ge(e_up_ready, e + 1)
                dve.wait_ge(e_gate_done, e + 1)
                if second(e):
                    dve.wait_ge(eh_low, e - 1)
                nc.vector.tensor_tensor(e_hidden[:, par, :], hid_ps[par][1][:, 0:CAP], e_gate[:, par, :],
                                        ALU.mult).then_inc(e_hidden_done, 1)
                dve.wait_ge(down_high, e + 1)
                nc.vector.tensor_tensor(w_part[1][:, par, EIN:], w_raw[:, r, EIN:],
                                        w_part[0][:, par, EIN:].bitcast(F32), ALU.subtract).then_inc(down_low, 1)
                dve.wait_ge(eh_high, e + 1)
                nc.vector.tensor_tensor(eh_part[1][:, par, :], e_hidden[:, par, :],
                                        eh_part[0][:, par, :].bitcast(F32), ALU.subtract).then_inc(eh_low, 1)

            expert_in(0, 0, 0)
            nc.vector.memset(y_in[:, :, :, :, :], 0.0).then_inc(y_cleared, 2)

            def experts(e, i, r):
                if is_expert(e + 1):
                    expert_in(*ring_of(i, r, 1))
                expert_hidden(e, r % 2, r)

            rings(dve, E, experts)

            def combine(n, i, r):
                dve.wait_ge(gathered[r], 16 * 2 * TOPK * (i + 1))
                for k in range(TOPK):
                    for t in range(2):
                        if k > 0:
                            dve.wait_ge(chain, NB * ROUTER_LINKS + 8 * n + 2 * (k - 1) + t + 1)
                        row = total[:, bass.ds(2 * n + t, 1), :].rearrange("p a d -> p (a d)")
                        last = nc.vector.scalar_tensor_tensor(
                            row, y_in[:, r, t, k, :], weight[:, bass.ds((2 * n + t) * TOPK + k, 1)], row,
                            ALU.mult, ALU.add)
                        last.then_inc(chain, 1)
                wait_first(dve, chain, NB * ROUTER_LINKS + 8 * n + 8, passed)
                for t in range(2):
                    row = total[:, bass.ds(2 * n + t, 1), :].rearrange("p a d -> p (a d)")
                    nc.vector.bn_stats(stats[:, r % 2, t, :], row).then_inc(added, 1)
                if second(n):
                    dve.wait_ge(normed, n - 1)
                wait_first(dve, added, 2 * n + 2, passed)
                for t in range(2):
                    last = nc.vector.bn_aggr(moments[:, r % 2, t, :], stats[:, r % 2, t, :])
                last.then_inc(stats_done, 1)
                dve.wait_ge(stats_done, n + 1)
                nc.vector.tensor_scalar(var_eps[:, r % 2, :], moments[:, r % 2, :, 1], LN_EPS, None, ALU.add)\
                    .then_inc(var_done, 1)
                if late(n):
                    apply_norm(*ring_of(i, r, -1))

            def apply_norm(n, i, r):
                dve.wait_ge(rstd_done, n + 1)
                if second(n):
                    dve.wait_ge(stored[r % 2], 16 * (2 * i + r // 2))
                for t in range(2):
                    row = total[:, bass.ds(2 * n + t, 1), :].rearrange("p a d -> p (a d)")
                    last = nc.vector.tensor_scalar(x_out[:, r % 2, t, :], row, moments[:, r % 2, t, 0:1],
                                                   rstd[:, r % 2, t:t + 1], ALU.subtract, ALU.mult)
                last.then_inc(normed, 1)

            rings(dve, PAIRS, combine)
            apply_norm(PAIRS - 1, PAIRS // RING - 1, RING - 1)

        @block.tensor
        def _(pe):
            pe.wait_ge(consts_in, CONSTS)

            def turn(blk):
                pe.wait_ge(xt_in, 16 * (blk + 1))
                if late(blk):
                    pe.wait_ge(gate_done, SC * blk)
                for k in range(KD):
                    for j in range(BT):
                        last = nc.tensor.transpose(hid_ps[k][0][:, j * P:(j + 1) * P],
                                                   xt_rows[:, j, k * P:(k + 1) * P], ident[:, :])
                last.then_inc(transposed, 1)

            def logits(blk):
                pe.wait_ge(xt_low, KD * (blk + 1))
                if late(blk):
                    pe.wait_ge(score_done, blk)
                else:
                    pe.wait_ge(ws_low, 1)
                for j in range(BT):
                    for i, (xp, wp) in enumerate(PARTS):
                        for k in range(KD):
                            last = nc.tensor.matmul(route_ps[:, j * E:(j + 1) * E],
                                                    xt_part[xp][:, k, j * P:(j + 1) * P], wr_part[wp][:, k, :],
                                                    start=(i == 0 and k == 0), stop=(i == 2 and k == KD - 1))
                last.then_inc(logits_done, 1)

            turn(0)
            logits(0)

            def tokens(blk, _, par):
                for c in range(SC):
                    for b, (ready, read) in enumerate(((gate_ready, gate_done), (up_ready, hidden_done))):
                        if late(blk):
                            pe.wait_ge(read, SC * (blk - 1) + c + 1)
                        if b == 0:
                            pe.wait_ge(xt_low, KD * (blk + 1))
                        for i, (wp, xp) in enumerate(PARTS):
                            for k in range(KD):
                                last = nc.tensor.matmul(hid_ps[c][b][:, :],
                                                        ws_part[wp][:, b, k, c * P:(c + 1) * P],
                                                        xt_part[xp][:, k, :],
                                                        start=(i == 0 and k == 0), stop=(i == 2 and k == KD - 1))
                        last.then_inc(ready, 1)
                if not (isinstance(blk, int) and blk == NB - 1):
                    turn(blk + 1)
                pe.wait_ge(member_done, blk + 1)
                pe.wait_ge(score_done, blk + 1)
                if late(blk):
                    pe.wait_ge(places_read, blk)
                for j in range(BT):
                    place = place_ps[:, j * E:(j + 1) * E]
                    nc.tensor.matmul(place, ones[:, :], members[:, :], start=True, stop=False)
                    for b in range(j):
                        nc.tensor.matmul(place, ones[:, :], member[:, b, :], start=False, stop=False)
                    last = nc.tensor.matmul(place, earlier[:, :], member[:, j, :], start=False, stop=True)
                last.then_inc(places_done, 1)
                pe.wait_ge(h_low, SC * (blk + 1))
                if late(blk):
                    pe.wait_ge(total_done, blk)
                for j in range(BT):
                    for c in range(SC):
                        for i, (hp, wp) in enumerate(PARTS):
                            last = nc.tensor.matmul(xt_ps[j // 2][:, (j % 2) * D:(j % 2 + 1) * D],
                                                    h_part[hp][:, c, j * P:(j + 1) * P], ws_part[wp][:, 2, c, :],
                                                    start=(c == 0 and i == 0), stop=(c == SC - 1 and i == 2))
                last.then_inc(shared_done, 1)
                if not (isinstance(blk, int) and blk == NB - 1):
                    logits(blk + 1)

            blocks(pe, tokens)
            pe.wait_ge(total_done, NB)

            def expert_turn(e, i, r):
                pe.wait_ge(slots_in[r], 16 * (i + 1))
                if second(e):
                    pe.wait_ge(e_low, e - 1)
                for k in range(KD):
                    for a in range(2):
                        at = k * CAP + a * CH2
                        last = nc.tensor.transpose(xt_ps[r % 2][:, at:at + CH2],
                                                   e_rows[:, r, a, k * P:(k + 1) * P], ident[0:CH2, 0:CH2])
                last.then_inc(e_turned, 1)

            def expert_hidden(e, par):
                pe.wait_ge(e_low, e + 1)
                pe.wait_ge(in_low, e + 1)
                for b, (ready, read) in enumerate(((e_gate_ready, e_gate_done), (e_up_ready, e_hidden_done))):
                    if second(e):
                        pe.wait_ge(read, e - 1)
                    for i, (wp, xp) in enumerate(PARTS):
                        for k in range(KD):
                            col = (b * KD + k) * I
                            last = nc.tensor.matmul(hid_ps[par][b][:, 0:CAP], w_part[wp][:, par, col:col + I],
                                                    e_part[xp][:, par, k, :],
                                                    start=(i == 0 and k == 0), stop=(i == 2 and k == KD - 1))
                    last.then_inc(ready, 1)

            def expert_out(e, i, r):
                pe.wait_ge(eh_low, e + 1)
                pe.wait_ge(down_low, e + 1)
                if late(e):
                    pe.wait_ge(y_copied, e)
                for a in range(2):
                    for i2, (hp, wp) in enumerate(PARTS):
                        last = nc.tensor.matmul(route_ps[0:CH2, a * D:(a + 1) * D],
                                                eh_part[hp][:, r % 2, a * CH2:(a + 1) * CH2],
                                                w_part[wp][:, r % 2, EIN:], start=(i2 == 0), stop=(i2 == 2))
                last.then_inc(y_ready, 1)

            expert_turn(0, 0, 0)

            def experts(e, i, r):
                if is_expert(e + 1):
                    expert_turn(*ring_of(i, r, 1))
                expert_hidden(e, r % 2)
                if late(e):
                    expert_out(*ring_of(i, r, -1))

            rings(pe, E, experts)
            expert_out(E - 1, E // RING - 1, RING - 1)


def rwkv_attention_moe_program(nc, a, out):
    x1 = nc.dram_tensor("x1", (TOKENS, D), F32).ap()
    x2 = nc.dram_tensor("x2", (TOKENS, D), F32).ap()
    x3 = nc.dram_tensor("x3", (TOKENS, D), F32).ap()
    slots = nc.dram_tensor("slots", (SLOTROWS, D), F32).ap()
    slots_out = nc.dram_tensor("slots_out", (SLOTROWS, D), F32).ap()
    rwkv_phase(nc, a["x_t"], a["x"], a["rkvo"], a["decay"], a["first"], a["mixes"], x1)
    ffn_phase(nc, a["ident"], a["ffn_gate_up"], a["ffn_down"], a["ffn_s_gate_up"], a["ffn_s_down"], x1, x2)
    attention_phase(nc, a["ident"], a["mla_latent"], a["mla_heads"], a["mla_pe"], a["mla_ln_q"], a["mla_ln_kv"],
                    a["rope_q"], a["rope_k"], a["mask"], x2, x3)
    moe_phase(nc, a["ident"], a["router_w"], a["e_bias"], a["counts"], a["earlier"], a["experts"], a["shared"],
              a["zeros"], x3, slots, slots_out, out)


def constants():
    inv = np.float32(1.0) / np.float32(10000.0) ** (np.arange(0, DR, 2, dtype=np.float32) / np.float32(DR))
    angle = np.outer(np.arange(SEQ, dtype=np.float32), inv.astype(np.float32)).astype(np.float32)
    cos = np.cos(np.concatenate([angle, angle], 1))
    sin = np.sin(np.concatenate([-angle, angle], 1))
    rope = np.stack([cos, sin]).reshape(2, 2, P, DR).transpose(2, 0, 1, 3).astype(np.float32)
    later = np.triu(np.ones((P, P), np.float32), 1)
    return {
        "ident": np.eye(P, dtype=np.float32),
        "rope_k": rope,
        "rope_q": rope * np.float32((DN + DR) ** -0.5),
        "mask": np.concatenate([np.zeros((P, P), np.float32), later * np.float32(MASKED)], 1),
        "counts": np.tile(np.arange(E, dtype=np.float32), (P, 1)),
        "earlier": later,
        "zeros": np.zeros((P, D), np.float32),
    }


def layouts(t):
    x = t["L0_attn_hidden_states"].reshape(TOKENS, D)

    def by_chunk(w):
        return w.reshape(CH, P, KD, P).transpose(0, 3, 2, 1).reshape(CH, P, D)

    def by_part(w):
        return w.reshape(KD, P, -1).transpose(1, 0, 2)

    qb = t["L1_attn_w_qb"].reshape(HEADS, DN + DR, QLR)
    kvb = t["L1_attn_w_kvb"].reshape(HEADS, DN + DV, KVL)
    heads = np.concatenate([qb[:, :DN], kvb[:, :DN], kvb[:, DN:],
                            t["L1_attn_w_o"].T.reshape(HEADS, DV, D)], 2)
    scales = np.zeros((2, HPAD), np.float32)
    scales[0, :HID] = t["L0_ffn_s_gate"]
    scales[1, :HID] = t["L0_ffn_s_up"]
    gate_up = [t[f"L1_ffn_W_{w}"].reshape(E, KD, P, I).transpose(0, 2, 1, 3).reshape(E, P, KD * I)
               for w in ("gate", "up")]
    return {
        "x": x,
        "x_t": x.T,
        "rkvo": np.concatenate([by_chunk(t[f"L0_attn_W{q}"]) for q in "rkv"]
                               + [t["L0_attn_Wo"].T.reshape(CH, P, D)], 2),
        "decay": t["L0_attn_time_decay"].T,
        "first": t["L0_attn_time_first"].T,
        "mixes": np.stack([t[f"L0_attn_time_mix_{q}"].reshape(KD, P) for q in "rkv"]).reshape(3 * KD, P).T,
        "ffn_gate_up": np.stack([t["L0_ffn_wq_gate"].T, t["L0_ffn_wq_up"].T]),
        "ffn_down": t["L0_ffn_wq_down"].T,
        "ffn_s_gate_up": scales.reshape(2, HC, P).transpose(2, 0, 1),
        "ffn_s_down": t["L0_ffn_s_down"],
        "mla_latent": np.concatenate([t["L1_attn_w_qa"], t["L1_attn_w_kva"]]).T,
        "mla_heads": heads.reshape(HEADS // HG, HG, P, MLAC).transpose(0, 2, 1, 3).reshape(HEADS // HG, P, -1),
        "mla_pe": qb[:, DN:].reshape(HEADS * DR, QLR).T.reshape(2, QP, -1).transpose(1, 0, 2).reshape(QP, -1),
        "mla_ln_q": t["L1_attn_q_a_ln_w"].reshape(2, QP).T,
        "mla_ln_kv": t["L1_attn_kv_a_ln_w"],
        "router_w": t["L1_ffn_router_w"].T,
        "e_bias": t["L1_ffn_e_bias"],
        "experts": np.concatenate(gate_up + [t["L1_ffn_W_down"]], 2),
        "shared": np.stack([by_part(t[f"L1_ffn_shared_{w}"].T) for w in ("gate", "up", "down")], 1)
        .reshape(P, -1),
    }


def kernel(**inputs):
    import concourse.bacc as bacc
    from concourse.bass_utils import run_bass_kernel_spmd

    nc = bacc.Bacc("TRN2", target_bir_lowering=False, num_devices=1)
    laid = {**layouts({k: np.asarray(v) for k, v in inputs.items()}), **constants()}
    arrays = {f"in_{k}": np.ascontiguousarray(v) for k, v in laid.items()}
    aps = {k: nc.dram_tensor(f"in_{k}", arrays[f"in_{k}"].shape, mybir.dt.from_np(arrays[f"in_{k}"].dtype),
                             kind="ExternalInput").ap() for k in laid}
    out = nc.dram_tensor("out", (TOKENS, D), F32, kind="ExternalOutput").ap()
    rwkv_attention_moe_program(nc, aps, out)
    r = run_bass_kernel_spmd(nc, [arrays], core_ids=[0])
    return r.results[0]["out"].reshape(TOKENS // SEQ, SEQ, D)
```
